# Optimizing a Trainium2 kernel written in Bass

```python
import numpy as np
import jax
import jax.numpy as jnp

def _softmax(x, axis=-1):
    return jax.nn.softmax(x, axis=axis)

def _gelu(x):
    return jax.nn.gelu(x, approximate=True)

def _silu(x):
    return jax.nn.silu(x)

def _sigmoid(x):
    return jax.nn.sigmoid(x)

def _layernorm(x, axis=-1, eps=1e-05):
    m = jnp.mean(x, axis=axis, keepdims=True)
    v = jnp.var(x, axis=axis, keepdims=True)
    return (x - m) / jnp.sqrt(v + eps)

def _scatter_add(tgt, idx, src, axis=0):
    return tgt.at[idx].add(src)

def _segment_sum(src, seg, n):
    return jax.ops.segment_sum(src, seg, n)
kernel_name = 'mk_early_fusion_d1_tok_img512_r4_a5b0e1'

def setup_inputs(seed: int=0):
    np.random.seed(seed)
    _w = jnp.asarray

    def _rec_inputs():
        import jax
        import jax.numpy as jnp
        _rk = jax.random.key(seed)
        x = -0.000477451 + 1.00034 * jax.random.normal(jax.random.fold_in(_rk, 1), (8, 32, 32, 29), jnp.float32)
        txt = 0.228173 + 0.721734 * jax.random.normal(jax.random.fold_in(_rk, 2), (8, 512, 128), jnp.float32)
        return (x, txt)
    x, txt = _rec_inputs()

    def _L0_tok_setup():
        import jax, jax.numpy as jnp
        import numpy as np
        import math
        H, W_DIM, D_MODEL, B = (32, 32, 128, 128)
        F_TOTAL = 29
        SEQ_LEN = H * W_DIM

        def make_pe(seq_len: int, d_model: int) -> jnp.ndarray:
            position = np.arange(seq_len, dtype=np.float32)[:, None]
            div_term = np.exp(np.arange(0, d_model, 2, dtype=np.float32) * (-math.log(10000.0) / d_model))
            pe = np.zeros((seq_len, d_model), dtype=np.float32)
            pe[:, 0::2] = np.sin(position * div_term)
            pe[:, 1::2] = np.cos(position * div_term)
            return jnp.asarray(pe)
        key = jax.random.key(seed)
        k1, k2 = jax.random.split(key)
        state_tensor = jax.random.normal(k1, (B, H, W_DIM, F_TOTAL), dtype=jnp.float32)
        W = jax.random.normal(k2, (F_TOTAL, D_MODEL), dtype=jnp.float32) * 0.05
        return {'state_tensor': state_tensor, 'W': W}
    _L0_tok_all = _L0_tok_setup()
    _L0_tok_in = {k: v for k, v in _L0_tok_all.items() if k in ('W',)}
    del _L0_tok_all

    def _L0_attn_setup():
        import jax, jax.numpy as jnp
        import numpy as np
        import math
        EPS = 1e-05

        def sinusoidal_pe(seq_len, d_model, dtype=jnp.float32):
            pos = jnp.arange(seq_len, dtype=jnp.float32)[:, None]
            div = jnp.exp(jnp.arange(0, d_model, 2, dtype=jnp.float32) * (-math.log(10000.0) / d_model))
            pe = jnp.zeros((seq_len, d_model), dtype=jnp.float32)
            pe = pe.at[:, 0::2].set(jnp.sin(pos * div))
            pe = pe.at[:, 1::2].set(jnp.cos(pos * div))
            return pe.astype(dtype)

        def rel_shift(pos_score):
            B, H, S1, S2 = pos_score.shape
            padded = jnp.pad(pos_score, ((0, 0), (0, 0), (0, 0), (1, 0)))
            return padded.reshape(B, H, S2 + 1, S1)[:, :, 1:, :].reshape(B, H, S1, S2)
        key = jax.random.key(seed)
        B, S, D, H = (4, 512, 128, 8)
        dh = D // H
        ks = jax.random.split(key, 12)
        scale = 0.02
        inp = {'inputs': jax.random.normal(ks[0], (B, S, D), dtype=jnp.float32), 'gamma': jnp.ones((D,), jnp.float32), 'beta': jnp.zeros((D,), jnp.float32), 'Wq': jax.random.normal(ks[1], (D, D), jnp.float32) * scale, 'bq': jnp.zeros((D,), jnp.float32), 'Wk': jax.random.normal(ks[2], (D, D), jnp.float32) * scale, 'bk': jnp.zeros((D,), jnp.float32), 'Wv': jax.random.normal(ks[3], (D, D), jnp.float32) * scale, 'bv': jnp.zeros((D,), jnp.float32), 'Wpos': jax.random.normal(ks[4], (D, D), jnp.float32) * scale, 'u_bias': jax.random.normal(ks[5], (H, dh), jnp.float32) * scale, 'v_bias': jax.random.normal(ks[6], (H, dh), jnp.float32) * scale, 'Wo': jax.random.normal(ks[7], (D, D), jnp.float32) * scale, 'bo': jnp.zeros((D,), jnp.float32)}
        return inp
    _L0_attn_all = _L0_attn_setup()
    _L0_attn_in = {k: v for k, v in _L0_attn_all.items() if k in ('gamma', 'beta', 'Wq', 'bq', 'Wk', 'bk', 'Wv', 'bv', 'Wpos', 'u_bias', 'v_bias', 'Wo', 'bo')}
    del _L0_attn_all

    def _L0_ffn_setup():
        import jax, jax.numpy as jnp
        import numpy as np
        import math
        B, T, D, H, E, TOPK = (8, 1024, 128, 512, 8, 2)
        CAP_FRAC = 1.0

        def _expert_ffn(x, w1, w2, w3):
            h = jax.nn.gelu(x @ w2 * (x @ w1), approximate=False)
            return h @ w3
        key = jax.random.key(seed)
        ks = jax.random.split(key, 6)
        x = jax.random.normal(ks[0], (B, T, D), dtype=jnp.float32)
        Wr = jax.random.normal(ks[1], (D, E), dtype=jnp.float32) * 0.02
        br = jnp.zeros((E,), dtype=jnp.float32)
        W1 = jax.random.normal(ks[2], (E, D, H), dtype=jnp.float32) * 0.02
        W2 = jax.random.normal(ks[3], (E, D, H), dtype=jnp.float32) * 0.02
        W3 = jax.random.normal(ks[4], (E, H, D), dtype=jnp.float32) * 0.02
        return {'x': x, 'Wr': Wr, 'br': br, 'W1': W1, 'W2': W2, 'W3': W3}
    _L0_ffn_all = _L0_ffn_setup()
    _L0_ffn_in = {k: v for k, v in _L0_ffn_all.items() if k in ('Wr', 'br', 'W1', 'W2', 'W3')}
    del _L0_ffn_all
    return {'x': x, 'txt': txt, 'L0_tok_W': _L0_tok_in['W'], 'L0_attn_gamma': _L0_attn_in['gamma'], 'L0_attn_beta': _L0_attn_in['beta'], 'L0_attn_Wq': _L0_attn_in['Wq'], 'L0_attn_bq': _L0_attn_in['bq'], 'L0_attn_Wk': _L0_attn_in['Wk'], 'L0_attn_bk': _L0_attn_in['bk'], 'L0_attn_Wv': _L0_attn_in['Wv'], 'L0_attn_bv': _L0_attn_in['bv'], 'L0_attn_Wpos': _L0_attn_in['Wpos'], 'L0_attn_u_bias': _L0_attn_in['u_bias'], 'L0_attn_v_bias': _L0_attn_in['v_bias'], 'L0_attn_Wo': _L0_attn_in['Wo'], 'L0_attn_bo': _L0_attn_in['bo'], 'L0_ffn_Wr': _L0_ffn_in['Wr'], 'L0_ffn_br': _L0_ffn_in['br'], 'L0_ffn_W1': _L0_ffn_in['W1'], 'L0_ffn_W2': _L0_ffn_in['W2'], 'L0_ffn_W3': _L0_ffn_in['W3']}

def reference(x, txt, L0_tok_W, L0_attn_gamma, L0_attn_beta, L0_attn_Wq, L0_attn_bq, L0_attn_Wk, L0_attn_bk, L0_attn_Wv, L0_attn_bv, L0_attn_Wpos, L0_attn_u_bias, L0_attn_v_bias, L0_attn_Wo, L0_attn_bo, L0_ffn_Wr, L0_ffn_br, L0_ffn_W1, L0_ffn_W2, L0_ffn_W3):
    import jax
    import jax.numpy as jnp

    def _L0_tok_ref(state_tensor, W):
        import jax, jax.numpy as jnp
        import numpy as np
        import math
        H, W_DIM, D_MODEL, B = (32, 32, 128, 128)
        F_TOTAL = 29
        SEQ_LEN = H * W_DIM

        def make_pe(seq_len: int, d_model: int) -> jnp.ndarray:
            position = np.arange(seq_len, dtype=np.float32)[:, None]
            div_term = np.exp(np.arange(0, d_model, 2, dtype=np.float32) * (-math.log(10000.0) / d_model))
            pe = np.zeros((seq_len, d_model), dtype=np.float32)
            pe[:, 0::2] = np.sin(position * div_term)
            pe[:, 1::2] = np.cos(position * div_term)
            return jnp.asarray(pe)
        b, h, w, f = state_tensor.shape
        s = h * w
        x = state_tensor.reshape(b, s, f)
        emb = jnp.einsum('bsf,fd->bsd', x, W)
        pe = make_pe(s * 2, W.shape[1])[:s]
        return emb + pe[None, :, :]

    def _L0_attn_ref(inputs, gamma, beta, Wq, bq, Wk, bk, Wv, bv, Wpos, u_bias, v_bias, Wo, bo):
        import jax, jax.numpy as jnp
        import numpy as np
        import math
        EPS = 1e-05

        def sinusoidal_pe(seq_len, d_model, dtype=jnp.float32):
            pos = jnp.arange(seq_len, dtype=jnp.float32)[:, None]
            div = jnp.exp(jnp.arange(0, d_model, 2, dtype=jnp.float32) * (-math.log(10000.0) / d_model))
            pe = jnp.zeros((seq_len, d_model), dtype=jnp.float32)
            pe = pe.at[:, 0::2].set(jnp.sin(pos * div))
            pe = pe.at[:, 1::2].set(jnp.cos(pos * div))
            return pe.astype(dtype)

        def rel_shift(pos_score):
            B, H, S1, S2 = pos_score.shape
            padded = jnp.pad(pos_score, ((0, 0), (0, 0), (0, 0), (1, 0)))
            return padded.reshape(B, H, S2 + 1, S1)[:, :, 1:, :].reshape(B, H, S1, S2)
        B, S, D = inputs.shape
        H, dh = u_bias.shape
        pos_emb = sinusoidal_pe(S, D)
        mu = jnp.mean(inputs, axis=-1, keepdims=True)
        var = jnp.var(inputs, axis=-1, keepdims=True)
        x = (inputs - mu) * jax.lax.rsqrt(var + EPS) * gamma + beta
        q = (x @ Wq.T + bq).reshape(B, S, H, dh)
        k = (x @ Wk.T + bk).reshape(B, S, H, dh)
        v = (x @ Wv.T + bv).reshape(B, S, H, dh)
        pos = (pos_emb @ Wpos.T).reshape(S, H, dh)
        content = jnp.einsum('bshd,bthd->bhst', q + u_bias, k)
        pos_score = jnp.einsum('bshd,thd->bhst', q + v_bias, pos)
        pos_score = rel_shift(pos_score)
        score = (content + pos_score) / jnp.sqrt(jnp.float32(D))
        attn = jax.nn.softmax(score, axis=-1)
        ctx = jnp.einsum('bhst,bthd->bshd', attn, v).reshape(B, S, D)
        out = ctx @ Wo.T + bo
        return out

    def _L0_ffn_ref(x, Wr, br, W1, W2, W3):
        import jax, jax.numpy as jnp
        import numpy as np
        import math
        B, T, D, H, E, TOPK = (8, 1024, 128, 512, 8, 2)
        CAP_FRAC = 1.0

        def _expert_ffn(x, w1, w2, w3):
            h = jax.nn.gelu(x @ w2 * (x @ w1), approximate=False)
            return h @ w3
        b, t, d = x.shape
        Bt = b * t
        x_flat = x.reshape(Bt, d)
        logits = x_flat.astype(jnp.float32) @ Wr + br
        vals, idx = jax.lax.top_k(logits, TOPK)
        scores = jax.nn.softmax(vals, axis=-1).astype(x.dtype).reshape(b, t, TOPK)
        onehot = jax.nn.one_hot(idx, E, dtype=jnp.float32)
        pos = jnp.cumsum(jnp.cumsum(onehot, axis=0), axis=1).astype(jnp.int32)
        capacity = math.floor(Bt * CAP_FRAC)
        mask3 = onehot * (pos < capacity)
        token_mask = mask3.sum(-1).reshape(b, t, TOPK)
        assign = jnp.einsum('tke,e->tk', mask3, jnp.arange(E, dtype=jnp.float32)).astype(jnp.int32)
        i_max = assign.reshape(b, t, TOPK).max(axis=-1)
        y = jnp.zeros_like(x)
        for i in range(E):
            yi = _expert_ffn(x, W1[i], W2[i], W3[i])
            y = jnp.where((i_max == i)[..., None], yi, y)
        expert_outputs = jnp.where(token_mask[..., None] > 0, y[:, :, None, :], x[:, :, None, :])
        return jnp.einsum('btkD,btk->btD', expert_outputs, scores)
    h = _L0_tok_ref(x, L0_tok_W)
    h = jnp.concatenate([h, txt], axis=1)
    h = h + _L0_attn_ref(_layernorm(h, axis=-1), L0_attn_gamma, L0_attn_beta, L0_attn_Wq, L0_attn_bq, L0_attn_Wk, L0_attn_bk, L0_attn_Wv, L0_attn_bv, L0_attn_Wpos, L0_attn_u_bias, L0_attn_v_bias, L0_attn_Wo, L0_attn_bo)
    h = h + _L0_ffn_ref(_layernorm(h, axis=-1), L0_ffn_Wr, L0_ffn_br, L0_ffn_W1, L0_ffn_W2, L0_ffn_W3)
    return h

_drawn_inputs = setup_inputs


def setup_inputs(seed=0):
    import zlib

    import numpy as np

    out = dict(_drawn_inputs(seed))
    spreads = {'L0_attn_gamma': (1.0, 0.6),
     'L0_attn_beta': (0.0, 0.8),
     'L0_attn_bq': (0.0, 0.8),
     'L0_attn_bk': (0.0, 0.8),
     'L0_attn_bv': (0.0, 0.288),
     'L0_attn_bo': (0.0, 0.1),
     'L0_ffn_br': (0.0, 0.491)}
    factors = {'L0_attn_Wq': 8.0,
     'L0_attn_Wk': 8.0,
     'L0_attn_Wpos': 8.0,
     'L0_attn_u_bias': 8.0,
     'L0_attn_v_bias': 8.0,
     'L0_ffn_Wr': 4.503,
     'L0_ffn_W1': 3.673,
     'L0_ffn_W2': 3.672,
     'L0_ffn_W3': 3.625}
    for name, (base, spread) in spreads.items():
        noise = np.random.default_rng([zlib.crc32(name.encode()), seed]).standard_normal(out[name].shape)
        drawn = base * np.exp(spread * noise) if base else spread * noise
        out[name] = jnp.asarray(drawn.astype(out[name].dtype))
    for name, factor in factors.items():
        out[name] = (out[name] * factor).astype(out[name].dtype)
    return out
```

```python
from contextlib import ExitStack

import numpy as np

import concourse.bass as bass
from concourse import mybir

F32 = mybir.dt.float32
F16 = mybir.dt.float16
I32 = mybir.dt.int32
U32 = mybir.dt.uint32
ACT = mybir.ActivationFunctionType
ALU = mybir.AluOpType
AX = mybir.AxisListType
ds = bass.ds

P = 128
B = 8
S_IMG, S_TXT = 1024, 512
S = S_IMG + S_TXT
D = 128
NH, DH = 8, 16
UNITS = B * NH
F_IN = 29
NE = 8
HID = 512
CH = 512
NT = S // P
NC = S // CH
TC = CH // P
NG = B * NT
NR = B * NC
TOKENS = B * S
SLOTS = NG + NE
PART = 3 * DH
EPS = 1e-5
QSCALE = float(1.0 / np.sqrt(np.float32(D)))
VW = 2 * DH
DW = P + 1


class Chain:

    def __init__(self, eng, sem, base=0):
        self.eng, self.sem, self.base, self.n = eng, sem, base, 0

    def add(self, ins):
        ins.then_inc(self.sem, 1)
        self.n += 1

    def settle(self):
        self.eng.wait_ge(self.sem, self.base + self.n)

    def settle_apart(self):
        self.settle()
        self.eng.sem_inc(self.sem, 1)
        self.n += 1


class Names:
    pass


def setup_block(nc, ctx, io, g):
    with ExitStack() as c:
        def sb(name, shape, dt=F32):
            return c.enter_context(nc.sbuf_tensor(name, shape, dt))

        def sem(name):
            return ctx.enter_context(nc.semaphore(name))

        wnat = sb("wnat", [P, 5, D])
        wph = sb("wph", [P, 2, D], F16)
        wpl = sb("wpl", [P, 2, D], F16)
        wpp = sb("wpp", [P, 2, D])
        vec = sb("vec", [P, 4])
        tmp = sb("tmp", [P, 4])
        hm = sb("hm", [P, NH + 1])
        bd = sb("bd", [P, NH + 1])
        zero = sb("zero", [P, 8 * D])
        pw = c.enter_context(nc.psum_tensor("pw", [P, 4, D], F32))
        prb = c.enter_context(nc.psum_tensor("prb", [P, 2, NH + 1], F32))
        s_in, s_wt, s_rb, s_chain, s_wp, s_zero, s_out, s_bd = (
            sem(n) for n in ("su_in", "su_wt", "su_rb", "su_chain", "su_wp", "su_zero", "su_out", "su_bd"))
        loads = [
            (wnat[:, 0, :], io.Wq), (wnat[:, 1, :], io.Wk), (wnat[:, 2, :], io.Wv), (wnat[:, 3, :], io.Wo),
            (wnat[:, 4, :], io.Wpos), (g.ident[:, :], io.ident), (g.ident16[:, :], io.ident16),
            (vec[:, 0:1], io.bq.unsqueeze(1)), (vec[:, 1:2], io.u.rearrange("h d -> (h d)").unsqueeze(1)),
            (vec[:, 2:3], io.v.rearrange("h d -> (h d)").unsqueeze(1)),
            (g.bk[:, 0:1], io.bk.unsqueeze(1)), (g.gamma[:, 0:1], io.gamma.unsqueeze(1)),
            (g.beta[:, 0:1], io.beta.unsqueeze(1)), (hm[:, :], io.head_mask),
        ]
        with nc.Block() as block:
            @block.sync
            def _(sp):
                for dst, src in loads:
                    sp.dma_start(dst, src).then_inc(s_in, 16)
                sp.wait_ge(s_zero, 1)
                rows = io.XS.rearrange("(p r) d -> p (r d)", p=P)
                for i in range(SLOTS // 8):
                    sp.dma_start(rows[:, i * 8 * D:(i + 1) * 8 * D], zero[:, :]).then_inc(s_out, 16)
                sp.wait_ge(s_wp, 1)
                for part, w in enumerate((wph, wpl, wph)):
                    rows = slice(part * DH, (part + 1) * DH)
                    sp.dma_start(io.WP3[0:NH, rows, :], w[:, :, :].rearrange("p a k -> p (a k)")).then_inc(s_out, 16)
                    sp.dma_start(io.WP3[NH, rows, :], w[0:DH, :, :].rearrange("p a k -> p (a k)")).then_inc(s_out, 16)
                sp.wait_ge(s_out, 16 * (SLOTS // 8 + 6))

            @block.tensor
            def _(pe):
                pe.wait_ge(s_in, 16 * len(loads))
                for i in range(4):
                    ins = pe.transpose(pw[:, i, :], wnat[:, i, :], g.ident[:, :])
                ins.then_inc(s_wt, 1)
                pe.wait_ge(s_bd, 1)
                for i in range(2):
                    ins = pe.matmul(prb[:, i, :], wpp[:, i, :], bd[:, :], start=True, stop=True)
                ins.then_inc(s_rb, 1)

            @block.vector
            def _(dve):
                ch = Chain(dve, s_chain)
                dve.memset(zero[:, :], 0.0).then_inc(s_zero, 1)
                dve.wait_ge(s_in, 16 * len(loads))
                ch.add(dve.tensor_tensor(tmp[:, 0:1], vec[:, 0:1], vec[:, 1:2], ALU.add))
                ch.add(dve.tensor_tensor(tmp[:, 1:2], vec[:, 2:3], vec[:, 1:2], ALU.subtract))
                wp = wnat[:, 4, :].rearrange("p (k two) -> p two k", two=2)
                half = D // 2
                ch.add(dve.tensor_copy(wpp[:, 0, 0:half], wp[:, 0, :]))
                ch.add(dve.tensor_copy(wpp[:, 0, half:D], wp[:, 1, :]))
                ch.add(dve.tensor_copy(wpp[:, 1, 0:half], wp[:, 1, :]))
                ch.add(dve.tensor_copy(wpp[:, 1, half:D], wp[:, 0, :]))
                ch.settle()
                ch.add(dve.tensor_scalar(g.bqs[:, 0:1], tmp[:, 0:1], QSCALE, None, ALU.mult))
                ch.add(dve.tensor_scalar(tmp[:, 2:3], tmp[:, 1:2], QSCALE, None, ALU.mult))
                ch.add(dve.tensor_copy(wph[:, :, :], wpp[:, :, :]))
                ch.settle()
                dve.tensor_scalar(bd[:, :], hm[:, :], tmp[:, 2:3], None, ALU.mult).then_inc(s_bd, 1)
                dve.tensor_tensor(wpl[:, :, :], wpp[:, :, :], wph[:, :, :], ALU.subtract).then_inc(s_wp, 1)
                dve.wait_ge(s_wt, 1)
                dve.tensor_copy(g.wt[:, :, :], pw[:, :, :])
                dve.wait_ge(s_rb, 1)
                dve.tensor_copy(g.rb[:, :, :], prb[:, :, :])


def embed_block(nc, ctx, io, g):
    with ExitStack() as c:
        def sb(name, shape, dt=F32):
            return c.enter_context(nc.sbuf_tensor(name, shape, dt))

        def bank(name):
            return c.enter_context(nc.psum_tensor(name, [P, CH], F32))

        def sem(name):
            return ctx.enter_context(nc.semaphore(name))

        x8 = sb("x8", [P, 8, F_IN])
        pe_tok = sb("pe_tok", [P, 8, D])
        wtok = sb("wtok", [F_IN, D])
        bvb = sb("bvb", [P, D])
        xt = sb("xt", [F_IN, 2, CH])
        h = sb("h", [P, NT, D])
        z = sb("z", [P, NT, D])
        z2 = sb("z2", [P, NT, D])
        st = sb("st", [P, NT, 6])
        mv = sb("mv", [P, NT, 2])
        std = sb("std", [P, NT])
        rstd = sb("rstd", [P, NT])
        var = sb("var", [P, NT])
        xn = sb("xn", [P, S])
        full = sb("full", [P, 2, S])
        hi = sb("hi", [P, 2, S], F16)
        lo = sb("lo", [P, 2, S], F16)
        vals = sb("vals", [P, NH, NT, VW])
        b_xt, b_emb, b_z, b_q, b_k, b_v = (bank(n) for n in ("b_xt", "b_emb", "b_z", "b_q", "b_k", "b_v"))
        (s_const, s_x, s_xt, s_xts, s_emb, s_hpart, s_h0, s_h0out, s_z, s_zt, s_xn, s_qk, s_full, s_lo, s_v, s_vs,
         s_free, s_out, s_var, s_std, s_chain) = (
            sem("em_" + n) for n in (
                "const", "x_in", "xt_ready", "xt_copied", "emb_ready", "h_part", "h_done", "h_stored", "z_done",
                "zt_ready", "xn_ready", "qk_ready", "full_ready", "lo_done", "v_ready", "v_done", "out_free",
                "out_stored", "var_ready", "std_ready", "chain"))
        links = 2 * (2 * NT + 3)

        def load(sp, b):
            sp.dma_start(x8[:, :, :], io.x[ds(b, 1)].rearrange("o a c f -> (o a c) f").rearrange(
                "(t p) f -> p t f", p=P)).then_inc(s_x, 16)
            sp.dma_start(h[:, 8:12, :], io.txt[ds(b, 1)].rearrange("o s d -> (o s) d").rearrange(
                "(t p) d -> p t d", p=P)).then_inc(s_x, 16)

        def store(sp, b, last):
            sp.wait_ge(s_h0, b + 1)
            sp.dma_start(io.H0[ds(b, 1)].rearrange("o p t d -> (o p) (t d)"),
                         h[:, :, :].rearrange("p t d -> p (t d)")).then_inc(s_h0out, 16)
            sp.wait_ge(s_h0out, 16 * (b + 1))
            sp.wait_ge(s_z, b + 1)
            if not last:
                load(sp, b + 1)
            sp.wait_ge(s_lo, NC * (b + 1))
            for t, parts in ((0, (hi, hi, lo)), (1, (hi, lo, hi))):
                dst = io.QK[ds(NH * b, NH), t, :, :]
                for part, w in enumerate(parts):
                    sp.dma_start(dst[:, part * DH:(part + 1) * DH, :], w[:, t, :]).then_inc(s_out, 16)
            sp.wait_ge(s_vs, NC * (b + 1) + 1)
            sp.dma_start(io.VS[ds(NH * b, NH)].rearrange("h p n -> p h n"),
                         vals[:, :, :, :].rearrange("p h t w -> p h (t w)")).then_inc(s_out, 16)
            sp.wait_ge(s_out, 16 * 7 * (b + 1))
            sp.sem_inc(s_free, 1)

        with nc.Block() as block:
            @block.sync
            def _(sp):
                sp.sem_inc(s_free, 1)
                load(sp, 0)
                sp.dma_start(pe_tok[:, :, :], io.pe_tok.rearrange("(t p) d -> p t d", p=P)).then_inc(s_const, 16)
                sp.dma_start(wtok[:, :], io.Wtok).then_inc(s_const, 16)
                sp.dma_start(bvb[:, :], io.bv.partition_broadcast(P)).then_inc(s_const, 16)
                with sp.Fori(0, B - 1) as b:
                    store(sp, b, False)
                store(sp, B - 1, True)
                sp.dma_start(io.QK[UNITS], io.QK[0]).then_inc(s_out, 16)
                sp.dma_start(io.VS[UNITS], io.VS[0]).then_inc(s_out, 16)
                sp.wait_ge(s_out, 16 * (7 * B + 2))

            @block.tensor
            def _(pe):
                pe.wait_ge(s_const, 48)
                with pe.Fori(0, B) as b:
                    pe.wait_ge(s_x, 32 * (b + 1))
                    for q in range(2):
                        if q == 1:
                            pe.wait_ge(s_xts, 2 * b + 1)
                        for t in range(TC):
                            ins = pe.transpose(b_xt[0:F_IN, t * P:(t + 1) * P], x8[:, TC * q + t, :], g.ident[:, :])
                        ins.then_inc(s_xt, 1)
                        pe.wait_ge(s_xts, 2 * b + q + 1)
                        if q == 1:
                            pe.wait_ge(s_hpart, 2 * b + 1)
                        for t in range(TC):
                            ins = pe.matmul(b_emb[:, t * P:(t + 1) * P], xt[:, q, t * P:(t + 1) * P], wtok[:, :],
                                            start=True, stop=True)
                        ins.then_inc(s_emb, 1)
                    pe.wait_ge(s_z, b + 1)
                    for k in range(NC):
                        for t in range(TC):
                            ins = pe.transpose(b_z[:, t * P:(t + 1) * P], z2[:, TC * k + t, :], g.ident[:, :])
                        ins.then_inc(s_zt, 1)
                        pe.wait_ge(s_xn, NC * b + k + 1)
                        pe.wait_ge(s_full, NC * b + k + 1)
                        pe.matmul(b_q[:, :], g.wt[:, 0, :], xn[:, k * CH:(k + 1) * CH], start=True, stop=True)
                        pe.matmul(b_k[:, :], g.wt[:, 1, :], xn[:, k * CH:(k + 1) * CH],
                                  start=True, stop=True).then_inc(s_qk, 1)
                        pe.wait_ge(s_vs, NC * b + k + 1)
                        for t in range(TC):
                            ins = pe.matmul(b_v[:, t * P:(t + 1) * P], xn[:, k * CH + t * P:k * CH + (t + 1) * P],
                                            g.wt[:, 2, :], start=True, stop=True)
                        ins.then_inc(s_v, 1)

            @block.scalar
            def _(act):
                act.sem_inc(s_full, 1)
                with act.Fori(0, B) as b:
                    for n in range(2):
                        act.wait_ge(s_var, 2 * b + n + 1)
                        act.activation(std[:, :], var[:, :], ACT.Sqrt).then_inc(s_std, 1)
                    for k in range(NC):
                        cols = slice(k * CH, (k + 1) * CH)
                        act.wait_ge(s_zt, NC * b + k + 1)
                        act.activation(xn[:, cols], b_z[:, :], ACT.Identity, bias=g.beta[:, 0:1],
                                       scale=g.gamma[:, 0:1]).then_inc(s_xn, 1)
                        act.wait_ge(s_qk, NC * b + k + 1)
                        if k == 0:
                            act.wait_ge(s_free, b + 1)
                        for dst in (full, hi):
                            act.activation(dst[:, 0, cols], b_q[:, :], ACT.Identity, bias=g.bqs[:, 0:1], scale=QSCALE)
                            ins = act.activation(dst[:, 1, cols], b_k[:, :], ACT.Identity, bias=g.bk[:, 0:1])
                        ins.then_inc(s_full, 1)

            @block.vector
            def _(dve):
                dve.sem_inc(s_vs, 1)
                dve.memset(vals[:, :, :, :], 1.0)
                dve.wait_ge(s_const, 48)
                with dve.Fori(0, B) as b:
                    ch = Chain(dve, s_chain, links * b)
                    dve.wait_ge(s_x, 32 * (b + 1))
                    for q in range(2):
                        dve.wait_ge(s_xt, 2 * b + q + 1)
                        dve.tensor_copy(xt[:, q, :], b_xt[0:F_IN, :]).then_inc(s_xts, 1)
                        dve.wait_ge(s_emb, 2 * b + q + 1)
                        dve.tensor_tensor(h[:, TC * q:TC * (q + 1), :], b_emb[:, :].rearrange("p (t d) -> p t d", t=TC),
                                          pe_tok[:, TC * q:TC * (q + 1), :], ALU.add).then_inc(s_hpart, 1)
                    dve.wait_ge(s_hpart, 2 * b + 2)
                    dve.sem_inc(s_h0, 1)
                    for n, (src, dst) in enumerate(((h, z), (z, z2))):
                        for t in range(NT):
                            ch.add(dve.bn_stats(st[:, t, :], src[:, t, :]))
                        ch.settle_apart()
                        for t in range(NT):
                            ins = dve.bn_aggr(mv[:, t, :], st[:, t, :])
                            if t == NT - 1:
                                ch.add(ins)
                        ch.settle()
                        dve.tensor_scalar(var[:, :], mv[:, :, 1], EPS, None, ALU.add).then_inc(s_var, 1)
                        dve.wait_ge(s_std, 2 * b + n + 1)
                        ch.add(dve.reciprocal(rstd[:, :], std[:, :]))
                        ch.settle()
                        for t in range(NT):
                            ch.add(dve.tensor_scalar(dst[:, t, :], src[:, t, :], mv[:, t, 0:1], rstd[:, t:t + 1],
                                                     ALU.subtract, ALU.mult))
                        ch.settle()
                    dve.sem_inc(s_z, 1)
                    dve.wait_ge(s_free, b + 1)
                    for k in range(NC):
                        dve.wait_ge(s_v, NC * b + k + 1)
                        dve.tensor_tensor(
                            vals[:, :, TC * k:TC * (k + 1), 0:DH],
                            b_v[:, :].rearrange("p (t h d) -> p h t d", t=TC, h=NH),
                            bvb[:, :].rearrange("p (h d) -> p h d", h=NH).unsqueeze(2).to_broadcast([P, NH, TC, DH]),
                            ALU.add).then_inc(s_vs, 1)
                        dve.wait_ge(s_full, NC * b + k + 2)
                        cols = slice(k * CH, (k + 1) * CH)
                        dve.tensor_tensor(lo[:, :, cols], full[:, :, cols], hi[:, :, cols],
                                          ALU.subtract).then_inc(s_lo, 1)
                    assert ch.n == links


def unit_order():
    steps, m = [], 0
    for n in range(NT * NC):
        steps.append(("S", n))
        if n % TC == 1 and n > TC:
            steps.append(("PV", n // TC - 1))
        if n in (2, 4, 6):
            steps.append(("R", n // 2 - 1))
        if n in (10, 12, 14, 16):
            steps.append(("X", n // 2 - 5))
        while m < NT * NC and n >= 14 and m < -(-(n - 13) * NT * NC // 18):
            steps.append(("PRE", m))
            m += 1
        if n == 33:
            steps.append(("NM", 0))
        if n == 34:
            steps.append(("GUARD", 0))
    assert m == NT * NC
    steps.append(("PV", NT * NC // TC - 1))
    return steps


PREPARE = ([("R", k) for k in range(NC)] + [("X", j) for j in range(4)] + [("PRE", m) for m in range(NT * NC)]
           + [("NM", 0), ("GUARD", 0)])
STEPS = NT * NC
GROUPS = STEPS // TC
SHARED = 3 + 4 + 1
SHARED_B = SHARED * NH + NC
LINKS_PREP = 2 * 4


def attend_block(nc, ctx, io, g):
    with ExitStack() as c:
        def sb(name, shape, dt=F32):
            return c.enter_context(nc.sbuf_tensor(name, shape, dt))

        def bank(name):
            return c.enter_context(nc.psum_tensor(name, [P, CH], F32))

        def sem(name):
            return ctx.enter_context(nc.semaphore("at_" + name))

        def pair(name, shape, dt=F32):
            return [sb(f"{name}{p}", shape, dt) for p in range(2)]

        tabs = sb("tabs", [P, 4, S], F16)
        rot = sb("rot", [P, 2, S])
        mask1 = sb("mask1", [P, 3, DW])
        mask2 = sb("mask2", [P, 3, DW], I32)
        pick = sb("pick", [P, 2, 2, VW])
        k3, q3 = pair("k3", [P, S], F16), pair("q3", [P, S], F16)
        vo, wp3 = pair("vo", [P, NT * VW]), pair("wp3", [PART, 2 * D], F16)
        ah, al = pair("ah", [P, S + 4], F16), pair("al", [P, S + 4], F16)
        dgh, dgl = pair("dgh", [P, NT, DW], F16), pair("dgl", [P, NT, DW], F16)
        ta, tb, af = sb("ta", [P, NC, CH]), sb("tb", [P, NC, CH]), sb("af", [P, NC, CH])
        dt = sb("dt", [P, 4, 3 * DW])
        pt = sb("pt", [P, 8, CH])
        part_max, nm, nmh = sb("part_max", [P, STEPS]), sb("nm", [P, NT]), sb("nmh", [NT, P], F16)
        osb = sb("osb", [P, NH, S])
        rl, cx = sb("rl", [P, CH]), sb("cx", [P, S])
        score = [bank(f"score{i}") for i in range(3)]
        pre = [bank(f"pre{i}") for i in range(2)]
        shared = [bank(f"shared{i}") for i in range(2)]
        o_bank = bank("o_bank")
        s_const, s_clear = sem("const"), sem("cleared")
        s_load = [sem("loaded0"), sem("loaded1")]
        s_score, s_exp, s_pv, s_evac = sem("score"), sem("exp"), sem("pv"), sem("evac")
        s_pre, s_max, s_shared, s_sread = sem("pre"), sem("max"), sem("shared"), sem("shared_read")
        s_a, s_dg = sem("a_ready"), sem("diag_ready")
        s_nm, s_guard = sem("nm"), sem("guard")
        s_cxout, s_cxfree = sem("cx_stored"), sem("cx_free")
        s_vchain, s_gchain, s_hi, s_apart = sem("vector_chain"), sem("gpsimd_chain"), sem("diag_hi"), sem("apart")
        order = unit_order()

        def scores(pe, n, p, u):
            k, t = n // NT, n % NT
            lo, hi = k * CH, (k + 1) * CH
            out = score[n % 3]
            pe.wait_ge(s_exp, u * STEPS + n + 1)
            keys = slice(t * P, (t + 1) * P)
            first = True
            a, b = max(lo, min(hi, t * P - 1)), max(lo, min(hi, t * P + P - 1))
            if lo < a:
                for tab, w in ((2, ah), (2, al), (3, ah)):
                    pe.matmul(out[:, 0:a - lo], tabs[:, tab, keys], w[p][:, lo + 2:a + 2], start=first, stop=False)
                    first = False
            if a < b:
                x = a - (t * P - 1)
                for w in (dgh, dgl):
                    pe.matmul(out[:, a - lo:b - lo], g.ident16[:, :], w[p][:, t, x:x + b - a], start=first,
                              stop=False)
                    first = False
            if b < hi:
                for tab, w in ((0, ah), (0, al), (1, ah)):
                    pe.matmul(out[:, b - lo:CH], tabs[:, tab, keys], w[p][:, b + 1:hi + 1], start=first, stop=False)
                    first = False
            if n == 0:
                pe.wait_ge(s_guard, 16 * (u + 1))
            pe.matmul(out[:, :], k3[p][0:PART + 1, keys], q3[p][0:PART + 1, lo:hi], start=False,
                      stop=True).then_inc(s_score, 1)

        def values(pe, q, p, u):
            pe.wait_ge(s_exp, u * STEPS + TC * (q + 1) + 3)
            if q % 3 == 0:
                pe.wait_ge(s_evac, u * NC + q // 3 + 1)
            for i in range(TC):
                t = (TC * q + i) % NT
                ins = pe.matmul(o_bank[VW * i:VW * (i + 1), :], vo[p][:, VW * t:VW * (t + 1)],
                                pt[:, ((GROUPS * p + q) % 2) * TC + i, :], start=(q % 3 == 0), stop=(q % 3 == 2),
                                tile_position=(0, VW * i))
            ins.then_inc(s_pv, 1)

        def turned(pe, k, p, use):
            pe.wait_ge(s_sread, use + 1)
            cols = slice(k * CH, (k + 1) * CH)
            pe.matmul(shared[0][:, :], wp3[p][:, 0:D], q3[p][0:PART, cols], start=True, stop=True)
            pe.matmul(shared[1][:, :], wp3[p][:, D:2 * D], q3[p][0:PART, cols], start=True,
                      stop=True).then_inc(s_shared, 1)

        def diagonal(pe, j, p, use):
            pe.wait_ge(s_sread, use + 1)
            for side in range(2):
                for i in range(3):
                    t = 3 * j + i
                    keys = slice(t * P, (t + 1) * P)
                    for n, (tab, w) in enumerate(((2 * side, ah), (2 * side, al), (2 * side + 1, ah))):
                        ins = pe.matmul(shared[side][:, i * DW:(i + 1) * DW], tabs[:, tab, keys],
                                        w[p][:, t * P + side:t * P + side + DW], start=(n == 0), stop=(n == 2))
            ins.then_inc(s_shared, 1)

        def premax(pe, m, p, v):
            t, k = m // NC, m % NC
            lo, hi = k * CH, (k + 1) * CH
            out = pre[m % 2]
            rows = slice(t * P, (t + 1) * P)
            pe.wait_ge(s_max, v * STEPS + m + 1)
            pieces = []
            a, b = max(lo, min(hi, t * P)), max(lo, min(hi, t * P + P))
            if lo < a:
                pieces.append((lo, a, ah[p][:, t * P + 1:t * P + P + 1], tabs[:, 0, lo:a], P))
            if a < b:
                pieces.append((a, b, dgh[p][:, t, 1:DW], g.ident16[:, :], P))
            if b < hi:
                if b == t * P + P:
                    pieces.append((b, b + 1, ah[p][:, t * P + 2:t * P + P + 1], tabs[:, 2, b:b + 1], P - 1))
                    b += 1
                pieces.append((b, hi, ah[p][:, t * P + 2:t * P + P + 2], tabs[:, 2, b:hi], P))
            pe.matmul(out[:, :], q3[p][0:PART, rows], k3[p][0:PART, lo:hi], start=True, stop=False)
            for i, (x, y, w, r, rows_out) in enumerate(pieces):
                ins = pe.matmul(out[0:rows_out, x - lo:y - lo], w, r, start=False, stop=(i == len(pieces) - 1))
            ins.then_inc(s_pre, 1)

        def turns(eng, body, batch_end):
            with eng.Fori(0, B) as b:
                with eng.Fori(0, NH // 2) as hp:
                    for p in range(2):
                        u = b * NH + hp * 2 + p
                        body(p=p, u=u, q=1 - p, v=u + 1, loads=b * (NH // 2) + hp + 1 + p,
                             use=b * SHARED_B + hp * (2 * SHARED) + SHARED * (p + 1), head=hp * 2 + p,
                             links=b * (NH * LINKS_PREP + NC) + hp * (2 * LINKS_PREP) + LINKS_PREP * (p + 1))
                batch_end(b)

        with nc.Block() as block:
            @block.sync
            def _(sp):
                for dst, src in ((tabs[:, :, :], io.tabs.rearrange("a p s -> p a s")),
                                 (rot[:, :, :], io.rot.rearrange("a p s -> p a s")),
                                 (mask1[:, :, :], io.mask1), (mask2[:, :, :], io.mask2), (pick[:, :, :, :], io.pick)):
                    sp.dma_start(dst, src).then_inc(s_const, 16)
                sp.sem_inc(s_cxfree, 1)
                sp.wait_ge(s_clear, 8)

                def load(q, v, head):
                    sp.dma_start(k3[q][0:PART, :], io.QK[ds(v, 1), 1].rearrange("o r s -> (o r) s")).then_inc(s_load[q], 16)
                    sp.dma_start(q3[q][0:PART, :], io.QK[ds(v, 1), 0].rearrange("o r s -> (o r) s")).then_inc(s_load[q], 16)
                    sp.dma_start(wp3[q][:, :], io.WP3[ds(head, 1)].rearrange("o r s -> (o r) s")).then_inc(s_load[q], 16)
                    sp.dma_start(vo[q][:, :], io.VS[ds(v, 1)].rearrange("o r s -> (o r) s")).then_inc(s_load[q], 16)

                def guard(q, use):
                    sp.wait_ge(s_sread, use + SHARED + 1)
                    sp.dma_start(q3[q][PART:PART + 1, :], nmh[:, :]).then_inc(s_guard, 16)

                load(0, 0, 0)
                guard(0, 0)

                def body(p, u, q, v, loads, use, head, links):
                    sp.wait_ge(s_pv, u * GROUPS + 2)
                    load(q, v, head + 1)
                    guard(q, use)

                def batch_end(b):
                    sp.wait_ge(s_sread, b * SHARED_B + SHARED * (NH + 1) + NC + 1)
                    sp.dma_start(io.CT[ds(b, 1)].rearrange("o p s -> (o p) s"), cx[:, :]).then_inc(s_cxout, 16)
                    sp.wait_ge(s_cxout, 16 * (b + 1))
                    sp.sem_inc(s_cxfree, 1)

                turns(sp, body, batch_end)
                sp.wait_ge(s_guard, 16 * (UNITS + 1))

            @block.tensor
            def _(pe):
                pe.sem_inc(s_pv, 2)
                pe.wait_ge(s_const, 16 * 5)

                def step(kind, n, p, u, q, v, loads, use):
                    if kind == "S":
                        scores(pe, n, p, u)
                    elif kind == "PV":
                        values(pe, n, p, u)
                    elif kind == "R":
                        if n == 0:
                            pe.wait_ge(s_load[q], loads * 64)
                        turned(pe, n, q, use + n)
                    elif kind == "X":
                        if n == 0:
                            pe.wait_ge(s_a, v * NC + NC)
                        diagonal(pe, n, q, use + 3 + n)
                    elif kind == "PRE":
                        if n % 9 == 0:
                            pe.wait_ge(s_dg, v * 4 + n // 9 + 1)
                        premax(pe, n, q, v)
                    elif kind == "GUARD":
                        pe.wait_ge(s_nm, v + 1)
                        pe.wait_ge(s_sread, use + 8)
                        pe.transpose(shared[0][0:NT, 0:P], nm[:, :], g.ident[:, :]).then_inc(s_shared, 1)

                for kind, n in PREPARE:
                    step(kind, n, None, None, 0, 0, 1, 0)

                def body(p, u, q, v, loads, use, head, links):
                    for kind, n in order:
                        step(kind, n, p, u, q, v, loads, use)

                def batch_end(b):
                    pe.wait_ge(s_evac, (b + 1) * (NH * NC) + 1)
                    for k in range(NC):
                        pe.wait_ge(s_sread, b * SHARED_B + SHARED * (NH + 1) + k + 1)
                        for what in range(2):
                            for par in range(2):
                                for hh in range(NH // 2):
                                    ins = pe.matmul(shared[what][VW * hh:VW * (hh + 1), :], pick[:, what, par, :],
                                                    osb[:, 2 * hh + par, k * CH:(k + 1) * CH], start=(par == 0),
                                                    stop=(par == 1), tile_position=(0, VW * hh))
                        ins.then_inc(s_shared, 1)

                turns(pe, body, batch_end)

            @block.scalar
            def _(act):
                act.sem_inc(s_exp, 3)

                def body(p, u, q, v, loads, use, head, links):
                    for kind, n in order:
                        if kind == "S":
                            act.wait_ge(s_score, u * STEPS + n + 1)
                            if n % TC == 0:
                                act.wait_ge(s_pv, u * GROUPS + n // TC + 1)
                            act.activation(pt[:, (4 * ((GROUPS * p + n // TC) % 2)) + n % TC, :], score[n % 3][:, :],
                                           ACT.Exp).then_inc(s_exp, 1)

                turns(act, body, lambda b: None)

            @block.vector
            def _(dve):
                for q in range(2):
                    dve.memset(k3[q][:, :], 1.0).then_inc(s_clear, 1)
                    dve.memset(q3[q][:, :], 1.0).then_inc(s_clear, 1)
                    dve.memset(ah[q][:, :], 0.0).then_inc(s_clear, 1)
                    dve.memset(al[q][:, :], 0.0).then_inc(s_clear, 1)
                dve.sem_inc(s_sread, 1)
                dve.sem_inc(s_max, 2)
                dve.sem_inc(s_evac, 1)
                dve.wait_ge(s_const, 16 * 5)

                def step(ch, kind, n, p, u, q, v, use, head):
                    if kind == "R":
                        cols = slice(n * CH, (n + 1) * CH)
                        dve.wait_ge(s_shared, use + n + 1)
                        dve.scalar_tensor_tensor(ta[:, n, :], shared[0][:, :], g.rb[:, 0, head], rot[:, 0, cols],
                                                 ALU.add, ALU.mult)
                        dve.scalar_tensor_tensor(tb[:, n, :], shared[1][:, :], g.rb[:, 1, head], rot[:, 1, cols],
                                                 ALU.add, ALU.mult).then_inc(s_sread, 1)
                    elif kind == "X":
                        dve.wait_ge(s_shared, use + 3 + n + 1)
                        w = dt[:, n, :].rearrange("p (t x) -> p t x", t=3)
                        ch.add(dve.tensor_tensor(w, shared[0][:, 0:3 * DW].rearrange("p (t x) -> p t x", t=3),
                                                 mask1[:, :, :], ALU.mult))
                        ch.settle_apart()
                        dve.copy_predicated(w, mask2[:, :, :], shared[1][:, 0:3 * DW].rearrange(
                            "p (t x) -> p t x", t=3)).then_inc(s_sread, 1)
                    elif kind == "PRE":
                        dve.wait_ge(s_pre, v * STEPS + n + 1)
                        dve.tensor_reduce(part_max[:, n:n + 1], pre[n % 2][:, :], AX.X, ALU.max).then_inc(s_max, 1)
                    elif kind == "NM":
                        dve.wait_ge(s_max, v * STEPS + STEPS + 2)
                        dve.tensor_reduce(nm[:, :], part_max[:, :].rearrange("p (t k) -> p t k", k=NC), AX.X,
                                          ALU.max, negate=True).then_inc(s_nm, 1)
                    elif kind == "GUARD":
                        dve.wait_ge(s_shared, use + 8)
                        dve.tensor_copy(nmh[:, :], shared[0][0:NT, 0:P]).then_inc(s_sread, 1)
                    elif kind == "PV" and n % 3 == 2:
                        dve.wait_ge(s_pv, u * GROUPS + n + 1 + 2)
                        k = n // 3
                        dve.tensor_copy(osb[:, ds(head[1], 1), k * CH:(k + 1) * CH].rearrange("p o s -> p (o s)"),
                                        o_bank[:, :]).then_inc(s_evac, 1)

                ch = Chain(dve, s_vchain)
                for kind, n in PREPARE:
                    step(ch, kind, n, None, None, 0, 0, 0, slice(0, 1))
                assert ch.n == LINKS_PREP

                def body(p, u, q, v, loads, use, head, links):
                    ch = Chain(dve, s_vchain, links)
                    for kind, n in order:
                        h = (None, head) if kind == "PV" else ds(head + 1, 1)
                        step(ch, kind, n, p, u, q, v, use, h)

                def batch_end(b):
                    ch = Chain(dve, s_vchain, b * (NH * LINKS_PREP + NC) + LINKS_PREP * (NH + 1))
                    dve.wait_ge(s_cxfree, b + 1)
                    for k in range(NC):
                        dve.wait_ge(s_shared, b * SHARED_B + SHARED * (NH + 1) + k + 1)
                        ch.add(dve.reciprocal(rl[:, :], shared[1][:, :]))
                        ch.settle()
                        dve.tensor_tensor(cx[:, k * CH:(k + 1) * CH], shared[0][:, :], rl[:, :],
                                          ALU.mult).then_inc(s_sread, 1)

                turns(dve, body, batch_end)

            @block.gpsimd
            def _(pool):
                def step(kind, n, q, v, use):
                    if kind == "R":
                        cols = slice(n * CH + 1, (n + 1) * CH + 1)
                        pool.wait_ge(s_sread, use + n + 2)
                        base = v * (NC * 2) + 2 * n
                        pool.tensor_tensor(af[:, n, :], ta[:, n, :], tb[:, n, :], ALU.add).then_inc(s_gchain, 1)
                        pool.wait_ge(s_gchain, base + 1)
                        pool.sem_inc(s_apart, 1)
                        pool.tensor_copy(ah[q][:, cols], af[:, n, :]).then_inc(s_gchain, 1)
                        pool.wait_ge(s_gchain, base + 2)
                        pool.tensor_tensor(al[q][:, cols], af[:, n, :], ah[q][:, cols], ALU.subtract).then_inc(s_a, 1)
                    elif kind == "X":
                        pool.wait_ge(s_sread, use + 3 + n + 2)
                        w = dt[:, n, :].rearrange("p (t x) -> p t x", t=3)
                        hi, lo = dgh[q][:, 3 * n:3 * n + 3, :], dgl[q][:, 3 * n:3 * n + 3, :]
                        pool.sem_inc(s_apart, 1)
                        pool.tensor_copy(hi, w).then_inc(s_hi, 1)
                        pool.wait_ge(s_hi, v * 4 + n + 1)
                        pool.tensor_tensor(lo, w, hi, ALU.subtract).then_inc(s_dg, 1)

                pool.wait_ge(s_clear, 8)
                for kind, n in PREPARE:
                    step(kind, n, 0, 0, 0)

                def body(p, u, q, v, loads, use, head, links):
                    for kind, n in order:
                        step(kind, n, q, v, use)

                turns(pool, body, lambda b: None)


def project_block(nc, ctx, io, g):
    with ExitStack() as c:
        def sb(name, shape, dt=F32):
            return c.enter_context(nc.sbuf_tensor(name, shape, dt))

        def bank(name):
            return c.enter_context(nc.psum_tensor(name, [P, CH], F32))

        def sem(name):
            return ctx.enter_context(nc.semaphore("pr_" + name))

        ct = [sb(f"ct{k}", [P, CH]) for k in range(NC)]
        h0 = [sb(f"h0_{k}", [P, TC, D]) for k in range(NC)]
        h1 = [sb(f"h1_{k}", [P, TC, D]) for k in range(NC)]
        xn = [sb(f"xn_{k}", [P, TC, D]) for k in range(NC)]
        xnt = [sb(f"xnt{k}", [P, CH]) for k in range(NC)]
        bob, brb, wr = sb("bob", [P, D]), sb("brb", [P, NE]), sb("wr", [P, NE])
        st, mv = sb("st2", [P, TC, 6]), sb("mv2", [P, TC, 2])
        var, std, rstd = sb("var2", [P, TC]), sb("std2", [P, TC]), sb("rstd2", [P, TC])
        b_o = [bank(f"b_o{i}") for i in range(3)]
        b_t, b_l = bank("b_t"), bank("b_l")
        s_const, s_o, s_hb, s_h1, s_var, s_std, s_xn, s_xt, s_xts, s_lg, s_lgr, s_out, s_free, s_chain = (
            sem(n) for n in ("const", "o_ready", "h_bias", "h1_done", "var", "std", "xn_done", "xt_ready",
                             "xt_copied", "logit_ready", "logit_read", "stored", "out_free", "chain"))
        s_in = [sem(f"in{k}") for k in range(NC)]
        links = 5

        with nc.Block() as block:
            @block.sync
            def _(sp):
                sp.dma_start(bob[:, :], io.bo.partition_broadcast(P)).then_inc(s_const, 16)
                sp.dma_start(brb[:, :], io.br.partition_broadcast(P)).then_inc(s_const, 16)
                sp.dma_start(wr[:, :], io.Wr).then_inc(s_const, 16)

                def load(b, k):
                    sp.dma_start(ct[k][:, :], io.CT[ds(b, 1), :, k * CH:(k + 1) * CH].rearrange(
                        "o p s -> (o p) s")).then_inc(s_in[k], 16)
                    sp.dma_start(h0[k][:, :, :], io.H0[ds(b, 1), :, TC * k:TC * (k + 1), :].rearrange(
                        "o p t d -> (o p) t d")).then_inc(s_in[k], 16)

                def store(b, last):
                    for k in range(NC):
                        r = b * NC + k
                        sp.wait_ge(s_xn, r + 1)
                        sp.dma_start(io.H1[ds(r, 1)].rearrange("o p n -> (o p) n"),
                                     h1[k][:, :, :].rearrange("p t d -> p (t d)")).then_inc(s_out, 16)
                        sp.dma_start(io.XN[ds(r, 1)].rearrange("o p n -> (o p) n"),
                                     xn[k][:, :, :].rearrange("p t d -> p (t d)")).then_inc(s_out, 16)
                        if not last:
                            load(b + 1, k)
                    sp.wait_ge(s_out, 32 * NC * (b + 1))
                    sp.sem_inc(s_free, 1)

                sp.sem_inc(s_free, 1)
                for k in range(NC):
                    load(0, k)
                with sp.Fori(0, B - 1) as b:
                    store(b, False)
                store(B - 1, True)

            @block.gpsimd
            def _(pool):
                pool.wait_ge(s_const, 48)
                with pool.Fori(0, B) as b:
                    for k in range(NC):
                        r = b * NC + k
                        pool.wait_ge(s_in[k], 32 * (b + 1))
                        pool.tensor_tensor(h0[k][:, :, :], h0[k][:, :, :],
                                           bob[:, :].unsqueeze(1).to_broadcast([P, TC, D]), ALU.add).then_inc(s_hb, 1)

            @block.tensor
            def _(pe):
                pe.wait_ge(s_const, 48)
                with pe.Fori(0, B) as b:
                    for k in range(NC):
                        r = b * NC + k
                        pe.wait_ge(s_in[k], 32 * (b + 1))
                        pe.wait_ge(s_h1, r + 1)
                        for t in range(TC):
                            ins = pe.matmul(b_o[k][:, t * P:(t + 1) * P], ct[k][:, t * P:(t + 1) * P], g.wt[:, 3, :],
                                            start=True, stop=True)
                        ins.then_inc(s_o, 1)
                        pe.wait_ge(s_xn, r + 1)
                        for t in range(TC):
                            ins = pe.transpose(b_t[:, t * P:(t + 1) * P], xn[k][:, t, :], g.ident[:, :])
                        ins.then_inc(s_xt, 1)
                        pe.wait_ge(s_xts, r + 1)
                        pe.wait_ge(s_lgr, r + 1)
                        for t in range(TC):
                            ins = pe.matmul(b_l[:, t * NE:(t + 1) * NE], xnt[k][:, t * P:(t + 1) * P], wr[:, :],
                                            start=True, stop=True)
                        ins.then_inc(s_lg, 1)

            @block.scalar
            def _(act):
                with act.Fori(0, B) as b:
                    for k in range(NC):
                        r = b * NC + k
                        act.wait_ge(s_var, r + 1)
                        act.activation(std[:, :], var[:, :], ACT.Sqrt).then_inc(s_std, 1)
                        act.wait_ge(s_xt, r + 1)
                        act.activation(xnt[k][:, :], b_t[:, :], ACT.Identity).then_inc(s_xts, 1)

            @block.vector
            def _(dve):
                dve.sem_inc(s_h1, 1)
                dve.sem_inc(s_lgr, 1)
                dve.wait_ge(s_const, 48)
                with dve.Fori(0, B) as b:
                    dve.wait_ge(s_free, b + 1)
                    for k in range(NC):
                        r = b * NC + k
                        ch = Chain(dve, s_chain, r * links)
                        dve.wait_ge(s_hb, r + 1)
                        dve.wait_ge(s_o, r + 1)
                        dve.tensor_tensor(h1[k][:, :, :], b_o[k][:, :].rearrange("p (t d) -> p t d", t=TC),
                                          h0[k][:, :, :], ALU.add).then_inc(s_h1, 1)
                        dve.wait_ge(s_h1, r + 2)
                        for t in range(TC):
                            ins = dve.bn_stats(st[:, t, :], h1[k][:, t, :])
                        ch.add(ins)
                        ch.settle_apart()
                        for t in range(TC):
                            ins = dve.bn_aggr(mv[:, t, :], st[:, t, :])
                        ch.add(ins)
                        ch.settle()
                        dve.tensor_scalar(var[:, :], mv[:, :, 1], EPS, None, ALU.add).then_inc(s_var, 1)
                        dve.wait_ge(s_std, r + 1)
                        ch.add(dve.reciprocal(rstd[:, :], std[:, :]))
                        ch.settle()
                        for t in range(TC):
                            ins = dve.tensor_scalar(xn[k][:, t, :], h1[k][:, t, :], mv[:, t, 0:1], rstd[:, t:t + 1],
                                                    ALU.subtract, ALU.mult)
                        ch.add(ins)
                        ch.settle()
                        dve.sem_inc(s_xn, 1)
                        dve.wait_ge(s_lg, r + 1)
                        dve.tensor_tensor(g.lg[:, ds(r * TC, TC), :],
                                          b_l[:, 0:TC * NE].rearrange("p (t e) -> p t e", t=TC),
                                          brb[:, :].unsqueeze(1).to_broadcast([P, TC, NE]),
                                          ALU.add).then_inc(s_lgr, 1)
                        assert ch.n == links


def route_block(nc, ctx, io, g):
    with ExitStack() as c:
        def sb(name, shape, dt=F32):
            return c.enter_context(nc.sbuf_tensor(name, shape, dt))

        def sem(name):
            return ctx.enter_context(nc.semaphore("ro_" + name))

        rank, index, before = sb("rank", [P, NE]), sb("index", [P, SLOTS]), sb("before", [P, NE, NE])
        tri, ones, last = sb("tri", [P, P]), sb("ones", [P, P]), sb("last", [P, 1])
        l2, key, oh0, oh1 = (sb(n, [P, NG, NE]) for n in ("l2", "key", "oh0", "oh1"))
        sa, sbb = sb("scan_a", [P, NG, NE]), sb("scan_b", [P, NG, NE])
        v0, v1, r0, r1, gap, ex, den, s0, s1, e0, e1, imax, tmp, posf = (
            sb(n, [P, NG]) for n in ("v0", "v1", "r0", "r1", "gap", "ex", "den", "s0", "s1", "e0", "e1", "imax",
                                     "tmpg", "posf"))
        cnt = sb("cnt", [P, 2, NE])
        full = sb("fullm", [P, 2, NE])
        drop, kept = sb("drop", [P, 2]), sb("kept", [P, 2])
        dsel = sb("dsel", [P, 2, NE])
        tot, nt, start, end, base = (sb(n, [P, NE]) for n in ("tot", "ntile", "start", "end", "base"))
        cmp_t, cmp_s, bsel = sb("cmp_t", [P, NE, NG]), sb("cmp_s", [P, SLOTS, NE]), sb("bsel", [P, NE, NE])
        tef = sb("tef", [P, SLOTS])
        cxl = sb("cxl", [P, 2])
        h1l, xnl = sb("h1l", [P, D]), sb("xnl", [P, D])
        rows, idx = [sb(f"rows{i}", [P, TC, D]) for i in range(2)], [sb(f"idx{i}", [P, TC], I32) for i in range(2)]
        bc, bp = (c.enter_context(nc.psum_tensor(n, [P, CH], F32)) for n in ("bc", "bp"))
        s_in, s_v, s_cnt, s_gap, s_ex, s_tp, s_pre, s_fix, s_fixed, s_pos = (
            sem(n) for n in ("in", "chain", "counts", "gap", "exp", "per_part", "prefix", "fix", "fixed", "pos"))
        s_row, s_idx, s_sc, s_apart = [sem("row0"), sem("row1")], sem("idx"), [sem("scat0"), sem("scat1")], sem("apart")
        TAIL = NR - 1
        with nc.Block() as block:
            @block.sync
            def _(sp):
                for dst, src in ((rank[:, :], io.rank), (index[:, :], io.index), (before[:, :, :], io.before),
                                 (tri[:, :], io.tri), (ones[:, :], io.ones), (last[:, :], io.last),
                                 (h1l[:, :], io.H1[TAIL, :, (TC - 1) * D:TC * D]),
                                 (xnl[:, :], io.XN[TAIL, :, (TC - 1) * D:TC * D])):
                    sp.dma_start(dst, src).then_inc(s_in, 16)
                sp.wait_ge(s_fix, 1)
                sp.dma_start(io.H1[TAIL, :, (TC - 1) * D:TC * D], h1l[:, :]).then_inc(s_fixed, 16)
                sp.wait_ge(s_fixed, 16)

            @block.scalar
            def _(act):
                act.wait_ge(s_gap, 1)
                act.activation(ex[:, :], gap[:, :], ACT.Exp).then_inc(s_ex, 1)

            @block.tensor
            def _(pe):
                pe.wait_ge(s_in, 16 * 8)
                pe.wait_ge(s_cnt, 1)
                pe.matmul(bc[:, 0:2 * NE], ones[:, :], cnt[:, :, :].rearrange("p a e -> p (a e)"), start=True,
                          stop=True).then_inc(s_pre, 1)
                pe.wait_ge(s_tp, 1)
                pe.matmul(bp[:, 0:NE], tri[:, :], sa[:, NG - 1, :], start=True, stop=True)
                pe.matmul(bp[:, NE:2 * NE], ones[:, :], sa[:, NG - 1, :], start=True, stop=True).then_inc(s_pre, 1)

            @block.vector
            def _(dve):
                ch = Chain(dve, s_v)

                def do(ins):
                    ch.add(ins)
                    ch.settle()

                def over_e(x):
                    return x.unsqueeze(2).to_broadcast([P, NG, NE])

                def over_g(x):
                    return x.unsqueeze(1).to_broadcast([P, NG, NE])

                dve.wait_ge(s_in, 16 * 8)
                for lg, v, r, oh in ((g.lg, v0, r0, oh0), (l2, v1, r1, oh1)):
                    if lg is l2:
                        do(dve.scalar_tensor_tensor(l2[:, :, :], oh0[:, :, :], -3e38, g.lg[:, :, :], ALU.mult, ALU.add))
                    do(dve.tensor_reduce(v[:, :], lg[:, :, :], AX.X, ALU.max))
                    do(dve.tensor_tensor(key[:, :, :], lg[:, :, :], over_e(v[:, :]), ALU.is_equal))
                    do(dve.tensor_tensor(oh[:, :, :], key[:, :, :], over_g(rank[:, :]), ALU.mult))
                    do(dve.tensor_reduce(r[:, :], oh[:, :, :], AX.X, ALU.max))
                    do(dve.tensor_tensor(oh[:, :, :], oh[:, :, :], over_e(r[:, :]), ALU.is_equal))
                dve.tensor_tensor(gap[:, :], v1[:, :], v0[:, :], ALU.subtract).then_inc(s_gap, 1)
                ch.add(dve.tensor_reduce(cnt[:, 0, :], oh0[:, :, :].rearrange("p g e -> p e g"), AX.X, ALU.add))
                ch.add(dve.tensor_tensor(key[:, :, :], oh0[:, :, :], oh1[:, :, :], ALU.add))
                ch.settle()
                dve.tensor_reduce(cnt[:, 1, :], key[:, :, :].rearrange("p g e -> p e g"), AX.X, ALU.add).then_inc(s_cnt, 1)
                dve.wait_ge(s_pre, 1)
                do(dve.tensor_scalar(full[:, :, :], bc[:, 0:2 * NE].rearrange("p (a e) -> p a e", a=2),
                                     float(TOKENS), last[:, 0:1], ALU.is_ge, ALU.mult))
                ch.add(dve.tensor_tensor(dsel[:, 0, :], full[:, 0, :], oh0[:, NG - 1, :], ALU.mult))
                ch.add(dve.tensor_tensor(dsel[:, 1, :], full[:, 1, :], oh1[:, NG - 1, :], ALU.mult))
                ch.settle()
                do(dve.tensor_reduce(drop[:, :], dsel[:, :, :], AX.X, ALU.add))
                do(dve.tensor_scalar(kept[:, :], drop[:, :], -1.0, 1.0, ALU.mult, ALU.add))
                ch.add(dve.tensor_scalar(e0[:, :], r0[:, :], -1.0, float(NE), ALU.mult, ALU.add))
                ch.add(dve.tensor_scalar(e1[:, :], r1[:, :], -1.0, float(NE), ALU.mult, ALU.add))
                ch.settle()
                tail = slice(NG - 1, NG)
                ch.add(dve.tensor_tensor(e0[:, tail], e0[:, tail], kept[:, 0:1], ALU.mult))
                ch.add(dve.tensor_tensor(e1[:, tail], e1[:, tail], kept[:, 1:2], ALU.mult))
                ch.settle()
                do(dve.tensor_tensor(imax[:, :], e0[:, :], e1[:, :], ALU.max))
                dve.wait_ge(s_ex, 1)
                do(dve.tensor_scalar(den[:, :], ex[:, :], 1.0, None, ALU.add))
                do(dve.reciprocal(s0[:, :], den[:, :]))
                do(dve.tensor_tensor(s1[:, :], s0[:, :], ex[:, :], ALU.mult))
                ch.add(dve.tensor_tensor(cxl[:, 0:1], s0[:, tail], drop[:, 0:1], ALU.mult))
                ch.add(dve.tensor_tensor(cxl[:, 1:2], s1[:, tail], drop[:, 1:2], ALU.mult))
                ch.settle()
                do(dve.tensor_tensor(cxl[:, 0:1], cxl[:, 0:1], cxl[:, 1:2], ALU.add))
                dve.scalar_tensor_tensor(h1l[:, :], xnl[:, :], cxl[:, 0:1], h1l[:, :], ALU.mult,
                                         ALU.add).then_inc(s_fix, 1)
                ch.add(dve.tensor_tensor(s0[:, tail], s0[:, tail], kept[:, 0:1], ALU.mult))
                ch.add(dve.tensor_tensor(s1[:, tail], s1[:, tail], kept[:, 1:2], ALU.mult))
                ch.settle()
                do(dve.tensor_tensor(g.cy[:, :], s0[:, :], s1[:, :], ALU.add))
                do(dve.tensor_tensor(oh0[:, :, :], over_e(imax[:, :]), over_g(index[:, 0:NE]), ALU.is_equal))
                src, dst, step = oh0, sbb, 1
                while step < NG:
                    ch.add(dve.tensor_copy(dst[:, 0:step, :], src[:, 0:step, :]))
                    ch.add(dve.tensor_tensor(dst[:, step:NG, :], src[:, step:NG, :], src[:, 0:NG - step, :], ALU.add))
                    ch.settle()
                    src, dst, step = dst, (sa if dst is sbb else sbb), 2 * step
                assert src is sbb
                do(dve.tensor_copy(sa[:, :, :], sbb[:, :, :]))
                dve.sem_inc(s_tp, 1)
                dve.wait_ge(s_pre, 2)
                do(dve.tensor_copy(tot[:, :], bp[:, NE:2 * NE]))
                do(dve.tensor_scalar(posf[:, :], index[:, 0:NG], float(P), None, ALU.mult))
                do(dve.tensor_tensor(cmp_t[:, :, :], tot[:, :].unsqueeze(2).to_broadcast([P, NE, NG]),
                                     posf[:, :].unsqueeze(1).to_broadcast([P, NE, NG]), ALU.is_gt))
                do(dve.tensor_reduce(nt[:, :], cmp_t[:, :, :], AX.X, ALU.add))
                do(dve.tensor_tensor(bsel[:, :, :], before[:, :, :], nt[:, :].unsqueeze(1).to_broadcast([P, NE, NE]),
                                     ALU.mult))
                do(dve.tensor_reduce(start[:, :], bsel[:, :, :], AX.X, ALU.add))
                do(dve.tensor_tensor(end[:, :], start[:, :], nt[:, :], ALU.add))
                do(dve.tensor_scalar(base[:, :], start[:, :], float(P), -1.0, ALU.mult, ALU.add))
                do(dve.tensor_tensor(base[:, :], bp[:, 0:NE], base[:, :], ALU.add))
                do(dve.tensor_tensor(key[:, :, :], sa[:, :, :], over_g(base[:, :]), ALU.add))
                do(dve.tensor_tensor(key[:, :, :], key[:, :, :], oh0[:, :, :], ALU.mult))
                do(dve.tensor_reduce(posf[:, :], key[:, :, :], AX.X, ALU.add))
                do(dve.tensor_copy(g.pos[:, :], posf[:, :]))
                dve.sem_inc(s_pos, 1)
                do(dve.tensor_tensor(cmp_s[:, :, :], index[:, :].unsqueeze(2).to_broadcast([P, SLOTS, NE]),
                                     end[:, :].unsqueeze(1).to_broadcast([P, SLOTS, NE]), ALU.is_ge))
                do(dve.tensor_reduce(tef[:, :], cmp_s[:, :, :], AX.X, ALU.add))
                do(dve.tensor_scalar(tef[:, :], tef[:, :], float(NE - 1), None, ALU.min))
                do(dve.tensor_copy(g.te[:, :], tef[:, :]))

            @block.gpsimd
            def _(pool):
                pool.wait_ge(s_pos, 1)
                with pool.Fori(0, NR // 2) as i:
                    for p in range(2):
                        pool.dma_start(rows[p][:, :, :].rearrange("p t d -> p (t d)"),
                                       io.XN[ds(2 * i + p, 1)].rearrange("o p n -> (o p) n")).then_inc(s_row[p], 16)
                        pool.tensor_copy(idx[p][:, :], g.pos[:, ds((2 * i + p) * TC, TC)]).then_inc(s_idx, 1)
                        pool.wait_ge(s_row[p], 16 * (i + 1))
                        pool.wait_ge(s_idx, 2 * i + p + 1)
                        pool.sem_inc(s_apart, 1)
                        for t in range(TC):
                            pool.indirect_dma_start(io.XS, bass.IndirectOffsetOnAxis(idx[p][:, t:t + 1], 0),
                                                    rows[p][:, t, :], None).then_inc(s_sc[p], 16)
                        if p == 1:
                            for q in range(2):
                                pool.wait_ge(s_sc[q], 16 * TC * (i + 1))
                            pool.sem_inc(s_apart, 1)
                pool.wait_ge(s_apart, 3 * (NR // 2))


def expert_block(nc, ctx, io, g):
    with ExitStack() as c:
        def sb(name, shape, dt=F32):
            return c.enter_context(nc.sbuf_tensor(name, shape, dt))

        def bank(name):
            return c.enter_context(nc.psum_tensor(name, [P, CH], F32))

        def sem(name):
            return ctx.enter_context(nc.semaphore("ex_" + name))

        w1, w2 = sb("w1", [P, NE, HID]), sb("w2", [P, NE, HID])
        w3 = sb("w3", [P, NE, TC, D])
        x = [sb(f"ex_x{i}", [P, D]) for i in range(2)]
        xt = [sb(f"ex_xt{i}", [P, P]) for i in range(2)]
        h1s = [sb(f"ex_h{i}", [P, HID]) for i in range(2)]
        pr = [sb(f"ex_pr{i}", [P, HID]) for i in range(2)]
        gl = [sb(f"ex_gl{i}", [P, HID]) for i in range(2)]
        gt = [sb(f"ex_gt{i}", [P, HID]) for i in range(2)]
        y = [sb(f"ex_y{i}", [P, D]) for i in range(2)]
        b_x, b_y = bank("b_x"), bank("b_y")
        b1, b2, bg = ([bank(f"{n}{i}") for i in range(2)] for n in ("b1_", "b2_", "bg_"))
        s_w, s_xt, s_xts, s_h, s_h1, s_pr, s_gl, s_gt, s_gts, s_y, s_ys, s_out = (
            sem(n) for n in ("weights", "xt_ready", "xt_copied", "h_ready", "h1_copied", "product", "gelu",
                             "gt_ready", "gt_copied", "y_ready", "y_copied", "stored"))
        s_x, s_yfree = [sem("x0_in"), sem("x1_in")], sem("y_free")
        with nc.Block() as block:
            @block.sync
            def _(sp):
                sp.dma_start(w2[:, :, :], io.W2.rearrange("e k h -> k e h")).then_inc(s_w, 16)
                sp.dma_start(w1[:, :, :], io.W1.rearrange("e k h -> k e h")).then_inc(s_w, 16)
                sp.dma_start(w3[:, :, :, :], io.W3.rearrange("e (c k) d -> k e c d", k=P)).then_inc(s_w, 16)
                xs = io.XS.rearrange("(s p) d -> s p d", p=P)
                ys = io.YS.rearrange("(s p) d -> s p d", p=P)

                def load(s, p):
                    sp.dma_start(x[p][:, :], xs[ds(s, 1)].rearrange("o p d -> (o p) d")).then_inc(s_x[p], 16)
                for p in range(2):
                    load(p, p)

                def turn(i, more):
                    for p in range(2):
                        s = 2 * i + p
                        if more:
                            sp.wait_ge(s_xt, s + 1)
                            load(s + 2, p)
                        sp.wait_ge(s_ys, s + 2)
                        sp.dma_start(ys[ds(s, 1)].rearrange("o p d -> (o p) d"), y[p][:, :]).then_inc(s_out, 16)
                        sp.wait_ge(s_out, 16 * (s + 1))
                        sp.sem_inc(s_yfree, 1)

                sp.sem_inc(s_yfree, 2)
                with sp.Fori(0, SLOTS // 2 - 1) as i:
                    turn(i, True)
                turn(SLOTS // 2 - 1, False)

            @block.tensor
            def _(pe):
                pe.wait_ge(s_w, 48)

                def first(s, p, nth):
                    pe.wait_ge(s_x[p], 16 * nth)
                    pe.transpose(b_x[:, 0:P], x[p][:, :], g.ident[:, :]).then_inc(s_xt, 1)
                    e = pe.value_load(g.te[0:1, ds(s, 1)], min_val=0, max_val=NE - 1)
                    pe.wait_ge(s_xts, s + 1)
                    pe.wait_ge(s_pr, s + 1)
                    pe.matmul(b1[p][:, :], xt[p][:, :], w1[:, ds(e, 1), :].rearrange("p o h -> p (o h)"),
                              start=True, stop=True)
                    pe.matmul(b2[p][:, :], xt[p][:, :], w2[:, ds(e, 1), :].rearrange("p o h -> p (o h)"),
                              start=True, stop=True).then_inc(s_h, 1)

                def second(s, p):
                    pe.wait_ge(s_gl, s + 1)
                    for q in range(TC):
                        ins = pe.transpose(bg[p][:, q * P:(q + 1) * P], gl[p][:, q * P:(q + 1) * P], g.ident[:, :])
                    ins.then_inc(s_gt, 1)
                    e = pe.value_load(g.te[0:1, ds(s, 1)], min_val=0, max_val=NE - 1)
                    pe.wait_ge(s_gts, s + 1)
                    pe.wait_ge(s_ys, s + 1)
                    for q in range(TC):
                        ins = pe.matmul(b_y[:, 0:D], gt[p][:, q * P:(q + 1) * P],
                                        w3[:, ds(e, 1), q, :].rearrange("p o d -> p (o d)"), start=(q == 0),
                                        stop=(q == TC - 1))
                    ins.then_inc(s_y, 1)

                first(0, 0, 1)
                with pe.Fori(0, SLOTS // 2 - 1) as i:
                    first(2 * i + 1, 1, i + 1)
                    second(2 * i, 0)
                    first(2 * i + 2, 0, i + 2)
                    second(2 * i + 1, 1)
                first(SLOTS - 1, 1, SLOTS // 2)
                second(SLOTS - 2, 0)
                second(SLOTS - 1, 1)

            @block.scalar
            def _(act):
                def first(s, p):
                    act.wait_ge(s_xt, s + 1)
                    act.activation(xt[p][:, :], b_x[:, 0:P], ACT.Identity).then_inc(s_xts, 1)
                    act.wait_ge(s_h, s + 1)
                    act.activation(h1s[p][:, :], b1[p][:, :], ACT.Identity).then_inc(s_h1, 1)

                def second(s, p):
                    act.wait_ge(s_pr, s + 3)
                    act.activation(gl[p][:, :], pr[p][:, :], ACT.Gelu).then_inc(s_gl, 1)

                first(0, 0)
                with act.Fori(0, SLOTS // 2 - 1) as i:
                    second(2 * i, 0)
                    first(2 * i + 1, 1)
                    second(2 * i + 1, 1)
                    first(2 * i + 2, 0)
                second(SLOTS - 2, 0)
                first(SLOTS - 1, 1)
                second(SLOTS - 1, 1)

            @block.vector
            def _(dve):
                dve.sem_inc(s_pr, 2)
                dve.sem_inc(s_ys, 1)

                def first(s, p):
                    dve.wait_ge(s_h1, s + 1)
                    dve.tensor_tensor(pr[p][:, :], b2[p][:, :], h1s[p][:, :], ALU.mult).then_inc(s_pr, 1)

                def second(s, p):
                    dve.wait_ge(s_gt, s + 1)
                    dve.tensor_copy(gt[p][:, :], bg[p][:, :]).then_inc(s_gts, 1)
                    dve.wait_ge(s_y, s + 1)
                    dve.wait_ge(s_yfree, s + 1)
                    dve.tensor_copy(y[p][:, :], b_y[:, 0:D]).then_inc(s_ys, 1)

                first(0, 0)
                with dve.Fori(0, SLOTS // 2 - 1) as i:
                    first(2 * i + 1, 1)
                    second(2 * i, 0)
                    first(2 * i + 2, 0)
                    second(2 * i + 1, 1)
                first(SLOTS - 1, 1)
                second(SLOTS - 2, 0)
                second(SLOTS - 1, 1)


def combine_block(nc, ctx, io, g):
    with ExitStack() as c:
        def sb(name, shape, dt=F32):
            return c.enter_context(nc.sbuf_tensor(name, shape, dt))

        def sem(name):
            return ctx.enter_context(nc.semaphore("co_" + name))

        idx = [sb(f"co_idx{i}", [P, TC], I32) for i in range(2)]
        cy = [sb(f"co_cy{i}", [P, TC]) for i in range(2)]
        yg = [sb(f"co_y{i}", [P, TC, D]) for i in range(2)]
        h1 = [sb(f"co_h{i}", [P, TC, D]) for i in range(2)]
        o = [sb(f"co_o{i}", [P, TC, D]) for i in range(2)]
        s_idx, s_done, s_out, s_ofree = sem("idx"), sem("done"), sem("stored"), sem("out_free")
        s_y, s_h = [sem("y0"), sem("y1")], [sem("h0"), sem("h1")]
        with nc.Block() as block:
            @block.gpsimd
            def _(pool):
                pool.sem_inc(s_done, 2)
                with pool.Fori(0, NR // 2) as i:
                    for p in range(2):
                        r = 2 * i + p
                        pool.wait_ge(s_done, r + 1)
                        pool.sem_inc(s_idx, 1)
                        pool.tensor_copy(idx[p][:, :], g.pos[:, ds(r * TC, TC)]).then_inc(s_idx, 1)
                        pool.wait_ge(s_idx, 3 * r + 2)
                        pool.sem_inc(s_idx, 1)
                        for t in range(TC):
                            pool.indirect_dma_start(yg[p][:, t, :], None, io.YS,
                                                    bass.IndirectOffsetOnAxis(idx[p][:, t:t + 1], 0)).then_inc(s_y[p], 16)

            @block.sync
            def _(sp):
                rows = io.out.rearrange("b s d -> (b s) d").rearrange("(r t p) d -> r p t d", t=TC, p=P)

                def load(r, p):
                    sp.dma_start(h1[p][:, :, :].rearrange("p t d -> p (t d)"),
                                 io.H1[ds(r, 1)].rearrange("o p n -> (o p) n")).then_inc(s_h[p], 16)

                def turn(i, more):
                    for p in range(2):
                        r = 2 * i + p
                        sp.wait_ge(s_done, r + 3)
                        if more:
                            load(r + 2, p)
                        sp.dma_start(rows[ds(r, 1)].rearrange("o p t d -> (o p) t d"), o[p][:, :, :]).then_inc(s_out, 16)
                        sp.wait_ge(s_out, 16 * (r + 1))
                        sp.sem_inc(s_ofree, 1)

                sp.sem_inc(s_ofree, 2)
                for p in range(2):
                    load(p, p)
                with sp.Fori(0, NR // 2 - 1) as i:
                    turn(i, True)
                turn(NR // 2 - 1, False)

            @block.vector
            def _(dve):
                with dve.Fori(0, NR // 2) as i:
                    for p in range(2):
                        r = 2 * i + p
                        dve.wait_ge(s_y[p], 16 * TC * (i + 1))
                        dve.wait_ge(s_h[p], 16 * (i + 1))
                        dve.wait_ge(s_ofree, r + 1)
                        for t in range(TC):
                            ins = dve.scalar_tensor_tensor(o[p][:, t, :], yg[p][:, t, :], g.cy[:, ds(r * TC + t, 1)],
                                                           h1[p][:, t, :], ALU.mult, ALU.add)
                        ins.then_inc(s_done, 1)


STAGES = (setup_block, embed_block, attend_block, project_block, route_block, expert_block, combine_block)


def program(nc, io):
    def dram(name, shape, dt=F32):
        return nc.dram_tensor(name, shape, dt, kind="Internal").ap()

    io.H0 = dram("h0_rows", (B, P, NT, D))
    io.QK = dram("qk_parts", (UNITS + 1, 2, PART, S), F16)
    io.VS = dram("v_rows", (UNITS + 1, P, NT * VW))
    io.WP3 = dram("wpos_parts", (NH + 1, PART, 2 * D), F16)
    io.CT = dram("context", (B, P, S))
    io.H1 = dram("residual", (NR, P, TC * D))
    io.XN = dram("normed_rows", (NR, P, TC * D))
    io.XS = dram("routed_rows", (SLOTS * P, D))
    io.YS = dram("expert_rows", (SLOTS * P, D))
    with ExitStack() as ctx:
        def sb(name, shape, dt=F32):
            return ctx.enter_context(nc.sbuf_tensor(name, shape, dt))

        g = Names()
        g.ident, g.ident16 = sb("ident_sb", [P, P]), sb("ident16_sb", [P, P], F16)
        g.wt = sb("wt", [P, 4, D])
        g.bqs, g.bk, g.gamma, g.beta = (sb(n, [P, 1]) for n in ("bqs", "bk_sb", "gamma_sb", "beta_sb"))
        g.rb = sb("rb", [P, 2, NH + 1])
        g.lg = sb("logits", [P, NG, NE])
        g.cy = sb("cy", [P, NG])
        g.pos = sb("pos", [P, NG], I32)
        g.te = sb("tile_expert", [P, SLOTS], I32)
        for stage in STAGES:
            stage(nc, ctx, io, g)


def tables():
    half = D // 2
    f = np.exp(np.arange(0, D, 2, dtype=np.float32) * np.float32(-np.log(10000.0) / D))
    w = f.astype(np.float64)[:, None]

    def table(n):
        return np.concatenate([np.sin(w * n), np.cos(w * n)], 0)

    j = np.arange(S, dtype=np.float64)[None, :]
    tabs = []
    for t in (table(j), table(j - S)):
        hi = t.astype(np.float16)
        tabs += [hi, (t - hi.astype(np.float64)).astype(np.float16)]
    turn = w * (S - 1 - j)
    rot = np.stack([np.concatenate([np.cos(turn), np.cos(turn)], 0), np.concatenate([-np.sin(turn), np.sin(turn)], 0)])
    pos = np.arange(2 * S_IMG, dtype=np.float32)[:, None]
    pe = np.zeros((2 * S_IMG, D), np.float32)
    pe[:, 0::2] = np.sin(pos * f)
    pe[:, 1::2] = np.cos(pos * f)
    row, col = np.arange(P)[:, None], np.arange(DW)[None, :]
    heads = np.zeros((P, NH + 1), np.float32)
    heads[np.arange(P), np.arange(P) // DH] = 1
    heads[:, NH] = heads[:, 0]
    pick = np.zeros((P, 2, 2, VW), np.float32)
    for g in range(4):
        for what in range(2):
            for par in range(2):
                for d in range(DH):
                    pick[g * VW + what * DH + d, what, par, par * DH + d] = 1
    last = np.zeros((P, 1), np.float32)
    last[P - 1] = 1
    c = {
        "pe_tok": pe[:S_IMG],
        "tabs": np.stack(tabs),
        "rot": rot.astype(np.float32),
        "ident": np.eye(P, dtype=np.float32),
        "ident16": np.eye(P, dtype=np.float16),
        "mask1": np.repeat((row < col).astype(np.float32)[:, None], 3, 1),
        "mask2": np.repeat((row > col).astype(np.int32)[:, None], 3, 1),
        "head_mask": heads,
        "pick": pick,
        "last": last,
        "tri": (row < np.arange(P)[None, :]).astype(np.float32),
        "ones": np.ones((P, P), np.float32),
        "rank": np.broadcast_to(NE - np.arange(NE, dtype=np.float32), (P, NE)).copy(),
        "index": np.broadcast_to(np.arange(SLOTS, dtype=np.float32), (P, SLOTS)).copy(),
        "before": np.broadcast_to((np.arange(NE)[None, :] < np.arange(NE)[:, None]).astype(np.float32),
                                  (P, NE, NE)).copy(),
    }
    return c


_INS = ["x", "txt", "L0_tok_W", "L0_attn_gamma", "L0_attn_beta", "L0_attn_Wq", "L0_attn_bq", "L0_attn_Wk",
        "L0_attn_bk", "L0_attn_Wv", "L0_attn_bv", "L0_attn_Wpos", "L0_attn_u_bias", "L0_attn_v_bias", "L0_attn_Wo",
        "L0_attn_bo", "L0_ffn_Wr", "L0_ffn_br", "L0_ffn_W1", "L0_ffn_W2", "L0_ffn_W3"]
_SHORT = ["x", "txt", "Wtok", "gamma", "beta", "Wq", "bq", "Wk", "bk", "Wv", "bv", "Wpos", "u", "v", "Wo", "bo",
          "Wr", "br", "W1", "W2", "W3"]


def kernel(**inputs):
    import concourse.bacc as bacc
    from concourse.bass_utils import run_bass_kernel_spmd

    nc = bacc.Bacc("TRN2", target_bir_lowering=False, num_devices=1)
    arrays, io = {}, Names()
    given = [(short, inputs[name]) for short, name in zip(_SHORT, _INS)] + list(tables().items())
    for name, a in given:
        a = np.ascontiguousarray(a)
        arrays[f"in_{name}"] = a
        vars(io)[name] = nc.dram_tensor(f"in_{name}", a.shape, mybir.dt.from_np(a.dtype), kind="ExternalInput").ap()
    io.out = nc.dram_tensor("out", (B, S, D), F32, kind="ExternalOutput").ap()
    program(nc, io)
    r = run_bass_kernel_spmd(nc, [arrays], core_ids=[0])
    return r.results[0]["out"]
```

```python
from contextlib import ExitStack

import numpy as np

import concourse.bass as bass
from concourse import mybir

F32 = mybir.dt.float32
F16 = mybir.dt.float16
I32 = mybir.dt.int32
U32 = mybir.dt.uint32
ACT = mybir.ActivationFunctionType
ALU = mybir.AluOpType
AX = mybir.AxisListType
ds = bass.ds

P = 128
B = 8
S_IMG, S_TXT = 1024, 512
S = S_IMG + S_TXT
D = 128
NH, DH = 8, 16
UNITS = B * NH
F_IN = 29
NE = 8
HID = 512
CH = 512
NT = S // P
NC = S // CH
TC = CH // P
NG = B * NT
NR = B * NC
TOKENS = B * S
SLOTS = NG + NE
PART = 3 * DH
EPS = 1e-5
QSCALE = float(1.0 / np.sqrt(np.float32(D)))
WSCALE = 64.0
UNROLL = 4
RING = 4
VW = 2 * DH
DW = P + 1


class Chain:

    def __init__(self, eng, sem, base=0):
        self.eng, self.sem, self.base, self.n = eng, sem, base, 0

    def add(self, ins):
        ins.then_inc(self.sem, 1)
        self.n += 1

    def settle(self):
        self.eng.wait_ge(self.sem, self.base + self.n)

    def settle_apart(self):
        self.settle()
        self.eng.sem_inc(self.sem, 1)
        self.n += 1


class Names:
    pass


def setup_block(nc, ctx, io, g):
    with ExitStack() as c:
        def sb(name, shape, dt=F32):
            return c.enter_context(nc.sbuf_tensor(name, shape, dt))

        def sem(name):
            return ctx.enter_context(nc.semaphore(name))

        wnat = sb("wnat", [P, 5, D])
        wph = sb("wph", [P, 2, D], F16)
        wpl = sb("wpl", [P, 2, D], F16)
        wpp = sb("wpp", [P, 2, D])
        vec = sb("vec", [P, 4])
        tmp = sb("tmp", [P, 4])
        hm = sb("hm", [P, NH + 1])
        bd = sb("bd", [P, NH + 1])
        zero = sb("zero", [P, 8 * D])
        pw = c.enter_context(nc.psum_tensor("pw", [P, 4, D], F32))
        prb = c.enter_context(nc.psum_tensor("prb", [P, 2, NH + 1], F32))
        s_in, s_wt, s_rb, s_chain, s_wp, s_zero, s_out, s_bd = (
            sem(n) for n in ("su_in", "su_wt", "su_rb", "su_chain", "su_wp", "su_zero", "su_out", "su_bd"))
        loads = [
            (wnat[:, 0, :], io.Wq), (wnat[:, 1, :], io.Wk), (wnat[:, 2, :], io.Wv), (wnat[:, 3, :], io.Wo),
            (wnat[:, 4, :], io.Wpos), (g.ident[:, :], io.ident), (g.ident16[:, :], io.ident16),
            (vec[:, 0:1], io.bq.unsqueeze(1)), (vec[:, 1:2], io.u.rearrange("h d -> (h d)").unsqueeze(1)),
            (vec[:, 2:3], io.v.rearrange("h d -> (h d)").unsqueeze(1)),
            (g.bk[:, 0:1], io.bk.unsqueeze(1)), (g.gamma[:, 0:1], io.gamma.unsqueeze(1)),
            (g.beta[:, 0:1], io.beta.unsqueeze(1)), (hm[:, :], io.head_mask),
        ]
        with nc.Block() as block:
            @block.sync
            def _(sp):
                for dst, src in loads:
                    sp.dma_start(dst, src).then_inc(s_in, 16)
                sp.wait_ge(s_zero, 1)
                rows = io.XS.rearrange("(p r) d -> p (r d)", p=P)
                for i in range(SLOTS // 8):
                    sp.dma_start(rows[:, i * 8 * D:(i + 1) * 8 * D], zero[:, :]).then_inc(s_out, 16)
                sp.wait_ge(s_wp, 1)
                for part, w in enumerate((wph, wpl, wph)):
                    rows = slice(part * DH, (part + 1) * DH)
                    sp.dma_start(io.WP3[0:NH, rows, :], w[:, :, :].rearrange("p a k -> p (a k)")).then_inc(s_out, 16)
                    sp.dma_start(io.WP3[NH, rows, :], w[0:DH, :, :].rearrange("p a k -> p (a k)")).then_inc(s_out, 16)
                sp.wait_ge(s_out, 16 * (SLOTS // 8 + 6))

            @block.tensor
            def _(pe):
                pe.wait_ge(s_in, 16 * len(loads))
                for i in range(4):
                    ins = pe.transpose(pw[:, i, :], wnat[:, i, :], g.ident[:, :])
                ins.then_inc(s_wt, 1)
                pe.wait_ge(s_bd, 1)
                for i in range(2):
                    ins = pe.matmul(prb[:, i, :], wpp[:, i, :], bd[:, :], start=True, stop=True)
                ins.then_inc(s_rb, 1)

            @block.vector
            def _(dve):
                ch = Chain(dve, s_chain)
                dve.memset(zero[:, :], 0.0).then_inc(s_zero, 1)
                dve.wait_ge(s_in, 16 * len(loads))
                ch.add(dve.tensor_tensor(tmp[:, 0:1], vec[:, 0:1], vec[:, 1:2], ALU.add))
                ch.add(dve.tensor_tensor(tmp[:, 1:2], vec[:, 2:3], vec[:, 1:2], ALU.subtract))
                wp = wnat[:, 4, :].rearrange("p (k two) -> p two k", two=2)
                half = D // 2
                ch.add(dve.tensor_copy(wpp[:, 0, 0:half], wp[:, 0, :]))
                ch.add(dve.tensor_copy(wpp[:, 0, half:D], wp[:, 1, :]))
                ch.add(dve.tensor_copy(wpp[:, 1, 0:half], wp[:, 1, :]))
                ch.add(dve.tensor_copy(wpp[:, 1, half:D], wp[:, 0, :]))
                ch.settle()
                ch.add(dve.tensor_scalar(g.bqs[:, 0:1], tmp[:, 0:1], QSCALE, None, ALU.mult))
                ch.add(dve.tensor_scalar(tmp[:, 2:3], tmp[:, 1:2], QSCALE, None, ALU.mult))
                ch.add(dve.tensor_copy(wph[:, :, :], wpp[:, :, :]))
                ch.settle()
                dve.tensor_scalar(bd[:, :], hm[:, :], tmp[:, 2:3], None, ALU.mult).then_inc(s_bd, 1)
                dve.tensor_tensor(wpl[:, :, :], wpp[:, :, :], wph[:, :, :], ALU.subtract).then_inc(s_wp, 1)
                dve.wait_ge(s_wt, 1)
                dve.tensor_copy(g.wt[:, :, :], pw[:, :, :])
                dve.wait_ge(s_rb, 1)
                dve.tensor_copy(g.rb[:, :, :], prb[:, :, :])


def embed_block(nc, ctx, io, g):
    with ExitStack() as c:
        def sb(name, shape, dt=F32):
            return c.enter_context(nc.sbuf_tensor(name, shape, dt))

        def bank(name):
            return c.enter_context(nc.psum_tensor(name, [P, CH], F32))

        def sem(name):
            return ctx.enter_context(nc.semaphore(name))

        x8 = sb("x8", [P, 8, F_IN])
        pe_tok = sb("pe_tok", [P, 8, D])
        wtok = sb("wtok", [F_IN, D])
        bvb = sb("bvb", [P, D])
        xt = sb("xt", [F_IN, 2, CH])
        h = sb("h", [P, NT, D])
        z = sb("z", [P, NT, D])
        z2 = [sb(f"z2_{p}", [P, NT, D]) for p in range(2)]
        st = sb("st", [P, NT, 6])
        mv = sb("mv", [P, NT, 2])
        std = sb("std", [P, NT])
        rstd = sb("rstd", [P, NT])
        var = sb("var", [P, NT])
        xn = sb("xn", [P, S])
        full = sb("full", [P, 2, S])
        hi, lo = ([sb(f"{n}{p}", [P, 2, S], F16) for p in range(2)] for n in ("hi", "lo"))
        vals = [sb(f"vals{p}", [P, NH, NT, VW]) for p in range(2)]
        b_xt, b_emb, b_z, b_q, b_k = (bank(n) for n in ("b_xt", "b_emb", "b_z", "b_q", "b_k"))
        b_v = [bank(f"b_v{i}") for i in range(NC)]
        (s_const, s_x, s_xt, s_xts, s_emb, s_hpart, s_h0, s_h0out, s_hread, s_z, s_zt, s_xn, s_qk, s_full, s_lo, s_v,
         s_vs, s_var, s_std, s_chain) = (
            sem("em_" + n) for n in (
                "const", "x_in", "xt_ready", "xt_copied", "emb_ready", "h_part", "h_done", "h_stored", "h_read",
                "z_done", "zt_ready", "xn_ready", "qk_ready", "full_ready", "lo_done", "v_ready", "v_done",
                "var_ready", "std_ready", "chain"))
        s_out = [sem(f"em_out_stored{p}") for p in range(2)]
        links = 2 * (2 * NT + 3)

        def all_turns(eng, turn):
            turn(-1, 1, None, 2, False)
            with eng.Fori(0, B // 2 - 1) as i:
                for p in range(2):
                    turn(2 * i + p, p, i, 2, True)
            turn(B - 2, 0, B // 2 - 1, 1, True)
            turn(B - 1, 1, B // 2 - 1, 0, True)

        with nc.Block() as block:
            @block.sync
            def _(sp):
                def load(b):
                    sp.dma_start(x8[:, :, :], io.x[ds(b, 1)].rearrange("o a c f -> (o a c) f").rearrange(
                        "(t p) f -> p t f", p=P)).then_inc(s_x, 16)
                    sp.dma_start(h[:, 8:12, :], io.txt[ds(b, 1)].rearrange("o s d -> (o s) d").rearrange(
                        "(t p) d -> p t d", p=P)).then_inc(s_x, 16)

                def turn(b, p, nth, ahead, here):
                    if ahead:
                        sp.wait_ge(s_h0, b + 2)
                        sp.dma_start(io.H0[ds(b + 1, 1)].rearrange("o p t d -> (o p) (t d)"),
                                     h[:, :, :].rearrange("p t d -> p (t d)")).then_inc(s_h0out, 16)
                        sp.wait_ge(s_h0out, 16 * (b + 2))
                        sp.wait_ge(s_hread, b + 2)
                        if ahead == 2:
                            load(b + 2)
                    if here:
                        sp.wait_ge(s_lo, NC * (b + 2))
                        for t, parts in ((0, (hi[p], hi[p], lo[p])), (1, (hi[p], lo[p], hi[p]))):
                            dst = io.QK[ds(NH * b, NH), t, :, :]
                            for part, w in enumerate(parts):
                                sp.dma_start(dst[:, part * DH:(part + 1) * DH, :], w[:, t, :]).then_inc(s_out[p], 16)
                        sp.wait_ge(s_vs, NC * (b + 1) + 1)
                        sp.dma_start(io.VS[ds(NH * b, NH)].rearrange("h p n -> p h n"),
                                     vals[p][:, :, :, :].rearrange("p h t w -> p h (t w)")).then_inc(s_out[p], 16)

                load(0)
                sp.dma_start(pe_tok[:, :, :], io.pe_tok.rearrange("(t p) d -> p t d", p=P)).then_inc(s_const, 16)
                sp.dma_start(wtok[:, :], io.Wtok).then_inc(s_const, 16)
                sp.dma_start(bvb[:, :], io.bv.partition_broadcast(P)).then_inc(s_const, 16)
                for p in range(2):
                    sp.sem_inc(s_out[p], 16 * 7)
                all_turns(sp, turn)
                for p in range(2):
                    sp.wait_ge(s_out[p], 16 * 7 * (B // 2 + 1))
                sp.dma_start(io.QK[UNITS], io.QK[0]).then_inc(s_h0out, 16)
                sp.dma_start(io.VS[UNITS], io.VS[0]).then_inc(s_h0out, 16)
                sp.wait_ge(s_h0out, 16 * (B + 2))

            @block.tensor
            def _(pe):
                pe.wait_ge(s_const, 48)

                def turn(b, p, nth, ahead, here):
                    if ahead:
                        pe.wait_ge(s_x, 32 * (b + 2))
                        for q in range(2):
                            if q == 1:
                                pe.wait_ge(s_xts, 2 * b + 3)
                            for t in range(TC):
                                ins = pe.transpose(b_xt[0:F_IN, t * P:(t + 1) * P], x8[:, TC * q + t, :], g.ident[:, :])
                            ins.then_inc(s_xt, 1)
                            pe.wait_ge(s_xts, 2 * b + q + 3)
                            if q == 1:
                                pe.wait_ge(s_hpart, 2 * b + 3)
                            for t in range(TC):
                                ins = pe.matmul(b_emb[:, t * P:(t + 1) * P], xt[:, q, t * P:(t + 1) * P], wtok[:, :],
                                                start=True, stop=True)
                            ins.then_inc(s_emb, 1)
                    if here:
                        pe.wait_ge(s_z, b + 1)
                        for k in range(NC):
                            for t in range(TC):
                                ins = pe.transpose(b_z[:, t * P:(t + 1) * P], z2[p][:, TC * k + t, :], g.ident[:, :])
                            ins.then_inc(s_zt, 1)
                            pe.wait_ge(s_xn, NC * b + k + 1)
                            pe.wait_ge(s_full, NC * b + k + 1)
                            pe.matmul(b_q[:, :], g.wt[:, 0, :], xn[:, k * CH:(k + 1) * CH], start=True, stop=True)
                            pe.matmul(b_k[:, :], g.wt[:, 1, :], xn[:, k * CH:(k + 1) * CH],
                                      start=True, stop=True).then_inc(s_qk, 1)
                            if k == 0:
                                pe.wait_ge(s_vs, NC * b + 1)
                            for t in range(TC):
                                ins = pe.matmul(b_v[k][:, t * P:(t + 1) * P], xn[:, k * CH + t * P:k * CH + (t + 1) * P],
                                                g.wt[:, 2, :], start=True, stop=True)
                            ins.then_inc(s_v, 1)

                all_turns(pe, turn)

            @block.scalar
            def _(act):
                act.sem_inc(s_full, 1)

                def turn(b, p, nth, ahead, here):
                    def root(n):
                        act.wait_ge(s_var, 2 * b + n + 3)
                        act.activation(std[:, :], var[:, :], ACT.Sqrt).then_inc(s_std, 1)

                    if ahead and not here:
                        root(0)
                        root(1)
                    if here:
                        for k in range(NC):
                            if ahead and k == NC - 1:
                                root(1)
                            cols = slice(k * CH, (k + 1) * CH)
                            act.wait_ge(s_zt, NC * b + k + 1)
                            act.activation(xn[:, cols], b_z[:, :], ACT.Identity, bias=g.beta[:, 0:1],
                                           scale=g.gamma[:, 0:1]).then_inc(s_xn, 1)
                            if ahead and k == 0:
                                root(0)
                            act.wait_ge(s_qk, NC * b + k + 1)
                            act.wait_ge(s_lo, NC * b + k + 1)
                            if k == 0:
                                act.wait_ge(s_out[p], 16 * 7 * (nth + 1))
                            for dst in (full, hi[p]):
                                act.activation(dst[:, 0, cols], b_q[:, :], ACT.Identity, bias=g.bqs[:, 0:1],
                                               scale=QSCALE)
                                ins = act.activation(dst[:, 1, cols], b_k[:, :], ACT.Identity, bias=g.bk[:, 0:1])
                            ins.then_inc(s_full, 1)

                all_turns(act, turn)

            @block.vector
            def _(dve):
                dve.sem_inc(s_vs, 1)
                dve.sem_inc(s_lo, NC)
                for p in range(2):
                    dve.memset(vals[p][:, :, :, :], 1.0)
                dve.wait_ge(s_const, 48)

                def turn(b, p, nth, ahead, here):
                    ch = Chain(dve, s_chain, links * (b + 1))

                    def parts(k):
                        dve.wait_ge(s_v, NC * b + k + 1)
                        if k == 0:
                            dve.wait_ge(s_out[p], 16 * 7 * (nth + 1))
                        dve.tensor_tensor(
                            vals[p][:, :, TC * k:TC * (k + 1), 0:DH],
                            b_v[k][:, :].rearrange("p (t h d) -> p h t d", t=TC, h=NH),
                            bvb[:, :].rearrange("p (h d) -> p h d", h=NH).unsqueeze(2).to_broadcast([P, NH, TC, DH]),
                            ALU.add).then_inc(s_vs, 1)
                        dve.wait_ge(s_full, NC * b + k + 2)
                        cols = slice(k * CH, (k + 1) * CH)
                        dve.tensor_tensor(lo[p][:, :, cols], full[:, :, cols], hi[p][:, :, cols],
                                          ALU.subtract).then_inc(s_lo, 1)

                    if not ahead:
                        for k in range(NC):
                            parts(k)
                        return
                    dve.wait_ge(s_x, 32 * (b + 2))
                    for q in range(2):
                        dve.wait_ge(s_xt, 2 * b + q + 3)
                        dve.tensor_copy(xt[:, q, :], b_xt[0:F_IN, :]).then_inc(s_xts, 1)
                        dve.wait_ge(s_emb, 2 * b + q + 3)
                        dve.tensor_tensor(h[:, TC * q:TC * (q + 1), :], b_emb[:, :].rearrange("p (t d) -> p t d", t=TC),
                                          pe_tok[:, TC * q:TC * (q + 1), :], ALU.add).then_inc(s_hpart, 1)
                    dve.wait_ge(s_hpart, 2 * b + 4)
                    dve.sem_inc(s_h0, 1)
                    for n, (src, dst) in enumerate(((h, z), (z, z2[1 - p]))):
                        for t in range(NT):
                            ch.add(dve.bn_stats(st[:, t, :], src[:, t, :]))
                        ch.settle_apart()
                        for t in range(NT):
                            ins = dve.bn_aggr(mv[:, t, :], st[:, t, :])
                            if t == NT - 1:
                                ch.add(ins)
                        ch.settle()
                        dve.tensor_scalar(var[:, :], mv[:, :, 1], EPS, None, ALU.add).then_inc(s_var, 1)
                        dve.wait_ge(s_std, 2 * b + n + 3)
                        ch.add(dve.reciprocal(rstd[:, :], std[:, :]))
                        ch.settle()
                        for t in range(NT):
                            ch.add(dve.tensor_scalar(dst[:, t, :], src[:, t, :], mv[:, t, 0:1], rstd[:, t:t + 1],
                                                     ALU.subtract, ALU.mult))
                        ch.settle()
                        dve.sem_inc(s_z if n else s_hread, 1)
                        if here:
                            parts(n)
                    if here:
                        parts(NC - 1)
                    assert ch.n == links

                all_turns(dve, turn)


def unit_order():
    after = {"R": (4, 6, 8), "RC": (6, 8, 10), "X": (10, 12, 14, 16), "XC": (11, 13, 15, 17), "EV": (14, 26),
             "PV": (5, 9, 13, 17, 21, 25, 29), "NM": (32,), "GUARD": (34,)}
    steps, m = [], 0

    def maxima(count):
        nonlocal m
        for _ in range(min(count, NT * NC - m)):
            steps.append(("PRE", m))
            m += 1

    for n in range(NT * NC):
        steps.append(("S", n))
        if n >= 16:
            maxima(1 if n == 16 else 2)
        for kind, places in after.items():
            if n in places:
                steps.append((kind, places.index(n)))
                if kind == "PV" and n >= 16:
                    maxima(1)
    assert m == NT * NC
    return steps + [("PV", NT * NC // TC - 2), ("PV", NT * NC // TC - 1), ("EV", NC - 1)]


PREPARE = ([(kind, k) for kind in ("R", "RC") for k in range(NC)]
           + [(kind, j) for j in range(4) for kind in ("X", "XC")] + [("PRE", m) for m in range(NT * NC)]
           + [("NM", 0), ("GUARD", 0)])
STEPS = NT * NC
GROUPS = STEPS // TC
SHARED = 3 + 4 + 1
SHARED_B = SHARED * NH + NC
LINKS_PREP = 2 * 4


def attend_block(nc, ctx, io, g):
    with ExitStack() as c:
        def sb(name, shape, dt=F32):
            return c.enter_context(nc.sbuf_tensor(name, shape, dt))

        def bank(name):
            return c.enter_context(nc.psum_tensor(name, [P, CH], F32))

        def sem(name):
            return ctx.enter_context(nc.semaphore("at_" + name))

        def pair(name, shape, dt=F32):
            return [sb(f"{name}{p}", shape, dt) for p in range(2)]

        tabs = sb("tabs", [P, 4, S], F16)
        rot = sb("rot", [P, 2, S])
        mask1 = sb("mask1", [P, 3, DW])
        mask2 = sb("mask2", [P, 3, DW], I32)
        pick = sb("pick", [P, 2, 2, VW])
        k3, q3 = pair("k3", [P, S], F16), pair("q3", [P, S], F16)
        vo, wp3 = pair("vo", [P, NT * VW]), pair("wp3", [PART, 2 * D], F16)
        ah, al = pair("ah", [P, S + 4], F16), pair("al", [P, S + 4], F16)
        dgh, dgl = pair("dgh", [P, NT, DW], F16), pair("dgl", [P, NT, DW], F16)
        ta, tb, af = sb("ta", [P, NC, CH]), sb("tb", [P, NC, CH]), sb("af", [P, NC, CH])
        dt = sb("dt", [P, 4, 3 * DW])
        pt = sb("pt", [P, 8, CH])
        part_max, nm, nmh = sb("part_max", [P, STEPS]), sb("nm", [P, NT]), sb("nmh", [NT, P], F16)
        osb = sb("osb", [P, NH, S])
        sums, cx = sb("sums", [P, S]), sb("cx", [P, S])
        score = [bank(f"score{i}") for i in range(3)]
        pre = [bank(f"pre{i}") for i in range(2)]
        shared = [bank(f"shared{i}") for i in range(2)]
        o_bank = bank("o_bank")
        s_const, s_clear = sem("const"), sem("cleared")
        s_load = [sem("loaded0"), sem("loaded1")]
        s_score, s_exp, s_pv, s_evac = sem("score"), sem("exp"), sem("pv"), sem("evac")
        s_pre, s_max, s_shared, s_sread = sem("pre"), sem("max"), sem("shared"), sem("shared_read")
        s_a, s_dg = sem("a_ready"), sem("diag_ready")
        s_nm, s_guard = sem("nm"), sem("guard")
        s_cxout, s_cxfree, s_apart = sem("cx_stored"), sem("cx_free"), sem("apart")
        s_sums, s_copied, s_cx, s_vchain, s_af, s_ah, s_dt, s_hi = (sem(n) for n in ("sums", "context_copied", "context", "vector_chain", "turned", "turned_hi", "diag", "diag_hi"))
        order = unit_order()

        def scores(pe, n, p, u):
            k, t = n // NT, n % NT
            lo, hi = k * CH, (k + 1) * CH
            out = score[n % 3]
            pe.wait_ge(s_exp, u * STEPS + n + 1)
            keys = slice(t * P, (t + 1) * P)
            first = True
            a, b = max(lo, min(hi, t * P - 1)), max(lo, min(hi, t * P + P - 1))
            if lo < a:
                for tab, w in ((2, ah), (2, al), (3, ah)):
                    pe.matmul(out[:, 0:a - lo], tabs[:, tab, keys], w[p][:, lo + 2:a + 2], start=first, stop=False)
                    first = False
            if a < b:
                x = a - (t * P - 1)
                for w in (dgh, dgl):
                    pe.matmul(out[:, a - lo:b - lo], g.ident16[:, :], w[p][:, t, x:x + b - a], start=first,
                              stop=False)
                    first = False
            if b < hi:
                for tab, w in ((0, ah), (0, al), (1, ah)):
                    pe.matmul(out[:, b - lo:CH], tabs[:, tab, keys], w[p][:, b + 1:hi + 1], start=first, stop=False)
                    first = False
            if n == 0:
                pe.wait_ge(s_guard, 16 * (u + 1))
            pe.matmul(out[:, :], k3[p][0:PART + 1, keys], q3[p][0:PART + 1, lo:hi], start=False,
                      stop=True).then_inc(s_score, 1)

        def values(pe, q, p, u):
            pe.wait_ge(s_exp, u * STEPS + TC * (q + 1) + 3)
            if q % 3 == 0:
                pe.wait_ge(s_evac, u * NC + q // 3 + 1)
            for i in range(TC):
                t = (TC * q + i) % NT
                ins = pe.matmul(o_bank[VW * i:VW * (i + 1), :], vo[p][:, VW * t:VW * (t + 1)],
                                pt[:, ((GROUPS * p + q) % 2) * TC + i, :], start=(q % 3 == 0), stop=(q % 3 == 2),
                                tile_position=(0, VW * i))
            ins.then_inc(s_pv, 1)

        def turned(pe, k, p, use):
            pe.wait_ge(s_sread, use + 1)
            cols = slice(k * CH, (k + 1) * CH)
            pe.matmul(shared[0][:, :], wp3[p][:, 0:D], q3[p][0:PART, cols], start=True, stop=True)
            pe.matmul(shared[1][:, :], wp3[p][:, D:2 * D], q3[p][0:PART, cols], start=True,
                      stop=True).then_inc(s_shared, 1)

        def diagonal(pe, j, p, use):
            pe.wait_ge(s_sread, use + 1)
            for side in range(2):
                for i in range(3):
                    t = 3 * j + i
                    keys = slice(t * P, (t + 1) * P)
                    for n, (tab, w) in enumerate(((2 * side, ah), (2 * side, al), (2 * side + 1, ah))):
                        ins = pe.matmul(shared[side][:, i * DW:(i + 1) * DW], tabs[:, tab, keys],
                                        w[p][:, t * P + side:t * P + side + DW], start=(n == 0), stop=(n == 2))
            ins.then_inc(s_shared, 1)

        def premax(pe, m, p, v):
            t, k = m // NC, m % NC
            lo, hi = k * CH, (k + 1) * CH
            out = pre[m % 2]
            rows = slice(t * P, (t + 1) * P)
            pe.wait_ge(s_max, v * STEPS + m + 1)
            pieces = []
            a, b = max(lo, min(hi, t * P)), max(lo, min(hi, t * P + P))
            if lo < a:
                pieces.append((lo, a, ah[p][:, t * P + 1:t * P + P + 1], tabs[:, 0, lo:a], P))
            if a < b:
                pieces.append((a, b, dgh[p][:, t, 1:DW], g.ident16[:, :], P))
            if b < hi:
                if b == t * P + P:
                    pieces.append((b, b + 1, ah[p][:, t * P + 2:t * P + P + 1], tabs[:, 2, b:b + 1], P - 1))
                    b += 1
                pieces.append((b, hi, ah[p][:, t * P + 2:t * P + P + 2], tabs[:, 2, b:hi], P))
            pe.matmul(out[:, :], q3[p][0:PART, rows], k3[p][0:PART, lo:hi], start=True, stop=False)
            for i, (x, y, w, r, rows_out) in enumerate(pieces):
                ins = pe.matmul(out[0:rows_out, x - lo:y - lo], w, r, start=False, stop=(i == len(pieces) - 1))
            ins.then_inc(s_pre, 1)

        def turns(eng, body, batch_end):
            with eng.Fori(0, B) as b:
                with eng.Fori(0, NH // 2) as hp:
                    for p in range(2):
                        u = b * NH + hp * 2 + p
                        body(p=p, u=u, q=1 - p, v=u + 1, loads=b * (NH // 2) + hp + 1 + p,
                             use=b * SHARED_B + hp * (2 * SHARED) + SHARED * (p + 1), head=hp * 2 + p,
                             links=b * (NH * LINKS_PREP) + hp * (2 * LINKS_PREP) + LINKS_PREP * (p + 1))
                batch_end(b)

        with nc.Block() as block:
            @block.sync
            def _(sp):
                for dst, src in ((tabs[:, :, :], io.tabs.rearrange("a p s -> p a s")),
                                 (rot[:, :, :], io.rot.rearrange("a p s -> p a s")),
                                 (mask1[:, :, :], io.mask1), (mask2[:, :, :], io.mask2), (pick[:, :, :, :], io.pick)):
                    sp.dma_start(dst, src).then_inc(s_const, 16)
                sp.wait_ge(s_clear, 8)

                def load(q, v, head):
                    sp.dma_start(k3[q][0:PART, :], io.QK[ds(v, 1), 1].rearrange("o r s -> (o r) s")).then_inc(s_load[q], 16)
                    sp.dma_start(q3[q][0:PART, :], io.QK[ds(v, 1), 0].rearrange("o r s -> (o r) s")).then_inc(s_load[q], 16)
                    sp.dma_start(wp3[q][:, :], io.WP3[ds(head, 1)].rearrange("o r s -> (o r) s")).then_inc(s_load[q], 16)
                    sp.dma_start(vo[q][:, :], io.VS[ds(v, 1)].rearrange("o r s -> (o r) s")).then_inc(s_load[q], 16)

                def guard(q, use):
                    sp.wait_ge(s_sread, use + SHARED + 1)
                    sp.dma_start(q3[q][PART:PART + 1, :], nmh[:, :]).then_inc(s_guard, 16)

                load(0, 0, 0)
                guard(0, 0)

                def body(p, u, q, v, loads, use, head, links):
                    sp.wait_ge(s_pv, u * GROUPS + 2)
                    load(q, v, head + 1)
                    guard(q, use)

                turns(sp, body, lambda b: None)
                sp.wait_ge(s_guard, 16 * (UNITS + 1))

            @block.tensor
            def _(pe):
                pe.sem_inc(s_pv, 2)
                pe.wait_ge(s_const, 16 * 5)

                def step(kind, n, p, u, q, v, loads, use):
                    if kind == "S":
                        scores(pe, n, p, u)
                    elif kind == "PV":
                        values(pe, n, p, u)
                    elif kind == "R":
                        if n == 0:
                            pe.wait_ge(s_load[q], loads * 64)
                        turned(pe, n, q, use + n)
                    elif kind == "X":
                        if n < NC:
                            pe.wait_ge(s_a, v * NC + n + 1)
                        diagonal(pe, n, q, use + 3 + n)
                    elif kind == "PRE":
                        if n % 9 == 0:
                            pe.wait_ge(s_dg, v * 4 + n // 9 + 1)
                        premax(pe, n, q, v)
                    elif kind == "GUARD":
                        pe.wait_ge(s_nm, v + 1)
                        pe.wait_ge(s_sread, use + 8)
                        pe.transpose(shared[0][0:NT, 0:P], nm[:, :], g.ident[:, :]).then_inc(s_shared, 1)

                for kind, n in PREPARE:
                    step(kind, n, None, None, 0, 0, 1, 0)

                def body(p, u, q, v, loads, use, head, links):
                    for kind, n in order:
                        step(kind, n, p, u, q, v, loads, use)

                def batch_end(b):
                    pe.wait_ge(s_evac, (b + 1) * (NH * NC) + 1)
                    pe.wait_ge(s_sread, b * SHARED_B + SHARED * (NH + 1) + 1)
                    for k in range(NC):
                        for what in (1, 0):
                            if k:
                                pe.wait_ge(s_copied, b * (2 * NC) + 2 * k - what)
                            for par in range(2):
                                for hh in range(NH // 2):
                                    ins = pe.matmul(shared[what][VW * hh:VW * (hh + 1), :], pick[:, what, par, :],
                                                    osb[:, 2 * hh + par, k * CH:(k + 1) * CH], start=(par == 0),
                                                    stop=(par == 1), tile_position=(0, VW * hh))
                            ins.then_inc(s_sums if what else s_shared, 1)

                turns(pe, body, batch_end)

            @block.scalar
            def _(act):
                act.sem_inc(s_exp, 3)
                act.sem_inc(s_cxfree, 1)
                act.wait_ge(s_clear, 8)

                def leading(kind, n, q, v):
                    if kind == "RC":
                        act.wait_ge(s_af, v * NC + n + 1)
                        act.activation(ah[q][:, n * CH + 1:(n + 1) * CH + 1], af[:, n, :], ACT.Identity).then_inc(s_ah, 1)
                    elif kind == "XC":
                        act.wait_ge(s_dt, v * 4 + n + 1)
                        act.activation(dgh[q][:, 3 * n:3 * n + 3, :], dt[:, n, :].rearrange("p (t x) -> p t x", t=3),
                                       ACT.Identity).then_inc(s_hi, 1)

                for kind, n in PREPARE:
                    leading(kind, n, 0, 0)

                def body(p, u, q, v, loads, use, head, links):
                    for kind, n in order:
                        leading(kind, n, q, v)
                        if kind == "S":
                            act.wait_ge(s_score, u * STEPS + n + 1)
                            if n % TC == 0:
                                act.wait_ge(s_pv, u * GROUPS + n // TC + 1)
                            act.activation(pt[:, (4 * ((GROUPS * p + n // TC) % 2)) + n % TC, :], score[n % 3][:, :],
                                           ACT.Exp).then_inc(s_exp, 1)

                def batch_end(b):
                    act.wait_ge(s_cxfree, b + 1)
                    for k in range(NC):
                        cols = slice(k * CH, (k + 1) * CH)
                        act.wait_ge(s_sums, b * NC + k + 1)
                        act.activation(sums[:, cols], shared[1][:, :], ACT.Identity).then_inc(s_copied, 1)
                        act.wait_ge(s_shared, b * SHARED_B + SHARED * (NH + 1) + k + 1)
                        act.activation(cx[:, cols], shared[0][:, :], ACT.Identity).then_inc(s_copied, 1)
                    act.wait_ge(s_copied, (b + 1) * (2 * NC))
                    act.sem_inc(s_sread, NC)

                turns(act, body, batch_end)

            @block.vector
            def _(dve):
                for q in range(2):
                    dve.memset(k3[q][:, :], 1.0).then_inc(s_clear, 1)
                    dve.memset(q3[q][:, :], 1.0).then_inc(s_clear, 1)
                    dve.memset(ah[q][:, :], 0.0).then_inc(s_clear, 1)
                    dve.memset(al[q][:, :], 0.0).then_inc(s_clear, 1)
                dve.sem_inc(s_sread, 1)
                dve.sem_inc(s_max, 2)
                dve.sem_inc(s_evac, 1)
                dve.wait_ge(s_const, 16 * 5)

                def step(ch, kind, n, p, u, q, v, use, head):
                    if kind == "R":
                        cols = slice(n * CH, (n + 1) * CH)
                        dve.wait_ge(s_shared, use + n + 1)
                        dve.scalar_tensor_tensor(ta[:, n, :], shared[0][:, :], g.rb[:, 0, head], rot[:, 0, cols],
                                                 ALU.add, ALU.mult)
                        dve.scalar_tensor_tensor(tb[:, n, :], shared[1][:, :], g.rb[:, 1, head], rot[:, 1, cols],
                                                 ALU.add, ALU.mult).then_inc(s_sread, 1)
                    elif kind == "X":
                        dve.wait_ge(s_shared, use + 3 + n + 1)
                        w = dt[:, n, :].rearrange("p (t x) -> p t x", t=3)
                        ch.add(dve.tensor_tensor(w, shared[0][:, 0:3 * DW].rearrange("p (t x) -> p t x", t=3),
                                                 mask1[:, :, :], ALU.mult))
                        ch.settle_apart()
                        dve.copy_predicated(w, mask2[:, :, :], shared[1][:, 0:3 * DW].rearrange(
                            "p (t x) -> p t x", t=3)).then_inc(s_sread, 1)
                        dve.wait_ge(s_sread, use + 3 + n + 2)
                        dve.sem_inc(s_dt, 1)
                    elif kind == "PRE":
                        dve.wait_ge(s_pre, v * STEPS + n + 1)
                        dve.tensor_reduce(part_max[:, n:n + 1], pre[n % 2][:, :], AX.X, ALU.max).then_inc(s_max, 1)
                    elif kind == "NM":
                        dve.wait_ge(s_max, v * STEPS + STEPS + 2)
                        dve.tensor_reduce(nm[:, :], part_max[:, :].rearrange("p (t k) -> p t k", k=NC), AX.X,
                                          ALU.max, negate=True).then_inc(s_nm, 1)
                    elif kind == "GUARD":
                        dve.wait_ge(s_shared, use + 8)
                        dve.tensor_copy(nmh[:, :], shared[0][0:NT, 0:P]).then_inc(s_sread, 1)
                    elif kind == "EV":
                        k = n
                        dve.wait_ge(s_pv, u * GROUPS + 3 * k + 3 + 2)
                        dve.tensor_copy(osb[:, ds(head[1], 1), k * CH:(k + 1) * CH].rearrange("p o s -> p (o s)"),
                                        o_bank[:, :]).then_inc(s_evac, 1)

                ch = Chain(dve, s_vchain)
                for kind, n in PREPARE:
                    step(ch, kind, n, None, None, 0, 0, 0, slice(0, 1))
                assert ch.n == LINKS_PREP

                def body(p, u, q, v, loads, use, head, links):
                    ch = Chain(dve, s_vchain, links)
                    for kind, n in order:
                        h = (None, head) if kind == "EV" else ds(head + 1, 1)
                        step(ch, kind, n, p, u, q, v, use, h)

                def batch_end(b):
                    for k in range(NC):
                        cols = slice(k * CH, (k + 1) * CH)
                        dve.wait_ge(s_copied, b * (2 * NC) + 2 * k + 2)
                        dve.reciprocal(sums[:, cols], sums[:, cols]).then_inc(s_cx, 1)
                        dve.wait_ge(s_cx, b * (2 * NC) + 2 * k + 1)
                        dve.tensor_tensor(cx[:, cols], cx[:, cols], sums[:, cols], ALU.mult).then_inc(s_cx, 1)

                turns(dve, body, batch_end)

            @block.gpsimd
            def _(pool):
                def step(kind, n, q, v, use):
                    if kind == "R":
                        pool.wait_ge(s_sread, use + n + 2)
                        pool.tensor_tensor(af[:, n, :], ta[:, n, :], tb[:, n, :], ALU.add).then_inc(s_af, 1)
                    elif kind == "RC":
                        cols = slice(n * CH + 1, (n + 1) * CH + 1)
                        pool.wait_ge(s_ah, v * NC + n + 1)
                        pool.tensor_tensor(al[q][:, cols], af[:, n, :], ah[q][:, cols], ALU.subtract).then_inc(s_a, 1)
                    elif kind == "XC":
                        pool.wait_ge(s_hi, v * 4 + n + 1)
                        pool.tensor_tensor(dgl[q][:, 3 * n:3 * n + 3, :], dt[:, n, :].rearrange("p (t x) -> p t x", t=3),
                                           dgh[q][:, 3 * n:3 * n + 3, :], ALU.subtract).then_inc(s_dg, 1)

                pool.wait_ge(s_clear, 8)
                for kind, n in PREPARE:
                    step(kind, n, 0, 0, 0)

                def body(p, u, q, v, loads, use, head, links):
                    for kind, n in order:
                        step(kind, n, q, v, use)

                def batch_end(b):
                    pool.wait_ge(s_cx, (b + 1) * (2 * NC))
                    pool.sem_inc(s_apart, 1)
                    pool.dma_start(io.CT[ds(b, 1)].rearrange("o p s -> (o p) s"), cx[:, :]).then_inc(s_cxout, 16)
                    pool.wait_ge(s_cxout, 16 * (b + 1))
                    pool.sem_inc(s_cxfree, 1)

                turns(pool, body, batch_end)
                pool.wait_ge(s_apart, B)



def project_block(nc, ctx, io, g):
    with ExitStack() as c:
        def sb(name, shape, dt=F32):
            return c.enter_context(nc.sbuf_tensor(name, shape, dt))

        def bank(name):
            return c.enter_context(nc.psum_tensor(name, [P, CH], F32))

        def sem(name):
            return ctx.enter_context(nc.semaphore("pr_" + name))

        ct = [sb(f"ct{k}", [P, CH]) for k in range(NC)]
        h0 = [sb(f"h0_{k}", [P, TC, D]) for k in range(NC)]
        h1 = [sb(f"h1_{k}", [P, TC, D]) for k in range(NC)]
        xn = [sb(f"xn_{k}", [P, TC, D]) for k in range(NC)]
        xnt = [sb(f"xnt{k}", [P, CH]) for k in range(NC)]
        bob, brb, wr = sb("bob", [P, D]), sb("brb", [P, NE]), sb("wr", [P, NE])
        st, mv = ([sb(f"{n}{k}", sh) for k in range(NC)] for n, sh in (("st2_", [P, TC, 6]), ("mv2_", [P, TC, 2])))
        var, std, rstd = ([sb(f"{n}2_{k}", [P, TC]) for k in range(NC)] for n in ("var", "std", "rstd"))
        b_o, b_t = ([bank(f"{n}{i}") for i in range(3)] for n in ("b_o", "b_t"))
        b_l = bank("b_l")
        s_const, s_o, s_hb, s_h1, s_var, s_std, s_xn, s_xt, s_xts, s_lg, s_lgr, s_chain = (
            sem(n) for n in ("const", "o_ready", "h_bias", "h1_done", "var", "std", "xn_done", "xt_ready",
                             "xt_copied", "logit_ready", "logit_read", "chain"))
        s_in, s_out = ([sem(f"{n}{k}") for k in range(NC)] for n in ("in", "stored"))
        links = 4

        def all_turns(eng, turn):
            def fixed(r):
                turn(r, r % NC, r // NC, lambda n: 0 <= r + n < NR)
            for r in range(-2, NC):
                fixed(r)
            with eng.Fori(0, B - 3) as i:
                for k in range(NC):
                    turn(NC * i + NC + k, k, i + 1, lambda n: True)
            for r in range(NR - 2 * NC, NR + 1):
                fixed(r)

        with nc.Block() as block:
            @block.sync
            def _(sp):
                sp.dma_start(bob[:, :], io.bo.partition_broadcast(P)).then_inc(s_const, 16)
                sp.dma_start(brb[:, :], io.br.partition_broadcast(P)).then_inc(s_const, 16)
                sp.dma_start(wr[:, :], io.Wr).then_inc(s_const, 16)
                contexts = io.CT.rearrange("b p (k s) -> b k p s", k=NC)
                tokens = io.H0.rearrange("b p (k t) d -> b k p t d", k=NC)

                def load(b, k):
                    sp.dma_start(ct[k][:, :], contexts[ds(b, 1), k].rearrange("o p s -> (o p) s")).then_inc(s_in[k], 16)
                    sp.dma_start(h0[k][:, :, :], tokens[ds(b, 1), k].rearrange(
                        "o p t d -> (o p) t d")).then_inc(s_in[k], 16)

                def turn(r, k, nth, has):
                    if has(NC + 1) and has(1):
                        sp.wait_ge(s_h1, r + 2)
                        load(nth + 1 + (k == NC - 1), (k + 1) % NC)
                    if has(0):
                        sp.wait_ge(s_xn, r + 1)
                        sp.dma_start(io.H1[ds(r, 1)].rearrange("o p n -> (o p) n"),
                                     h1[k][:, :, :].rearrange("p t d -> p (t d)")).then_inc(s_out[k], 16)
                        sp.dma_start(io.XN[ds(r, 1)].rearrange("o p n -> (o p) n"),
                                     xn[k][:, :, :].rearrange("p t d -> p (t d)")).then_inc(s_out[k], 16)

                for k in range(NC):
                    sp.sem_inc(s_out[k], 32)
                    load(0, k)
                all_turns(sp, turn)
                for k in range(NC):
                    sp.wait_ge(s_out[k], 32 * (B + 1))

            @block.gpsimd
            def _(pool):
                pool.wait_ge(s_const, 48)
                with pool.Fori(0, B) as b:
                    for k in range(NC):
                        pool.wait_ge(s_in[k], 32 * (b + 1))
                        pool.tensor_tensor(h0[k][:, :, :], h0[k][:, :, :],
                                           bob[:, :].unsqueeze(1).to_broadcast([P, TC, D]), ALU.add).then_inc(s_hb, 1)

            @block.tensor
            def _(pe):
                pe.wait_ge(s_const, 48)

                def turn(r, k, nth, has):
                    before, ahead = (k - 1) % NC, (k + 2) % NC
                    if has(2):
                        pe.wait_ge(s_in[ahead], 32 * (nth + 1 + (k > 0)))
                        if has(-1):
                            pe.wait_ge(s_h1, r)
                        for t in range(TC):
                            ins = pe.matmul(b_o[ahead][:, t * P:(t + 1) * P], ct[ahead][:, t * P:(t + 1) * P],
                                            g.wt[:, 3, :], start=True, stop=True)
                        ins.then_inc(s_o, 1)
                    if has(-1):
                        pe.wait_ge(s_xts, r)
                        pe.wait_ge(s_lgr, r)
                        for t in range(TC):
                            ins = pe.matmul(b_l[:, t * NE:(t + 1) * NE], xnt[before][:, t * P:(t + 1) * P], wr[:, :],
                                            start=True, stop=True)
                        ins.then_inc(s_lg, 1)
                    if has(0):
                        pe.wait_ge(s_xn, r + 1)
                        if has(-NC):
                            pe.wait_ge(s_xts, r - NC + 1)
                        for t in range(TC):
                            ins = pe.transpose(b_t[k][:, t * P:(t + 1) * P], xn[k][:, t, :], g.ident[:, :])
                        ins.then_inc(s_xt, 1)

                all_turns(pe, turn)

            @block.scalar
            def _(act):
                def turn(r, k, nth, has):
                    before, after = (k - 1) % NC, (k + 1) % NC
                    if has(1):
                        act.wait_ge(s_var, r + 2)
                        act.activation(std[after][:, :], var[after][:, :], ACT.Sqrt).then_inc(s_std, 1)
                    if has(0):
                        act.wait_ge(s_xt, r + 1)
                        if has(-NC):
                            act.wait_ge(s_lg, r - NC + 1)
                        act.activation(xnt[k][:, :], b_t[k][:, :], ACT.Identity).then_inc(s_xts, 1)

                all_turns(act, turn)

            @block.vector
            def _(dve):
                dve.sem_inc(s_lgr, 1)
                dve.wait_ge(s_const, 48)

                def turn(r, k, nth, has):
                    before, after = (k - 1) % NC, (k + 1) % NC
                    ch = Chain(dve, s_chain, (r + 2) * links)

                    def step(ins):
                        ch.add(ins)
                        ch.settle()
                    if has(1):
                        j = after
                        dve.wait_ge(s_hb, r + 2)
                        dve.wait_ge(s_o, r + 2)
                        dve.wait_ge(s_out[j], 32 * (nth + 1 + (k == NC - 1)))
                        dve.tensor_tensor(h1[j][:, :, :], b_o[j][:, :].rearrange("p (t d) -> p t d", t=TC),
                                          h0[j][:, :, :], ALU.add).then_inc(s_h1, 1)
                        dve.wait_ge(s_h1, r + 2)
                        for t in range(TC):
                            ins = dve.bn_stats(st[j][:, t, :], h1[j][:, t, :])
                        ch.add(ins)
                        ch.settle_apart()
                        for t in range(TC):
                            ins = dve.bn_aggr(mv[j][:, t, :], st[j][:, t, :])
                        step(ins)
                        dve.tensor_scalar(var[j][:, :], mv[j][:, :, 1], EPS, None, ALU.add).then_inc(s_var, 1)
                    else:
                        dve.sem_inc(s_chain, 3)
                        ch.n = 3
                    if has(0):
                        dve.wait_ge(s_std, r + 1)
                        step(dve.reciprocal(rstd[k][:, :], std[k][:, :]))
                        for t in range(TC):
                            ins = dve.tensor_scalar(xn[k][:, t, :], h1[k][:, t, :], mv[k][:, t, 0:1],
                                                    rstd[k][:, t:t + 1], ALU.subtract, ALU.mult)
                        ins.then_inc(s_xn, 1)
                    else:
                        dve.sem_inc(s_chain, 1)
                        ch.n += 1
                    if has(-1):
                        dve.wait_ge(s_lg, r)
                        dve.tensor_tensor(g.lg[:, ds((r - 1) * TC, TC), :],
                                          b_l[:, 0:TC * NE].rearrange("p (t e) -> p t e", t=TC),
                                          brb[:, :].unsqueeze(1).to_broadcast([P, TC, NE]),
                                          ALU.add).then_inc(s_lgr, 1)
                    assert ch.n == links

                all_turns(dve, turn)


def route_block(nc, ctx, io, g):
    g.wh, g.wl = (ctx.enter_context(nc.sbuf_tensor(n, [P, 2, NE, HID], F16)) for n in ("w12_hi", "w12_lo"))
    g.w3 = ctx.enter_context(nc.sbuf_tensor("w3", [P, NE, TC, D], F32))
    g.s_w = ctx.enter_context(nc.semaphore("expert_weights"))
    with ExitStack() as c:
        def sb(name, shape, dt=F32):
            return c.enter_context(nc.sbuf_tensor(name, shape, dt))

        def sem(name):
            return ctx.enter_context(nc.semaphore("ro_" + name))

        w12 = sb("w12", [P, 2, NE, HID])
        s_w12, s_whi = sem("w12_in"), sem("w12_hi_done")
        rank, index, before = sb("rank", [P, NE]), sb("index", [P, SLOTS]), sb("before", [P, NE, NE])
        tri, ones, last = sb("tri", [P, P]), sb("ones", [P, P]), sb("last", [P, 1])
        l2, key, oh0, oh1 = (sb(n, [P, NG, NE]) for n in ("l2", "key", "oh0", "oh1"))
        sa, sbb = sb("scan_a", [P, NG, NE]), sb("scan_b", [P, NG, NE])
        v0, v1, r0, r1, gap, ex, den, s0, s1, e0, e1, imax, tmp, posf = (
            sb(n, [P, NG]) for n in ("v0", "v1", "r0", "r1", "gap", "ex", "den", "s0", "s1", "e0", "e1", "imax",
                                     "tmpg", "posf"))
        cnt = sb("cnt", [P, 2, NE])
        full = sb("fullm", [P, 2, NE])
        drop, kept = sb("drop", [P, 2]), sb("kept", [P, 2])
        dsel = sb("dsel", [P, 2, NE])
        tot, nt, start, end, base = (sb(n, [P, NE]) for n in ("tot", "ntile", "start", "end", "base"))
        cmp_t, cmp_s, bsel = sb("cmp_t", [P, NE, NG]), sb("cmp_s", [P, SLOTS, NE]), sb("bsel", [P, NE, NE])
        tef = sb("tef", [P, SLOTS])
        cxl = sb("cxl", [P, 2])
        h1l, xnl = sb("h1l", [P, D]), sb("xnl", [P, D])
        rows, idx = [sb(f"rows{i}", [P, TC, D]) for i in range(RING)], [sb(f"idx{i}", [P, TC], I32) for i in range(RING)]
        bc, bp = (c.enter_context(nc.psum_tensor(n, [P, CH], F32)) for n in ("bc", "bp"))
        s_in, s_v, s_cnt, s_gap, s_ex, s_tp, s_pre, s_fix, s_fixed, s_pos = (
            sem(n) for n in ("in", "chain", "counts", "gap", "exp", "per_part", "prefix", "fix", "fixed", "pos"))
        s_idx, s_apart = sem("idx"), sem("apart")
        s_row, s_sc = ([sem(f"{n}{i}") for i in range(RING)] for n in ("row", "scattered"))
        TAIL = NR - 1
        with nc.Block() as block:
            @block.sync
            def _(sp):
                for dst, src in ((rank[:, :], io.rank), (index[:, :], io.index), (before[:, :, :], io.before),
                                 (tri[:, :], io.tri), (ones[:, :], io.ones), (last[:, :], io.last),
                                 (h1l[:, :], io.H1[TAIL, :, (TC - 1) * D:TC * D]),
                                 (xnl[:, :], io.XN[TAIL, :, (TC - 1) * D:TC * D])):
                    sp.dma_start(dst, src).then_inc(s_in, 16)

                def load(r, p):
                    sp.dma_start(rows[p][:, :, :].rearrange("p t d -> p (t d)"),
                                 io.XN[ds(r, 1)].rearrange("o p n -> (o p) n")).then_inc(s_row[p], 16)

                for p in range(RING):
                    load(p, p)
                sp.dma_start(w12[:, 0, :, :], io.W1.rearrange("e k h -> k e h")).then_inc(s_w12, 16)
                sp.dma_start(w12[:, 1, :, :], io.W2.rearrange("e k h -> k e h")).then_inc(s_w12, 16)
                sp.dma_start(g.w3[:, :, :, :], io.W3.rearrange("e (c k) d -> k e c d", k=P)).then_inc(g.s_w, 16)
                sp.wait_ge(s_fix, 1)
                sp.dma_start(io.H1[TAIL, :, (TC - 1) * D:TC * D], h1l[:, :]).then_inc(s_fixed, 16)
                with sp.Fori(0, NR // RING - 1) as i:
                    for p in range(RING):
                        sp.wait_ge(s_sc[p], 16 * TC * (i + 1))
                        load(RING * (i + 1) + p, p)
                sp.wait_ge(s_fixed, 16)

            @block.scalar
            def _(act):
                act.wait_ge(s_gap, 1)
                act.activation(ex[:, :], gap[:, :], ACT.Exp).then_inc(s_ex, 1)
                act.wait_ge(s_w12, 32)
                act.activation(g.wh[:, :, :, :], w12[:, :, :, :], ACT.Identity, scale=WSCALE).then_inc(s_whi, 1)

            @block.tensor
            def _(pe):
                pe.wait_ge(s_in, 16 * 8)
                pe.wait_ge(s_cnt, 1)
                pe.matmul(bc[:, 0:2 * NE], ones[:, :], cnt[:, :, :].rearrange("p a e -> p (a e)"), start=True,
                          stop=True).then_inc(s_pre, 1)
                pe.wait_ge(s_tp, 1)
                pe.matmul(bp[:, 0:NE], tri[:, :], sa[:, NG - 1, :], start=True, stop=True)
                pe.matmul(bp[:, NE:2 * NE], ones[:, :], sa[:, NG - 1, :], start=True, stop=True).then_inc(s_pre, 1)

            @block.vector
            def _(dve):
                ch = Chain(dve, s_v)

                def do(ins):
                    ch.add(ins)
                    ch.settle()

                def over_e(x):
                    return x.unsqueeze(2).to_broadcast([P, NG, NE])

                def over_g(x):
                    return x.unsqueeze(1).to_broadcast([P, NG, NE])

                dve.wait_ge(s_in, 16 * 8)
                for lg, v, r, oh in ((g.lg, v0, r0, oh0), (l2, v1, r1, oh1)):
                    if lg is l2:
                        do(dve.scalar_tensor_tensor(l2[:, :, :], oh0[:, :, :], -3e38, g.lg[:, :, :], ALU.mult, ALU.add))
                    do(dve.tensor_reduce(v[:, :], lg[:, :, :], AX.X, ALU.max))
                    do(dve.tensor_tensor(key[:, :, :], lg[:, :, :], over_e(v[:, :]), ALU.is_equal))
                    do(dve.tensor_tensor(oh[:, :, :], key[:, :, :], over_g(rank[:, :]), ALU.mult))
                    do(dve.tensor_reduce(r[:, :], oh[:, :, :], AX.X, ALU.max))
                    do(dve.tensor_tensor(oh[:, :, :], oh[:, :, :], over_e(r[:, :]), ALU.is_equal))
                dve.tensor_tensor(gap[:, :], v1[:, :], v0[:, :], ALU.subtract).then_inc(s_gap, 1)
                ch.add(dve.tensor_reduce(cnt[:, 0, :], oh0[:, :, :].rearrange("p g e -> p e g"), AX.X, ALU.add))
                ch.add(dve.tensor_tensor(key[:, :, :], oh0[:, :, :], oh1[:, :, :], ALU.add))
                ch.settle()
                dve.tensor_reduce(cnt[:, 1, :], key[:, :, :].rearrange("p g e -> p e g"), AX.X, ALU.add).then_inc(s_cnt, 1)
                dve.wait_ge(s_pre, 1)
                do(dve.tensor_scalar(full[:, :, :], bc[:, 0:2 * NE].rearrange("p (a e) -> p a e", a=2),
                                     float(TOKENS), last[:, 0:1], ALU.is_ge, ALU.mult))
                ch.add(dve.tensor_tensor(dsel[:, 0, :], full[:, 0, :], oh0[:, NG - 1, :], ALU.mult))
                ch.add(dve.tensor_tensor(dsel[:, 1, :], full[:, 1, :], oh1[:, NG - 1, :], ALU.mult))
                ch.settle()
                do(dve.tensor_reduce(drop[:, :], dsel[:, :, :], AX.X, ALU.add))
                do(dve.tensor_scalar(kept[:, :], drop[:, :], -1.0, 1.0, ALU.mult, ALU.add))
                ch.add(dve.tensor_scalar(e0[:, :], r0[:, :], -1.0, float(NE), ALU.mult, ALU.add))
                ch.add(dve.tensor_scalar(e1[:, :], r1[:, :], -1.0, float(NE), ALU.mult, ALU.add))
                ch.settle()
                tail = slice(NG - 1, NG)
                ch.add(dve.tensor_tensor(e0[:, tail], e0[:, tail], kept[:, 0:1], ALU.mult))
                ch.add(dve.tensor_tensor(e1[:, tail], e1[:, tail], kept[:, 1:2], ALU.mult))
                ch.settle()
                do(dve.tensor_tensor(imax[:, :], e0[:, :], e1[:, :], ALU.max))
                dve.wait_ge(s_ex, 1)
                do(dve.tensor_scalar(den[:, :], ex[:, :], 1.0, None, ALU.add))
                do(dve.reciprocal(s0[:, :], den[:, :]))
                do(dve.tensor_tensor(s1[:, :], s0[:, :], ex[:, :], ALU.mult))
                ch.add(dve.tensor_tensor(cxl[:, 0:1], s0[:, tail], drop[:, 0:1], ALU.mult))
                ch.add(dve.tensor_tensor(cxl[:, 1:2], s1[:, tail], drop[:, 1:2], ALU.mult))
                ch.settle()
                do(dve.tensor_tensor(cxl[:, 0:1], cxl[:, 0:1], cxl[:, 1:2], ALU.add))
                dve.scalar_tensor_tensor(h1l[:, :], xnl[:, :], cxl[:, 0:1], h1l[:, :], ALU.mult,
                                         ALU.add).then_inc(s_fix, 1)
                ch.add(dve.tensor_tensor(s0[:, tail], s0[:, tail], kept[:, 0:1], ALU.mult))
                ch.add(dve.tensor_tensor(s1[:, tail], s1[:, tail], kept[:, 1:2], ALU.mult))
                ch.settle()
                do(dve.tensor_tensor(g.cy[:, :], s0[:, :], s1[:, :], ALU.add))
                do(dve.tensor_tensor(oh0[:, :, :], over_e(imax[:, :]), over_g(index[:, 0:NE]), ALU.is_equal))
                src, dst, step = oh0, sbb, 1
                while step < NG:
                    ch.add(dve.tensor_copy(dst[:, 0:step, :], src[:, 0:step, :]))
                    ch.add(dve.tensor_tensor(dst[:, step:NG, :], src[:, step:NG, :], src[:, 0:NG - step, :], ALU.add))
                    ch.settle()
                    src, dst, step = dst, (sa if dst is sbb else sbb), 2 * step
                assert src is sbb
                do(dve.tensor_copy(sa[:, :, :], sbb[:, :, :]))
                dve.sem_inc(s_tp, 1)
                dve.wait_ge(s_pre, 2)
                do(dve.tensor_copy(tot[:, :], bp[:, NE:2 * NE]))
                do(dve.tensor_scalar(posf[:, :], index[:, 0:NG], float(P), None, ALU.mult))
                do(dve.tensor_tensor(cmp_t[:, :, :], tot[:, :].unsqueeze(2).to_broadcast([P, NE, NG]),
                                     posf[:, :].unsqueeze(1).to_broadcast([P, NE, NG]), ALU.is_gt))
                do(dve.tensor_reduce(nt[:, :], cmp_t[:, :, :], AX.X, ALU.add))
                do(dve.tensor_tensor(bsel[:, :, :], before[:, :, :], nt[:, :].unsqueeze(1).to_broadcast([P, NE, NE]),
                                     ALU.mult))
                do(dve.tensor_reduce(start[:, :], bsel[:, :, :], AX.X, ALU.add))
                do(dve.tensor_tensor(end[:, :], start[:, :], nt[:, :], ALU.add))
                do(dve.tensor_scalar(base[:, :], start[:, :], float(P), -1.0, ALU.mult, ALU.add))
                do(dve.tensor_tensor(base[:, :], bp[:, 0:NE], base[:, :], ALU.add))
                do(dve.tensor_tensor(key[:, :, :], sa[:, :, :], over_g(base[:, :]), ALU.add))
                do(dve.tensor_tensor(key[:, :, :], key[:, :, :], oh0[:, :, :], ALU.mult))
                do(dve.tensor_reduce(posf[:, :], key[:, :, :], AX.X, ALU.add))
                do(dve.tensor_copy(g.pos[:, :], posf[:, :]))
                dve.sem_inc(s_pos, 1)
                do(dve.tensor_tensor(cmp_s[:, :, :], index[:, :].unsqueeze(2).to_broadcast([P, SLOTS, NE]),
                                     end[:, :].unsqueeze(1).to_broadcast([P, SLOTS, NE]), ALU.is_ge))
                do(dve.tensor_reduce(tef[:, :], cmp_s[:, :, :], AX.X, ALU.add))
                do(dve.tensor_scalar(tef[:, :], tef[:, :], float(NE - 1), None, ALU.min))
                do(dve.tensor_copy(g.te[:, :], tef[:, :]))
                dve.wait_ge(s_whi, 1)
                do(dve.scalar_tensor_tensor(g.wl[:, :, :, :], w12[:, :, :, :], WSCALE, g.wh[:, :, :, :], ALU.mult,
                                            ALU.subtract))

            @block.gpsimd
            def _(pool):
                pool.wait_ge(s_pos, 1)
                with pool.Fori(0, NR // RING) as i:
                    for p in range(RING):
                        r = RING * i + p
                        pool.wait_ge(s_row[p], 16 * (i + 1))
                        pool.sem_inc(s_apart, 1)
                        pool.tensor_copy(idx[p][:, :], g.pos[:, ds(r * TC, TC)]).then_inc(s_idx, 1)
                        pool.wait_ge(s_idx, r + 1)
                        pool.sem_inc(s_apart, 1)
                        for t in range(TC):
                            pool.indirect_dma_start(io.XS, bass.IndirectOffsetOnAxis(idx[p][:, t:t + 1], 0),
                                                    rows[p][:, t, :], None).then_inc(s_sc[p], 16)
                pool.wait_ge(s_apart, 2 * NR)
                for p in range(RING):
                    pool.wait_ge(s_sc[p], 16 * NR // RING * TC)


def expert_block(nc, ctx, io, g):
    with ExitStack() as c:
        def sb(name, shape, dt=F32):
            return c.enter_context(nc.sbuf_tensor(name, shape, dt))

        def bank(name):
            return c.enter_context(nc.psum_tensor(name, [P, CH], F32))

        def sem(name):
            return ctx.enter_context(nc.semaphore("ex_" + name))

        x = [sb(f"ex_x{i}", [P, D]) for i in range(2)]
        xth, xtl = ([sb(f"ex_{n}{i}", [P, P], F16) for i in range(2)] for n in ("xth", "xtl"))
        h1s = [sb(f"ex_h{i}", [P, HID]) for i in range(2)]
        pr = [sb(f"ex_pr{i}", [P, HID]) for i in range(2)]
        gl = [sb(f"ex_gl{i}", [P, HID]) for i in range(2)]
        y = [sb(f"ex_y{i}", [P, D]) for i in range(2)]
        b_x, b_y = bank("b_x"), bank("b_y")
        b1, b2 = ([bank(f"{n}{i}") for i in range(2)] for n in ("b1_", "b2_"))
        s_xt, s_xth, s_xts, s_h, s_h1, s_pr, s_gl, s_y, s_ys = (
            sem(n) for n in ("xt_ready", "xt_hi", "xt_copied", "h_ready", "h1_copied", "product", "gelu", "y_ready",
                             "y_copied"))
        s_x, s_out = [sem("x0_in"), sem("x1_in")], [sem("y0_stored"), sem("y1_stored")]

        def all_turns(eng, turn, experts=None):
            def several(s, count, turn_of):
                e = experts(s - 1, count + 1) if experts else [None] * (count + 1)
                for n in range(count):
                    turn_of(n, e[n:n + 2])

            def fixed(s, e):
                turn(s, s % 2, s // 2, lambda k: 0 <= s + k < SLOTS, e)

            loops = (SLOTS - 6) // UNROLL
            rest = 2 + UNROLL * loops
            fixed(-1, None)
            fixed(0, [None] + (experts(0, 1) if experts else []))
            several(1, 1, lambda n, e: fixed(1, e))
            with eng.Fori(0, loops) as i:
                several(UNROLL * i + 2, UNROLL, lambda n, e: turn(
                    UNROLL * i + 2 + n, n % 2, UNROLL // 2 * i + 1 + n // 2, lambda k: True, e))
            several(rest, SLOTS - rest, lambda n, e: fixed(rest + n, e))
            fixed(SLOTS, experts(SLOTS - 1, 1) if experts else None)

        with nc.Block() as block:
            @block.sync
            def _(sp):
                xs = io.XS.rearrange("(s p) d -> s p d", p=P)
                ys = io.YS.rearrange("(s p) d -> s p d", p=P)

                def load(s, p):
                    sp.dma_start(x[p][:, :], xs[ds(s, 1)].rearrange("o p d -> (o p) d")).then_inc(s_x[p], 16)

                def turn(s, p, nth, has, e):
                    if has(3):
                        sp.wait_ge(s_xt, s + 2)
                        load(s + 3, 1 - p)
                    if has(-1):
                        sp.wait_ge(s_ys, s - 1 + 2)
                        sp.dma_start(ys[ds(s - 1, 1)].rearrange("o p d -> (o p) d"),
                                     y[1 - p][:, :]).then_inc(s_out[1 - p], 16)

                for p in range(2):
                    sp.sem_inc(s_out[p], 16)
                    load(p, p)
                all_turns(sp, turn)
                for p in range(2):
                    sp.wait_ge(s_out[p], 16 * (SLOTS // 2 + 1))

            @block.tensor
            def _(pe):
                pe.wait_ge(g.s_w, 16)

                def turn(s, p, nth, has, e):
                    if has(1):
                        pe.wait_ge(s_x[1 - p], 16 * (nth + 1 + p))
                        pe.wait_ge(s_xts, s + 2)
                        pe.transpose(b_x[:, 0:P], x[1 - p][:, :], g.ident[:, :]).then_inc(s_xt, 1)
                    if has(0):
                        pe.wait_ge(s_xts, s + 2)
                        pe.wait_ge(s_pr, s + 1)
                        for i, out in enumerate((b1[p], b2[p])):
                            for q in range(TC):
                                for n, (w, xs) in enumerate(((g.wh, xth), (g.wh, xtl), (g.wl, xth))):
                                    ins = pe.matmul(out[:, q * P:(q + 1) * P],
                                                    w[:, i, ds(e[1], 1), q * P:(q + 1) * P].rearrange("p o h -> p (o h)"),
                                                    xs[p][:, :], start=(n == 0), stop=(n == 2))
                        ins.then_inc(s_h, 1)
                    if has(-1):
                        pe.wait_ge(s_gl, s)
                        pe.wait_ge(s_ys, s)
                        for q in range(TC):
                            ins = pe.matmul(b_y[:, 0:D], gl[1 - p][:, q * P:(q + 1) * P],
                                            g.w3[:, ds(e[0], 1), q, :].rearrange("p o d -> p (o d)"), start=(q == 0),
                                            stop=(q == TC - 1))
                        ins.then_inc(s_y, 1)

                registers = [pe.alloc_register(f"expert{n}") for n in range(SLOTS % UNROLL + 2 * UNROLL)]

                def experts(s, count):
                    pe.load(registers[:count], g.te[0:1, ds(s, count)])
                    return [pe.snap(r, min_val=0, max_val=NE - 1) for r in registers[:count]]

                all_turns(pe, turn, experts)

            @block.scalar
            def _(act):
                def turn(s, p, nth, has, e):
                    if has(1):
                        act.wait_ge(s_xt, s + 2)
                        if has(-1):
                            act.wait_ge(s_h, s)
                        act.activation(xth[1 - p][:, :], b_x[:, 0:P], ACT.Identity).then_inc(s_xth, 1)
                    if has(-1):
                        act.wait_ge(s_pr, s + 2)
                        act.activation(gl[1 - p][:, :], pr[1 - p][:, :], ACT.Gelu).then_inc(s_gl, 1)
                    if has(0):
                        act.wait_ge(s_h, s + 1)
                        act.activation(h1s[p][:, :], b1[p][:, :], ACT.Identity,
                                       scale=WSCALE ** -2).then_inc(s_h1, 1)

                all_turns(act, turn)

            @block.vector
            def _(dve):
                dve.sem_inc(s_pr, 2)
                dve.sem_inc(s_ys, 1)
                dve.sem_inc(s_xts, 1)

                def turn(s, p, nth, has, e):
                    if has(1):
                        dve.wait_ge(s_xth, s + 2)
                        dve.tensor_tensor(xtl[1 - p][:, :], b_x[:, 0:P], xth[1 - p][:, :],
                                          ALU.subtract).then_inc(s_xts, 1)
                    if has(0):
                        dve.wait_ge(s_h1, s + 1)
                        dve.tensor_tensor(pr[p][:, :], b2[p][:, :], h1s[p][:, :], ALU.mult).then_inc(s_pr, 1)
                    if has(-1):
                        dve.wait_ge(s_y, s)
                        dve.wait_ge(s_out[1 - p], 16 * (nth + p))
                        dve.tensor_copy(y[1 - p][:, :], b_y[:, 0:D]).then_inc(s_ys, 1)

                all_turns(dve, turn)


def combine_block(nc, ctx, io, g):
    with ExitStack() as c:
        def sb(name, shape, dt=F32):
            return c.enter_context(nc.sbuf_tensor(name, shape, dt))

        def sem(name):
            return ctx.enter_context(nc.semaphore("co_" + name))

        idx = [sb(f"co_idx{i}", [P, TC], I32) for i in range(2)]
        cy = [sb(f"co_cy{i}", [P, TC]) for i in range(2)]
        yg = [sb(f"co_y{i}", [P, TC, D]) for i in range(2)]
        h1 = [sb(f"co_h{i}", [P, TC, D]) for i in range(2)]
        o = [sb(f"co_o{i}", [P, TC, D]) for i in range(2)]
        s_idx, s_done, s_out, s_ofree = sem("idx"), sem("done"), sem("stored"), sem("out_free")
        s_y, s_h = [sem("y0"), sem("y1")], [sem("h0"), sem("h1")]
        with nc.Block() as block:
            @block.gpsimd
            def _(pool):
                pool.sem_inc(s_done, 2)
                with pool.Fori(0, NR // 2) as i:
                    for p in range(2):
                        r = 2 * i + p
                        pool.wait_ge(s_done, r + 1)
                        pool.sem_inc(s_idx, 1)
                        pool.tensor_copy(idx[p][:, :], g.pos[:, ds(r * TC, TC)]).then_inc(s_idx, 1)
                        pool.wait_ge(s_idx, 3 * r + 2)
                        pool.sem_inc(s_idx, 1)
                        for t in range(TC):
                            pool.indirect_dma_start(yg[p][:, t, :], None, io.YS,
                                                    bass.IndirectOffsetOnAxis(idx[p][:, t:t + 1], 0)).then_inc(s_y[p], 16)

            @block.sync
            def _(sp):
                rows = io.out.rearrange("b s d -> (b s) d").rearrange("(r t p) d -> r p t d", t=TC, p=P)

                def load(r, p):
                    sp.dma_start(h1[p][:, :, :].rearrange("p t d -> p (t d)"),
                                 io.H1[ds(r, 1)].rearrange("o p n -> (o p) n")).then_inc(s_h[p], 16)

                def turn(i, more):
                    for p in range(2):
                        r = 2 * i + p
                        sp.wait_ge(s_done, r + 3)
                        if more:
                            load(r + 2, p)
                        sp.dma_start(rows[ds(r, 1)].rearrange("o p t d -> (o p) t d"), o[p][:, :, :]).then_inc(s_out, 16)
                        sp.wait_ge(s_out, 16 * (r + 1))
                        sp.sem_inc(s_ofree, 1)

                sp.sem_inc(s_ofree, 2)
                for p in range(2):
                    load(p, p)
                with sp.Fori(0, NR // 2 - 1) as i:
                    turn(i, True)
                turn(NR // 2 - 1, False)

            @block.vector
            def _(dve):
                with dve.Fori(0, NR // 2) as i:
                    for p in range(2):
                        r = 2 * i + p
                        dve.wait_ge(s_y[p], 16 * TC * (i + 1))
                        dve.wait_ge(s_h[p], 16 * (i + 1))
                        dve.wait_ge(s_ofree, r + 1)
                        for t in range(TC):
                            ins = dve.scalar_tensor_tensor(o[p][:, t, :], yg[p][:, t, :], g.cy[:, ds(r * TC + t, 1)],
                                                           h1[p][:, t, :], ALU.mult, ALU.add)
                        ins.then_inc(s_done, 1)


STAGES = (setup_block, embed_block, attend_block, project_block, route_block, expert_block, combine_block)


def program(nc, io):
    def dram(name, shape, dt=F32):
        return nc.dram_tensor(name, shape, dt, kind="Internal").ap()

    io.H0 = dram("h0_rows", (B, P, NT, D))
    io.QK = dram("qk_parts", (UNITS + 1, 2, PART, S), F16)
    io.VS = dram("v_rows", (UNITS + 1, P, NT * VW))
    io.WP3 = dram("wpos_parts", (NH + 1, PART, 2 * D), F16)
    io.CT = dram("context", (B, P, S))
    io.H1 = dram("residual", (NR, P, TC * D))
    io.XN = dram("normed_rows", (NR, P, TC * D))
    io.XS = dram("routed_rows", (SLOTS * P, D))
    io.YS = dram("expert_rows", (SLOTS * P, D))
    with ExitStack() as ctx:
        def sb(name, shape, dt=F32):
            return ctx.enter_context(nc.sbuf_tensor(name, shape, dt))

        g = Names()
        g.ident, g.ident16 = sb("ident_sb", [P, P]), sb("ident16_sb", [P, P], F16)
        g.wt = sb("wt", [P, 4, D])
        g.bqs, g.bk, g.gamma, g.beta = (sb(n, [P, 1]) for n in ("bqs", "bk_sb", "gamma_sb", "beta_sb"))
        g.rb = sb("rb", [P, 2, NH + 1])
        g.lg = sb("logits", [P, NG, NE])
        g.cy = sb("cy", [P, NG])
        g.pos = sb("pos", [P, NG], I32)
        g.te = sb("tile_expert", [P, SLOTS], I32)
        for stage in STAGES:
            stage(nc, ctx, io, g)


def tables():
    half = D // 2
    f = np.exp(np.arange(0, D, 2, dtype=np.float32) * np.float32(-np.log(10000.0) / D))
    w = f.astype(np.float64)[:, None]

    def table(n):
        return np.concatenate([np.sin(w * n), np.cos(w * n)], 0)

    j = np.arange(S, dtype=np.float64)[None, :]
    tabs = []
    for t in (table(j), table(j - S)):
        hi = t.astype(np.float16)
        tabs += [hi, (t - hi.astype(np.float64)).astype(np.float16)]
    turn = w * (S - 1 - j)
    rot = np.stack([np.concatenate([np.cos(turn), np.cos(turn)], 0), np.concatenate([-np.sin(turn), np.sin(turn)], 0)])
    pos = np.arange(2 * S_IMG, dtype=np.float32)[:, None]
    pe = np.zeros((2 * S_IMG, D), np.float32)
    pe[:, 0::2] = np.sin(pos * f)
    pe[:, 1::2] = np.cos(pos * f)
    row, col = np.arange(P)[:, None], np.arange(DW)[None, :]
    heads = np.zeros((P, NH + 1), np.float32)
    heads[np.arange(P), np.arange(P) // DH] = 1
    heads[:, NH] = heads[:, 0]
    pick = np.zeros((P, 2, 2, VW), np.float32)
    for g in range(4):
        for what in range(2):
            for par in range(2):
                for d in range(DH):
                    pick[g * VW + what * DH + d, what, par, par * DH + d] = 1
    last = np.zeros((P, 1), np.float32)
    last[P - 1] = 1
    c = {
        "pe_tok": pe[:S_IMG],
        "tabs": np.stack(tabs),
        "rot": rot.astype(np.float32),
        "ident": np.eye(P, dtype=np.float32),
        "ident16": np.eye(P, dtype=np.float16),
        "mask1": np.repeat((row < col).astype(np.float32)[:, None], 3, 1),
        "mask2": np.repeat((row > col).astype(np.int32)[:, None], 3, 1),
        "head_mask": heads,
        "pick": pick,
        "last": last,
        "tri": (row < np.arange(P)[None, :]).astype(np.float32),
        "ones": np.ones((P, P), np.float32),
        "rank": np.broadcast_to(NE - np.arange(NE, dtype=np.float32), (P, NE)).copy(),
        "index": np.broadcast_to(np.arange(SLOTS, dtype=np.float32), (P, SLOTS)).copy(),
        "before": np.broadcast_to((np.arange(NE)[None, :] < np.arange(NE)[:, None]).astype(np.float32),
                                  (P, NE, NE)).copy(),
    }
    return c


_INS = ["x", "txt", "L0_tok_W", "L0_attn_gamma", "L0_attn_beta", "L0_attn_Wq", "L0_attn_bq", "L0_attn_Wk",
        "L0_attn_bk", "L0_attn_Wv", "L0_attn_bv", "L0_attn_Wpos", "L0_attn_u_bias", "L0_attn_v_bias", "L0_attn_Wo",
        "L0_attn_bo", "L0_ffn_Wr", "L0_ffn_br", "L0_ffn_W1", "L0_ffn_W2", "L0_ffn_W3"]
_SHORT = ["x", "txt", "Wtok", "gamma", "beta", "Wq", "bq", "Wk", "bk", "Wv", "bv", "Wpos", "u", "v", "Wo", "bo",
          "Wr", "br", "W1", "W2", "W3"]


def kernel(**inputs):
    import concourse.bacc as bacc
    from concourse.bass_utils import run_bass_kernel_spmd

    nc = bacc.Bacc("TRN2", target_bir_lowering=False, num_devices=1)
    arrays, io = {}, Names()
    given = [(short, inputs[name]) for short, name in zip(_SHORT, _INS)] + list(tables().items())
    for name, a in given:
        a = np.ascontiguousarray(a)
        arrays[f"in_{name}"] = a
        vars(io)[name] = nc.dram_tensor(f"in_{name}", a.shape, mybir.dt.from_np(a.dtype), kind="ExternalInput").ap()
    io.out = nc.dram_tensor("out", (B, S, D), F32, kind="ExternalOutput").ap()
    program(nc, io)
    r = run_bass_kernel_spmd(nc, [arrays], core_ids=[0])
    return r.results[0]["out"]
```

```python
from contextlib import ExitStack

import numpy as np

import concourse.bass as bass
from concourse import mybir

F32 = mybir.dt.float32
F16 = mybir.dt.float16
I32 = mybir.dt.int32
U32 = mybir.dt.uint32
ACT = mybir.ActivationFunctionType
ALU = mybir.AluOpType
AX = mybir.AxisListType
ds = bass.ds

P = 128
B = 8
S_IMG, S_TXT = 1024, 512
S = S_IMG + S_TXT
D = 128
NH, DH = 8, 16
UNITS = B * NH
F_IN = 29
NE = 8
HID = 512
CH = 512
NT = S // P
NC = S // CH
TC = CH // P
NG = B * NT
NR = B * NC
TOKENS = B * S
SLOTS = NG + NE
PART = 3 * DH
EPS = 1e-5
QSCALE = float(1.0 / np.sqrt(np.float32(D)))
WSCALE = 64.0
HEADS = 4
UNROLL = 8
ROW = 2 * D + 2
BLANK = SLOTS * P // UNITS
RING = 4
VW = 2 * DH
DW = P + 1


class Chain:

    def __init__(self, eng, sem, base=0):
        self.eng, self.sem, self.base, self.n = eng, sem, base, 0

    def add(self, ins):
        ins.then_inc(self.sem, 1)
        self.n += 1

    def settle(self):
        self.eng.wait_ge(self.sem, self.base + self.n)

    def settle_apart(self):
        self.settle()
        self.eng.sem_inc(self.sem, 1)
        self.n += 1


class Names:
    pass


def setup_block(nc, ctx, io, g):
    with ExitStack() as c:
        def sb(name, shape, dt=F32):
            return c.enter_context(nc.sbuf_tensor(name, shape, dt))

        def sem(name):
            return ctx.enter_context(nc.semaphore(name))

        wnat = sb("wnat", [P, 5, D])
        wph = sb("wph", [P, 2, D], F16)
        wpl = sb("wpl", [P, 2, D], F16)
        wpp = sb("wpp", [P, 2, D])
        vec = sb("vec", [P, 3])
        tmp = sb("tmp", [P, 3])
        hm = sb("hm", [P, NH + 1])
        bd = sb("bd", [P, NH + 1])
        pw = c.enter_context(nc.psum_tensor("pw", [P, 4, D], F32))
        prb = c.enter_context(nc.psum_tensor("prb", [P, 2, NH + 1], F32))
        s_in, s_wt, s_rb, s_chain, s_wp, s_out, s_bd = (
            sem(n) for n in ("su_in", "su_wt", "su_rb", "su_chain", "su_wp", "su_out", "su_bd"))
        loads = [
            (wnat[:, 0, :], io.Wq), (wnat[:, 1, :], io.Wk), (wnat[:, 2, :], io.Wv), (wnat[:, 3, :], io.Wo),
            (wnat[:, 4, :], io.Wpos), (g.ident[:, :], io.ident), (g.ident16[:, :], io.ident16),
            (vec[:, 0:1], io.bq.unsqueeze(1)), (vec[:, 1:2], io.u.rearrange("h d -> (h d)").unsqueeze(1)),
            (vec[:, 2:3], io.v.rearrange("h d -> (h d)").unsqueeze(1)),
            (g.bk[:, 0:1], io.bk.unsqueeze(1)), (g.gamma[:, 0:1], io.gamma.unsqueeze(1)),
            (g.beta[:, 0:1], io.beta.unsqueeze(1)), (hm[:, :], io.head_mask),
        ]
        with nc.Block() as block:
            @block.sync
            def _(sp):
                for dst, src in loads:
                    sp.dma_start(dst, src).then_inc(s_in, 16)
                sp.wait_ge(s_wp, 1)
                for part, w in enumerate((wph, wpl, wph)):
                    rows = slice(part * DH, (part + 1) * DH)
                    sp.dma_start(io.WP3[0:NH, rows, :], w[:, :, :].rearrange("p a k -> p (a k)")).then_inc(s_out, 16)
                    sp.dma_start(io.WP3[NH, rows, :], w[0:DH, :, :].rearrange("p a k -> p (a k)")).then_inc(s_out, 16)
                sp.wait_ge(s_out, 16 * 6)

            @block.tensor
            def _(pe):
                pe.wait_ge(s_in, 16 * len(loads))
                for i in range(4):
                    ins = pe.transpose(pw[:, i, :], wnat[:, i, :], g.ident[:, :])
                ins.then_inc(s_wt, 1)
                pe.wait_ge(s_bd, 1)
                for i in range(2):
                    ins = pe.matmul(prb[:, i, :], wpp[:, i, :], bd[:, :], start=True, stop=True)
                ins.then_inc(s_rb, 1)

            @block.vector
            def _(dve):
                ch = Chain(dve, s_chain)
                dve.wait_ge(s_in, 16 * len(loads))
                ch.add(dve.tensor_tensor(tmp[:, 0:1], vec[:, 0:1], vec[:, 1:2], ALU.add))
                ch.add(dve.tensor_tensor(tmp[:, 1:2], vec[:, 2:3], vec[:, 1:2], ALU.subtract))
                wp = wnat[:, 4, :].rearrange("p (k two) -> p two k", two=2)
                half = D // 2
                ch.add(dve.tensor_copy(wpp[:, 0, 0:half], wp[:, 0, :]))
                ch.add(dve.tensor_copy(wpp[:, 0, half:D], wp[:, 1, :]))
                ch.add(dve.tensor_copy(wpp[:, 1, 0:half], wp[:, 1, :]))
                ch.add(dve.tensor_copy(wpp[:, 1, half:D], wp[:, 0, :]))
                ch.settle()
                ch.add(dve.tensor_scalar(g.bqs[:, 0:1], tmp[:, 0:1], QSCALE, None, ALU.mult))
                ch.add(dve.tensor_scalar(tmp[:, 2:3], tmp[:, 1:2], QSCALE, None, ALU.mult))
                ch.add(dve.tensor_copy(wph[:, :, :], wpp[:, :, :]))
                ch.settle()
                dve.tensor_scalar(bd[:, :], hm[:, :], tmp[:, 2:3], None, ALU.mult).then_inc(s_bd, 1)
                dve.tensor_tensor(wpl[:, :, :], wpp[:, :, :], wph[:, :, :], ALU.subtract).then_inc(s_wp, 1)
                dve.wait_ge(s_wt, 1)
                dve.tensor_copy(g.wt[:, :, :], pw[:, :, :])
                dve.wait_ge(s_rb, 1)
                dve.tensor_copy(g.rb[:, :, :], prb[:, :, :])


def embed_block(nc, ctx, io, g):
    def kept(name, shape, dt=F32):
        return ctx.enter_context(nc.sbuf_tensor(name, shape, dt))

    g.tabs = kept("tabs", [P, 4, S], F16)
    g.rot = kept("rot", [P, 2, S])
    g.mask1 = kept("mask1", [P, 3, DW])
    g.mask2 = kept("mask2", [P, 3, DW], I32)
    g.pick = kept("pick", [P, 2, 2, VW])
    g.s_tables = ctx.enter_context(nc.semaphore("tables"))
    with ExitStack() as c:
        def sb(name, shape, dt=F32):
            return c.enter_context(nc.sbuf_tensor(name, shape, dt))

        def bank(name):
            return c.enter_context(nc.psum_tensor(name, [P, CH], F32))

        def sem(name):
            return ctx.enter_context(nc.semaphore(name))

        x8 = sb("x8", [P, 8, F_IN])
        pe_tok = sb("pe_tok", [P, 8, D])
        wtok = sb("wtok", [F_IN, D])
        bvb = sb("bvb", [P, D])
        xt = sb("xt", [F_IN, 2, CH])
        h = sb("h", [P, NT, D])
        z = sb("z", [P, NT, D])
        z2 = [sb(f"z2_{p}", [P, NT, D]) for p in range(2)]
        st = sb("st", [P, NT, 6])
        mv = sb("mv", [P, NT, 2])
        std = sb("std", [P, NT])
        rstd = sb("rstd", [P, NT])
        var = sb("var", [P, NT])
        xn = sb("xn", [P, S])
        full = sb("full", [P, 2, S])
        hi, lo = ([sb(f"{n}{p}", [P, 2, S], F16) for p in range(2)] for n in ("hi", "lo"))
        vals = [sb(f"vals{p}", [P, NH, NT, VW]) for p in range(2)]
        b_xt, b_emb, b_z, b_q, b_k = (bank(n) for n in ("b_xt", "b_emb", "b_z", "b_q", "b_k"))
        b_v = [bank(f"b_v{i}") for i in range(NC)]
        (s_const, s_x, s_xt, s_xts, s_emb, s_hpart, s_h0, s_h0out, s_hread, s_z, s_zt, s_xn, s_qk, s_full, s_lo, s_v,
         s_vs, s_var, s_std, s_chain) = (
            sem("em_" + n) for n in (
                "const", "x_in", "xt_ready", "xt_copied", "emb_ready", "h_part", "h_done", "h_stored", "h_read",
                "z_done", "zt_ready", "xn_ready", "qk_ready", "full_ready", "lo_done", "v_ready", "v_done",
                "var_ready", "std_ready", "chain"))
        s_out = [sem(f"em_out_stored{p}") for p in range(2)]
        links = 2 * (2 * NT + 3)

        def all_turns(eng, turn):
            turn(-1, 1, None, 2, False)
            with eng.Fori(0, B // 2 - 1) as i:
                for p in range(2):
                    turn(2 * i + p, p, i, 2, True)
            turn(B - 2, 0, B // 2 - 1, 1, True)
            turn(B - 1, 1, B // 2 - 1, 0, True)

        with nc.Block() as block:
            @block.sync
            def _(sp):
                def load(b):
                    sp.dma_start(x8[:, :, :], io.x[ds(b, 1)].rearrange("o a c f -> (o a c) f").rearrange(
                        "(t p) f -> p t f", p=P)).then_inc(s_x, 16)
                    sp.dma_start(h[:, 8:12, :], io.txt[ds(b, 1)].rearrange("o s d -> (o s) d").rearrange(
                        "(t p) d -> p t d", p=P)).then_inc(s_x, 16)

                def turn(b, p, nth, ahead, here):
                    if ahead:
                        sp.wait_ge(s_h0, b + 2)
                        sp.dma_start(io.H0[ds(b + 1, 1)].rearrange("o p t d -> (o p) (t d)"),
                                     h[:, :, :].rearrange("p t d -> p (t d)")).then_inc(s_h0out, 16)
                        sp.wait_ge(s_h0out, 16 * (b + 2))
                        sp.wait_ge(s_hread, b + 2)
                        if ahead == 2:
                            load(b + 2)
                    if here:
                        sp.wait_ge(s_lo, NC * (b + 2))
                        for t, parts in ((0, (hi[p], hi[p], lo[p])), (1, (hi[p], lo[p], hi[p]))):
                            dst = io.QK[ds(NH * b, NH), t, :, :]
                            for part, w in enumerate(parts):
                                sp.dma_start(dst[:, part * DH:(part + 1) * DH, :], w[:, t, :]).then_inc(s_out[p], 16)
                        sp.wait_ge(s_vs, NC * (b + 1) + 1)
                        sp.dma_start(io.VS[ds(NH * b, NH)].rearrange("h p n -> p h n"),
                                     vals[p][:, :, :, :].rearrange("p h t w -> p h (t w)")).then_inc(s_out[p], 16)

                load(0)
                sp.dma_start(pe_tok[:, :, :], io.pe_tok.rearrange("(t p) d -> p t d", p=P)).then_inc(s_const, 16)
                sp.dma_start(wtok[:, :], io.Wtok).then_inc(s_const, 16)
                sp.dma_start(bvb[:, :], io.bv.partition_broadcast(P)).then_inc(s_const, 16)
                for p in range(2):
                    sp.sem_inc(s_out[p], 16 * 7)
                all_turns(sp, turn)
                for p in range(2):
                    sp.wait_ge(s_out[p], 16 * 7 * (B // 2 + 1))

            @block.gpsimd
            def _(pool):
                pool.wait_ge(s_hread, 1)
                for dst, src in ((g.tabs[:, :, :], io.tabs.rearrange("a p s -> p a s")),
                                 (g.rot[:, :, :], io.rot.rearrange("a p s -> p a s")),
                                 (g.mask1[:, :, :], io.mask1), (g.mask2[:, :, :], io.mask2),
                                 (g.pick[:, :, :, :], io.pick)):
                    pool.dma_start(dst, src).then_inc(g.s_tables, 16)

                def turn(b, p, nth, ahead, here):
                    for k in range(NC if here else 0):
                        cols = slice(k * CH, (k + 1) * CH)
                        if k == 0:
                            pool.wait_ge(s_out[p], 16 * 7 * (nth + 1))
                        pool.wait_ge(s_full, NC * b + k + 2)
                        pool.tensor_tensor(lo[p][:, :, cols], full[:, :, cols], hi[p][:, :, cols],
                                           ALU.subtract).then_inc(s_lo, 1)

                all_turns(pool, turn)

            @block.tensor
            def _(pe):
                pe.wait_ge(s_const, 48)

                def turn(b, p, nth, ahead, here):
                    if ahead:
                        pe.wait_ge(s_x, 32 * (b + 2))
                        for q in range(2):
                            if q == 1:
                                pe.wait_ge(s_xts, 2 * b + 3)
                            for t in range(TC):
                                ins = pe.transpose(b_xt[0:F_IN, t * P:(t + 1) * P], x8[:, TC * q + t, :], g.ident[:, :])
                            ins.then_inc(s_xt, 1)
                            pe.wait_ge(s_xts, 2 * b + q + 3)
                            if q == 1:
                                pe.wait_ge(s_hpart, 2 * b + 3)
                            for t in range(TC):
                                ins = pe.matmul(b_emb[:, t * P:(t + 1) * P], xt[:, q, t * P:(t + 1) * P], wtok[:, :],
                                                start=True, stop=True)
                            ins.then_inc(s_emb, 1)
                    if here:
                        pe.wait_ge(s_z, b + 1)
                        for k in range(NC):
                            for t in range(TC):
                                ins = pe.transpose(b_z[:, t * P:(t + 1) * P], z2[p][:, TC * k + t, :], g.ident[:, :])
                            ins.then_inc(s_zt, 1)
                            pe.wait_ge(s_xn, NC * b + k + 1)
                            pe.wait_ge(s_full, NC * b + k + 1)
                            pe.matmul(b_q[:, :], g.wt[:, 0, :], xn[:, k * CH:(k + 1) * CH], start=True, stop=True)
                            pe.matmul(b_k[:, :], g.wt[:, 1, :], xn[:, k * CH:(k + 1) * CH],
                                      start=True, stop=True).then_inc(s_qk, 1)
                            if k == 0:
                                pe.wait_ge(s_vs, NC * b + 1)
                            for t in range(TC):
                                ins = pe.matmul(b_v[k][:, t * P:(t + 1) * P], xn[:, k * CH + t * P:k * CH + (t + 1) * P],
                                                g.wt[:, 2, :], start=True, stop=True)
                            ins.then_inc(s_v, 1)

                all_turns(pe, turn)

            @block.scalar
            def _(act):
                act.sem_inc(s_full, 1)

                def turn(b, p, nth, ahead, here):
                    def root(n):
                        act.wait_ge(s_var, 2 * b + n + 3)
                        act.activation(std[:, :], var[:, :], ACT.Sqrt).then_inc(s_std, 1)

                    if ahead and not here:
                        root(0)
                        root(1)
                    if here:
                        for k in range(NC):
                            if ahead and k == NC - 1:
                                root(1)
                            cols = slice(k * CH, (k + 1) * CH)
                            act.wait_ge(s_zt, NC * b + k + 1)
                            act.activation(xn[:, cols], b_z[:, :], ACT.Identity, bias=g.beta[:, 0:1],
                                           scale=g.gamma[:, 0:1]).then_inc(s_xn, 1)
                            if ahead and k == 0:
                                root(0)
                            act.wait_ge(s_qk, NC * b + k + 1)
                            act.wait_ge(s_lo, NC * b + k + 1)
                            if k == 0:
                                act.wait_ge(s_out[p], 16 * 7 * (nth + 1))
                            for dst in (full, hi[p]):
                                act.activation(dst[:, 0, cols], b_q[:, :], ACT.Identity, bias=g.bqs[:, 0:1],
                                               scale=QSCALE)
                                ins = act.activation(dst[:, 1, cols], b_k[:, :], ACT.Identity, bias=g.bk[:, 0:1])
                            ins.then_inc(s_full, 1)

                all_turns(act, turn)

            @block.vector
            def _(dve):
                dve.sem_inc(s_vs, 1)
                dve.sem_inc(s_lo, NC)
                for p in range(2):
                    dve.memset(vals[p][:, :, :, :], 1.0)
                dve.wait_ge(s_const, 48)

                def turn(b, p, nth, ahead, here):
                    ch = Chain(dve, s_chain, links * (b + 1))

                    def parts(k):
                        dve.wait_ge(s_v, NC * b + k + 1)
                        if k == 0:
                            dve.wait_ge(s_out[p], 16 * 7 * (nth + 1))
                        dve.tensor_tensor(
                            vals[p][:, :, TC * k:TC * (k + 1), 0:DH],
                            b_v[k][:, :].rearrange("p (t h d) -> p h t d", t=TC, h=NH),
                            bvb[:, :].rearrange("p (h d) -> p h d", h=NH).unsqueeze(2).to_broadcast([P, NH, TC, DH]),
                            ALU.add).then_inc(s_vs, 1)

                    if not ahead:
                        for k in range(NC):
                            parts(k)
                        return
                    dve.wait_ge(s_x, 32 * (b + 2))
                    for q in range(2):
                        dve.wait_ge(s_xt, 2 * b + q + 3)
                        dve.tensor_copy(xt[:, q, :], b_xt[0:F_IN, :]).then_inc(s_xts, 1)
                        dve.wait_ge(s_emb, 2 * b + q + 3)
                        dve.tensor_tensor(h[:, TC * q:TC * (q + 1), :], b_emb[:, :].rearrange("p (t d) -> p t d", t=TC),
                                          pe_tok[:, TC * q:TC * (q + 1), :], ALU.add).then_inc(s_hpart, 1)
                    dve.wait_ge(s_hpart, 2 * b + 4)
                    dve.sem_inc(s_h0, 1)
                    for n, (src, dst) in enumerate(((h, z), (z, z2[1 - p]))):
                        for t in range(NT):
                            ch.add(dve.bn_stats(st[:, t, :], src[:, t, :]))
                        ch.settle_apart()
                        for t in range(NT):
                            ins = dve.bn_aggr(mv[:, t, :], st[:, t, :])
                            if t == NT - 1:
                                ch.add(ins)
                        ch.settle()
                        dve.tensor_scalar(var[:, :], mv[:, :, 1], EPS, None, ALU.add).then_inc(s_var, 1)
                        dve.wait_ge(s_std, 2 * b + n + 3)
                        ch.add(dve.reciprocal(rstd[:, :], std[:, :]))
                        ch.settle()
                        for t in range(NT):
                            ch.add(dve.tensor_scalar(dst[:, t, :], src[:, t, :], mv[:, t, 0:1], rstd[:, t:t + 1],
                                                     ALU.subtract, ALU.mult))
                        ch.settle()
                        dve.sem_inc(s_z if n else s_hread, 1)
                        if here:
                            parts(n)
                    if here:
                        parts(NC - 1)
                    assert ch.n == links

                all_turns(dve, turn)


def unit_order():
    after = {"R": (5, 7, 9), "RC": (7, 9, 11), "X": (10, 12, 14, 16), "XC": (11, 13, 15, 17), "EV": (14, 26),
             "PV": (5, 9, 13, 17, 21, 25, 29), "NM": (32,), "GUARD": (34,)}
    steps, m = [], 0

    def maxima(count):
        nonlocal m
        for _ in range(min(count, NT * NC - m)):
            steps.append(("PRE", m))
            m += 1

    for n in range(NT * NC):
        steps.append(("S", n))
        if n >= 16:
            maxima(1 if n == 16 else 2)
        for kind, places in after.items():
            if n in places:
                steps.append((kind, places.index(n)))
                if kind == "PV" and n >= 16:
                    maxima(1)
    assert m == NT * NC
    return steps + [("PV", NT * NC // TC - 2), ("PV", NT * NC // TC - 1), ("EV", NC - 1)]


PREPARE = ([(kind, k) for kind in ("R", "RC") for k in range(NC)]
           + [(kind, j) for j in range(4) for kind in ("X", "XC")] + [("PRE", m) for m in range(NT * NC)]
           + [("NM", 0), ("GUARD", 0)])
STEPS = NT * NC
GROUPS = STEPS // TC
SHARED = 3 + 4 + 1
SHARED_B = SHARED * NH + NC
LINKS_PREP = 2 * 4


def attend_block(nc, ctx, io, g):
    with ExitStack() as c:
        def sb(name, shape, dt=F32):
            return c.enter_context(nc.sbuf_tensor(name, shape, dt))

        def bank(name):
            return c.enter_context(nc.psum_tensor(name, [P, CH], F32))

        def sem(name):
            return ctx.enter_context(nc.semaphore("at_" + name))

        def pair(name, shape, dt=F32):
            return [sb(f"{name}{p}", shape, dt) for p in range(2)]

        tabs, rot, mask1, mask2, pick = g.tabs, g.rot, g.mask1, g.mask2, g.pick
        k3, q3 = pair("k3", [P, S], F16), pair("q3", [P, S], F16)
        vo, wp3 = pair("vo", [P, NT * VW]), pair("wp3", [PART, 2 * D], F16)
        ah, al = pair("ah", [P, S + 4], F16), pair("al", [P, S + 4], F16)
        dgh, dgl = pair("dgh", [P, NT, DW], F16), pair("dgl", [P, NT, DW], F16)
        ta, tb, af = sb("ta", [P, NC, CH]), sb("tb", [P, NC, CH]), sb("af", [P, NC, CH])
        dt = sb("dt", [P, 4, 3 * DW])
        pt = sb("pt", [P, 8, CH])
        part_max, nm, nmh = sb("part_max", [P, STEPS]), sb("nm", [P, NT]), sb("nmh", [NT, P], F16)
        osb = sb("osb", [P, NH, S])
        sums, cx = sb("sums", [P, S]), sb("cx", [P, S])
        score = [bank(f"score{i}") for i in range(3)]
        pre = [bank(f"pre{i}") for i in range(2)]
        shared = [bank(f"shared{i}") for i in range(2)]
        o_bank = bank("o_bank")
        s_clear, s_ahead = sem("cleared"), sem("unit_ahead")
        s_load = [sem("loaded0"), sem("loaded1")]
        s_score, s_exp, s_pv, s_evac = sem("score"), sem("exp"), sem("pv"), sem("evac")
        s_pre, s_max, s_shared, s_sread = sem("pre"), sem("max"), sem("shared"), sem("shared_read")
        s_a, s_dg = sem("a_ready"), sem("diag_ready")
        s_nm, s_guard, s_blank = sem("nm"), sem("guard"), sem("blank_rows")
        s_cxout, s_cxfree, s_apart = sem("cx_stored"), sem("cx_free"), sem("apart")
        s_sums, s_copied, s_cx, s_vchain, s_af, s_ah, s_dt, s_hi = (sem(n) for n in ("sums", "context_copied", "context", "vector_chain", "turned", "turned_hi", "diag", "diag_hi"))
        order = unit_order()

        def scores(pe, n, p, u):
            k, t = n // NT, n % NT
            lo, hi = k * CH, (k + 1) * CH
            out = score[n % 3]
            pe.wait_ge(s_exp, u * STEPS + n + 1)
            keys = slice(t * P, (t + 1) * P)
            first = True
            a, b = max(lo, min(hi, t * P - 1)), max(lo, min(hi, t * P + P - 1))
            if lo < a:
                for tab, w in ((2, ah), (2, al), (3, ah)):
                    pe.matmul(out[:, 0:a - lo], tabs[:, tab, keys], w[p][:, lo + 2:a + 2], start=first, stop=False)
                    first = False
            if a < b:
                x = a - (t * P - 1)
                for w in (dgh, dgl):
                    pe.matmul(out[:, a - lo:b - lo], g.ident16[:, :], w[p][:, t, x:x + b - a], start=first,
                              stop=False)
                    first = False
            if b < hi:
                for tab, w in ((0, ah), (0, al), (1, ah)):
                    pe.matmul(out[:, b - lo:CH], tabs[:, tab, keys], w[p][:, b + 1:hi + 1], start=first, stop=False)
                    first = False
            if n == 0:
                pe.wait_ge(s_guard, 16 * (u + 1))
            pe.matmul(out[:, :], k3[p][0:PART + 1, keys], q3[p][0:PART + 1, lo:hi], start=False,
                      stop=True).then_inc(s_score, 1)

        def values(pe, q, p, u):
            pe.wait_ge(s_exp, u * STEPS + TC * (q + 1) + 3)
            if q % 3 == 0:
                pe.wait_ge(s_evac, u * NC + q // 3 + 1)
            for i in range(TC):
                t = (TC * q + i) % NT
                ins = pe.matmul(o_bank[VW * i:VW * (i + 1), :], vo[p][:, VW * t:VW * (t + 1)],
                                pt[:, ((GROUPS * p + q) % 2) * TC + i, :], start=(q % 3 == 0), stop=(q % 3 == 2),
                                tile_position=(0, VW * i))
            ins.then_inc(s_pv, 1)

        def turned(pe, k, p, use):
            pe.wait_ge(s_sread, use + 1)
            cols = slice(k * CH, (k + 1) * CH)
            pe.matmul(shared[0][:, :], wp3[p][:, 0:D], q3[p][0:PART, cols], start=True, stop=True)
            pe.matmul(shared[1][:, :], wp3[p][:, D:2 * D], q3[p][0:PART, cols], start=True,
                      stop=True).then_inc(s_shared, 1)

        def diagonal(pe, j, p, use):
            pe.wait_ge(s_sread, use + 1)
            for side in range(2):
                for i in range(3):
                    t = 3 * j + i
                    keys = slice(t * P, (t + 1) * P)
                    for n, (tab, w) in enumerate(((2 * side, ah), (2 * side, al), (2 * side + 1, ah))):
                        ins = pe.matmul(shared[side][:, i * DW:(i + 1) * DW], tabs[:, tab, keys],
                                        w[p][:, t * P + side:t * P + side + DW], start=(n == 0), stop=(n == 2))
            ins.then_inc(s_shared, 1)

        def premax(pe, m, p, v):
            t, k = m // NC, m % NC
            lo, hi = k * CH, (k + 1) * CH
            out = pre[m % 2]
            rows = slice(t * P, (t + 1) * P)
            pe.wait_ge(s_max, v * STEPS + m + 1)
            pieces = []
            a, b = max(lo, min(hi, t * P)), max(lo, min(hi, t * P + P))
            if lo < a:
                pieces.append((lo, a, ah[p][:, t * P + 1:t * P + P + 1], tabs[:, 0, lo:a], P))
            if a < b:
                pieces.append((a, b, dgh[p][:, t, 1:DW], g.ident16[:, :], P))
            if b < hi:
                if b == t * P + P:
                    pieces.append((b, b + 1, ah[p][:, t * P + 2:t * P + P + 1], tabs[:, 2, b:b + 1], P - 1))
                    b += 1
                pieces.append((b, hi, ah[p][:, t * P + 2:t * P + P + 2], tabs[:, 2, b:hi], P))
            pe.matmul(out[:, :], q3[p][0:PART, rows], k3[p][0:PART, lo:hi], start=True, stop=False)
            for i, (x, y, w, r, rows_out) in enumerate(pieces):
                ins = pe.matmul(out[0:rows_out, x - lo:y - lo], w, r, start=False, stop=(i == len(pieces) - 1))
            ins.then_inc(s_pre, 1)

        def turns(eng, body, batch_end):
            with eng.Fori(0, B) as b:
                with eng.Fori(0, NH // HEADS) as hp:
                    for n in range(HEADS):
                        p, head = n % 2, hp * HEADS + n
                        u = b * NH + head
                        body(p=p, u=u, q=1 - p, v=u + 1, loads=b * (NH // 2) + hp * (HEADS // 2) + n // 2 + 1 + p,
                             use=b * SHARED_B + hp * (HEADS * SHARED) + SHARED * (n + 1), head=head,
                             links=b * (NH * LINKS_PREP) + hp * (HEADS * LINKS_PREP) + LINKS_PREP * (n + 1))
                batch_end(b)

        with nc.Block() as block:
            @block.sync
            def _(sp):
                def load(q, v, head):
                    sp.dma_start(k3[q][0:PART, :], io.QK[ds(v, 1), 1].rearrange("o r s -> (o r) s")).then_inc(s_load[q], 16)
                    sp.dma_start(q3[q][0:PART, :], io.QK[ds(v, 1), 0].rearrange("o r s -> (o r) s")).then_inc(s_load[q], 16)
                    sp.dma_start(wp3[q][:, :], io.WP3[ds(head, 1)].rearrange("o r s -> (o r) s")).then_inc(s_load[q], 16)
                    sp.dma_start(vo[q][:, :], io.VS[ds(v, 1)].rearrange("o r s -> (o r) s")).then_inc(s_load[q], 16)

                def guard(q, use):
                    sp.wait_ge(s_sread, use + SHARED + 1)
                    sp.dma_start(q3[q][PART:PART + 1, :], nmh[:, :]).then_inc(s_guard, 16)

                blank_rows = io.XS.rearrange("(u a r) d -> u a (r d)", u=UNITS, a=16)
                sp.wait_ge(s_clear, 2)
                load(0, 0, 0)
                sp.dma_start(io.QK[UNITS], io.QK[0]).then_inc(s_ahead, 16)
                sp.dma_start(io.VS[UNITS], io.VS[0]).then_inc(s_ahead, 16)
                guard(0, 0)
                sp.wait_ge(s_clear, 8)

                def body(p, u, q, v, loads, use, head, links):
                    sp.wait_ge(s_pv, u * GROUPS + 2)
                    load(q, v, head + 1)
                    guard(q, use)
                    sp.dma_start(blank_rows[ds(u, 1)].rearrange("o a n -> (o a) n"),
                                 io.blank[p].rearrange("(a r) d -> a (r d)", a=16)).then_inc(s_blank, 16)

                turns(sp, body, lambda b: sp.wait_ge(s_ahead, 32))
                sp.wait_ge(s_guard, 16 * (UNITS + 1))
                sp.wait_ge(s_blank, 16 * UNITS)

            @block.tensor
            def _(pe):
                pe.sem_inc(s_pv, 2)
                pe.wait_ge(g.s_tables, 16 * 5)

                def step(kind, n, p, u, q, v, loads, use):
                    if kind == "S":
                        scores(pe, n, p, u)
                    elif kind == "PV":
                        values(pe, n, p, u)
                    elif kind == "R":
                        if n == 0:
                            pe.wait_ge(s_load[q], loads * 64)
                        turned(pe, n, q, use + n)
                    elif kind == "X":
                        if n < NC:
                            pe.wait_ge(s_a, v * NC + n + 1)
                        diagonal(pe, n, q, use + 3 + n)
                    elif kind == "PRE":
                        if n % 9 == 0:
                            pe.wait_ge(s_dg, v * 4 + n // 9 + 1)
                        premax(pe, n, q, v)
                    elif kind == "GUARD":
                        pe.wait_ge(s_nm, v + 1)
                        pe.wait_ge(s_sread, use + 8)
                        pe.transpose(shared[0][0:NT, 0:P], nm[:, :], g.ident[:, :]).then_inc(s_shared, 1)

                for kind, n in PREPARE:
                    step(kind, n, None, None, 0, 0, 1, 0)

                def body(p, u, q, v, loads, use, head, links):
                    for kind, n in order:
                        step(kind, n, p, u, q, v, loads, use)

                def batch_end(b):
                    pe.wait_ge(s_evac, (b + 1) * (NH * NC) + 1)
                    pe.wait_ge(s_sread, b * SHARED_B + SHARED * (NH + 1) + 1)
                    for k in range(NC):
                        for what in (1, 0):
                            if k:
                                pe.wait_ge(s_copied, b * (2 * NC) + 2 * k - what)
                            for par in range(2):
                                for hh in range(NH // 2):
                                    ins = pe.matmul(shared[what][VW * hh:VW * (hh + 1), :], pick[:, what, par, :],
                                                    osb[:, 2 * hh + par, k * CH:(k + 1) * CH], start=(par == 0),
                                                    stop=(par == 1), tile_position=(0, VW * hh))
                            ins.then_inc(s_sums if what else s_shared, 1)

                turns(pe, body, batch_end)

            @block.scalar
            def _(act):
                act.sem_inc(s_exp, 3)
                act.sem_inc(s_cxfree, 1)
                act.wait_ge(s_clear, 8)

                def leading(kind, n, q, v):
                    if kind == "RC":
                        act.wait_ge(s_af, v * NC + n + 1)
                        act.activation(ah[q][:, n * CH + 1:(n + 1) * CH + 1], af[:, n, :], ACT.Identity).then_inc(s_ah, 1)
                    elif kind == "XC":
                        act.wait_ge(s_dt, v * 4 + n + 1)
                        act.activation(dgh[q][:, 3 * n:3 * n + 3, :], dt[:, n, :].rearrange("p (t x) -> p t x", t=3),
                                       ACT.Identity).then_inc(s_hi, 1)

                for kind, n in PREPARE:
                    leading(kind, n, 0, 0)

                def body(p, u, q, v, loads, use, head, links):
                    for kind, n in order:
                        leading(kind, n, q, v)
                        if kind == "S":
                            act.wait_ge(s_score, u * STEPS + n + 1)
                            if n % TC == 0:
                                act.wait_ge(s_pv, u * GROUPS + n // TC + 1)
                            act.activation(pt[:, (4 * ((GROUPS * p + n // TC) % 2)) + n % TC, :], score[n % 3][:, :],
                                           ACT.Exp).then_inc(s_exp, 1)

                def batch_end(b):
                    act.wait_ge(s_cxfree, b + 1)
                    for k in range(NC):
                        cols = slice(k * CH, (k + 1) * CH)
                        act.wait_ge(s_sums, b * NC + k + 1)
                        act.activation(sums[:, cols], shared[1][:, :], ACT.Identity).then_inc(s_copied, 1)
                        act.wait_ge(s_shared, b * SHARED_B + SHARED * (NH + 1) + k + 1)
                        act.activation(cx[:, cols], shared[0][:, :], ACT.Identity).then_inc(s_copied, 1)
                    act.wait_ge(s_copied, (b + 1) * (2 * NC))
                    act.sem_inc(s_sread, NC)

                turns(act, body, batch_end)

            @block.vector
            def _(dve):
                for q in range(2):
                    dve.memset(k3[q][32:64, :], 1.0).then_inc(s_clear, 1)
                    dve.memset(q3[q][32:64, :], 1.0).then_inc(s_clear, 1)
                    for w in (ah, al):
                        dve.memset(w[q][:, 0:1], 0.0)
                        dve.memset(w[q][:, S + 1:S + 4], 0.0).then_inc(s_clear, 1)
                dve.sem_inc(s_sread, 1)
                dve.sem_inc(s_max, 2)
                dve.sem_inc(s_evac, 1)
                dve.wait_ge(g.s_tables, 16 * 5)

                def step(ch, kind, n, p, u, q, v, use, head):
                    if kind == "R":
                        cols = slice(n * CH, (n + 1) * CH)
                        dve.wait_ge(s_shared, use + n + 1)
                        dve.scalar_tensor_tensor(ta[:, n, :], shared[0][:, :], g.rb[:, 0, head], rot[:, 0, cols],
                                                 ALU.add, ALU.mult)
                        dve.scalar_tensor_tensor(tb[:, n, :], shared[1][:, :], g.rb[:, 1, head], rot[:, 1, cols],
                                                 ALU.add, ALU.mult).then_inc(s_sread, 1)
                    elif kind == "X":
                        dve.wait_ge(s_shared, use + 3 + n + 1)
                        w = dt[:, n, :].rearrange("p (t x) -> p t x", t=3)
                        ch.add(dve.tensor_tensor(w, shared[0][:, 0:3 * DW].rearrange("p (t x) -> p t x", t=3),
                                                 mask1[:, :, :], ALU.mult))
                        ch.settle_apart()
                        dve.copy_predicated(w, mask2[:, :, :], shared[1][:, 0:3 * DW].rearrange(
                            "p (t x) -> p t x", t=3)).then_inc(s_sread, 1)
                        dve.wait_ge(s_sread, use + 3 + n + 2)
                        dve.sem_inc(s_dt, 1)
                    elif kind == "PRE":
                        dve.wait_ge(s_pre, v * STEPS + n + 1)
                        dve.tensor_reduce(part_max[:, n:n + 1], pre[n % 2][:, :], AX.X, ALU.max).then_inc(s_max, 1)
                    elif kind == "NM":
                        dve.wait_ge(s_max, v * STEPS + STEPS + 2)
                        dve.tensor_reduce(nm[:, :], part_max[:, :].rearrange("p (t k) -> p t k", k=NC), AX.X,
                                          ALU.max, negate=True).then_inc(s_nm, 1)
                    elif kind == "GUARD":
                        dve.wait_ge(s_shared, use + 8)
                        dve.tensor_copy(nmh[:, :], shared[0][0:NT, 0:P]).then_inc(s_sread, 1)
                    elif kind == "EV":
                        k = n
                        dve.wait_ge(s_pv, u * GROUPS + 3 * k + 3 + 2)
                        dve.tensor_copy(osb[:, ds(head[1], 1), k * CH:(k + 1) * CH].rearrange("p o s -> p (o s)"),
                                        o_bank[:, :]).then_inc(s_evac, 1)

                ch = Chain(dve, s_vchain)
                for kind, n in PREPARE:
                    step(ch, kind, n, None, None, 0, 0, 0, slice(0, 1))
                assert ch.n == LINKS_PREP

                def body(p, u, q, v, loads, use, head, links):
                    ch = Chain(dve, s_vchain, links)
                    for kind, n in order:
                        h = (None, head) if kind == "EV" else ds(head + 1, 1)
                        step(ch, kind, n, p, u, q, v, use, h)

                def batch_end(b):
                    for k in range(NC):
                        cols = slice(k * CH, (k + 1) * CH)
                        dve.wait_ge(s_copied, b * (2 * NC) + 2 * k + 2)
                        dve.reciprocal(sums[:, cols], sums[:, cols]).then_inc(s_cx, 1)
                        dve.wait_ge(s_cx, b * (2 * NC) + 2 * k + 1)
                        dve.tensor_tensor(cx[:, cols], cx[:, cols], sums[:, cols], ALU.mult).then_inc(s_cx, 1)

                turns(dve, body, batch_end)

            @block.gpsimd
            def _(pool):
                def step(kind, n, q, v, use):
                    if kind == "R":
                        pool.wait_ge(s_sread, use + n + 2)
                        pool.tensor_tensor(af[:, n, :], ta[:, n, :], tb[:, n, :], ALU.add).then_inc(s_af, 1)
                    elif kind == "RC":
                        cols = slice(n * CH + 1, (n + 1) * CH + 1)
                        pool.wait_ge(s_ah, v * NC + n + 1)
                        pool.tensor_tensor(al[q][:, cols], af[:, n, :], ah[q][:, cols], ALU.subtract).then_inc(s_a, 1)
                    elif kind == "XC":
                        pool.wait_ge(s_hi, v * 4 + n + 1)
                        pool.tensor_tensor(dgl[q][:, 3 * n:3 * n + 3, :], dt[:, n, :].rearrange("p (t x) -> p t x", t=3),
                                           dgh[q][:, 3 * n:3 * n + 3, :], ALU.subtract).then_inc(s_dg, 1)

                pool.wait_ge(s_clear, 8)
                for kind, n in PREPARE:
                    step(kind, n, 0, 0, 0)

                def body(p, u, q, v, loads, use, head, links):
                    for kind, n in order:
                        step(kind, n, q, v, use)

                def batch_end(b):
                    pool.wait_ge(s_cx, (b + 1) * (2 * NC))
                    pool.sem_inc(s_apart, 1)
                    pool.dma_start(io.CT[ds(b, 1)].rearrange("o p s -> (o p) s"), cx[:, :]).then_inc(s_cxout, 16)
                    pool.wait_ge(s_cxout, 16 * (b + 1))
                    pool.sem_inc(s_cxfree, 1)

                turns(pool, body, batch_end)
                pool.wait_ge(s_apart, B)



def project_block(nc, ctx, io, g):
    with ExitStack() as c:
        def sb(name, shape, dt=F32):
            return c.enter_context(nc.sbuf_tensor(name, shape, dt))

        def bank(name):
            return c.enter_context(nc.psum_tensor(name, [P, CH], F32))

        def sem(name):
            return ctx.enter_context(nc.semaphore("pr_" + name))

        ct = [sb(f"ct{k}", [P, CH]) for k in range(NC)]
        h0 = [sb(f"h0_{k}", [P, TC, D]) for k in range(NC)]
        h1 = [sb(f"h1_{k}", [P, TC, D]) for k in range(NC)]
        xn = [sb(f"xn_{k}", [P, TC, D]) for k in range(NC)]
        xnt = [sb(f"xnt{k}", [P, CH]) for k in range(NC)]
        bob, brb, wr = sb("bob", [P, D]), sb("brb", [P, NE]), sb("wr", [P, NE])
        st, mv = ([sb(f"{n}{k}", sh) for k in range(NC)] for n, sh in (("st2_", [P, TC, 6]), ("mv2_", [P, TC, 2])))
        var, std, rstd = ([sb(f"{n}2_{k}", [P, TC]) for k in range(NC)] for n in ("var", "std", "rstd"))
        b_o, b_t = ([bank(f"{n}{i}") for i in range(3)] for n in ("b_o", "b_t"))
        b_l = bank("b_l")
        s_const, s_o, s_hb, s_h1, s_var, s_std, s_xn, s_xt, s_xts, s_lg, s_lgr, s_chain = (
            sem(n) for n in ("const", "o_ready", "h_bias", "h1_done", "var", "std", "xn_done", "xt_ready",
                             "xt_copied", "logit_ready", "logit_read", "chain"))
        s_in, s_out = ([sem(f"{n}{k}") for k in range(NC)] for n in ("in", "stored"))
        links = 4

        def all_turns(eng, turn):
            def fixed(r):
                turn(r, r % NC, r // NC, lambda n: 0 <= r + n < NR)
            for r in range(-2, NC):
                fixed(r)
            with eng.Fori(0, B - 3) as i:
                for k in range(NC):
                    turn(NC * i + NC + k, k, i + 1, lambda n: True)
            for r in range(NR - 2 * NC, NR + 1):
                fixed(r)

        with nc.Block() as block:
            @block.sync
            def _(sp):
                sp.dma_start(bob[:, :], io.bo.partition_broadcast(P)).then_inc(s_const, 16)
                sp.dma_start(brb[:, :], io.br.partition_broadcast(P)).then_inc(s_const, 16)
                sp.dma_start(wr[:, :], io.Wr).then_inc(s_const, 16)
                contexts = io.CT.rearrange("b p (k s) -> b k p s", k=NC)
                tokens = io.H0.rearrange("b p (k t) d -> b k p t d", k=NC)

                def load(b, k):
                    sp.dma_start(ct[k][:, :], contexts[ds(b, 1), k].rearrange("o p s -> (o p) s")).then_inc(s_in[k], 16)
                    sp.dma_start(h0[k][:, :, :], tokens[ds(b, 1), k].rearrange(
                        "o p t d -> (o p) t d")).then_inc(s_in[k], 16)

                def turn(r, k, nth, has):
                    if has(NC + 1) and has(1):
                        sp.wait_ge(s_h1, r + 2)
                        load(nth + 1 + (k == NC - 1), (k + 1) % NC)
                    if has(0):
                        sp.wait_ge(s_xn, r + 1)
                        sp.dma_start(io.H1[ds(r, 1)].rearrange("o p n -> (o p) n"),
                                     h1[k][:, :, :].rearrange("p t d -> p (t d)")).then_inc(s_out[k], 16)
                        sp.dma_start(io.XN[ds(r, 1)].rearrange("o p n -> (o p) n"),
                                     xn[k][:, :, :].rearrange("p t d -> p (t d)")).then_inc(s_out[k], 16)

                for k in range(NC):
                    sp.sem_inc(s_out[k], 32)
                    load(0, k)
                all_turns(sp, turn)
                for k in range(NC):
                    sp.wait_ge(s_out[k], 32 * (B + 1))

            @block.gpsimd
            def _(pool):
                pool.wait_ge(s_const, 48)
                with pool.Fori(0, B) as b:
                    for k in range(NC):
                        pool.wait_ge(s_in[k], 32 * (b + 1))
                        pool.tensor_tensor(h0[k][:, :, :], h0[k][:, :, :],
                                           bob[:, :].unsqueeze(1).to_broadcast([P, TC, D]), ALU.add).then_inc(s_hb, 1)

            @block.tensor
            def _(pe):
                pe.wait_ge(s_const, 48)

                def turn(r, k, nth, has):
                    before, ahead = (k - 1) % NC, (k + 2) % NC
                    if has(2):
                        pe.wait_ge(s_in[ahead], 32 * (nth + 1 + (k > 0)))
                        if has(-1):
                            pe.wait_ge(s_h1, r)
                        for t in range(TC):
                            ins = pe.matmul(b_o[ahead][:, t * P:(t + 1) * P], ct[ahead][:, t * P:(t + 1) * P],
                                            g.wt[:, 3, :], start=True, stop=True)
                        ins.then_inc(s_o, 1)
                    if has(-1):
                        pe.wait_ge(s_xts, r)
                        pe.wait_ge(s_lgr, r)
                        for t in range(TC):
                            ins = pe.matmul(b_l[:, t * NE:(t + 1) * NE], xnt[before][:, t * P:(t + 1) * P], wr[:, :],
                                            start=True, stop=True)
                        ins.then_inc(s_lg, 1)
                    if has(0):
                        pe.wait_ge(s_xn, r + 1)
                        if has(-NC):
                            pe.wait_ge(s_xts, r - NC + 1)
                        for t in range(TC):
                            ins = pe.transpose(b_t[k][:, t * P:(t + 1) * P], xn[k][:, t, :], g.ident[:, :])
                        ins.then_inc(s_xt, 1)

                all_turns(pe, turn)

            @block.scalar
            def _(act):
                def turn(r, k, nth, has):
                    after = (k + 1) % NC
                    if has(1):
                        act.wait_ge(s_var, r + 2)
                        act.activation(std[after][:, :], var[after][:, :], ACT.Sqrt).then_inc(s_std, 1)
                    if has(0):
                        act.wait_ge(s_xt, r + 1)
                        if has(-NC):
                            act.wait_ge(s_lg, r - NC + 1)
                        act.activation(xnt[k][:, :], b_t[k][:, :], ACT.Identity).then_inc(s_xts, 1)

                all_turns(act, turn)

            @block.vector
            def _(dve):
                dve.sem_inc(s_lgr, 1)
                dve.wait_ge(s_const, 48)

                def turn(r, k, nth, has):
                    after = (k + 1) % NC
                    ch = Chain(dve, s_chain, (r + 2) * links)

                    def step(ins):
                        ch.add(ins)
                        ch.settle()
                    if has(1):
                        j = after
                        dve.wait_ge(s_hb, r + 2)
                        dve.wait_ge(s_o, r + 2)
                        dve.wait_ge(s_out[j], 32 * (nth + 1 + (k == NC - 1)))
                        dve.tensor_tensor(h1[j][:, :, :], b_o[j][:, :].rearrange("p (t d) -> p t d", t=TC),
                                          h0[j][:, :, :], ALU.add).then_inc(s_h1, 1)
                        dve.wait_ge(s_h1, r + 2)
                        for t in range(TC):
                            ins = dve.bn_stats(st[j][:, t, :], h1[j][:, t, :])
                        ch.add(ins)
                        ch.settle_apart()
                        for t in range(TC):
                            ins = dve.bn_aggr(mv[j][:, t, :], st[j][:, t, :])
                        step(ins)
                        dve.tensor_scalar(var[j][:, :], mv[j][:, :, 1], EPS, None, ALU.add).then_inc(s_var, 1)
                    else:
                        dve.sem_inc(s_chain, 3)
                        ch.n = 3
                    if has(0):
                        dve.wait_ge(s_std, r + 1)
                        step(dve.reciprocal(rstd[k][:, :], std[k][:, :]))
                        for t in range(TC):
                            ins = dve.tensor_scalar(xn[k][:, t, :], h1[k][:, t, :], mv[k][:, t, 0:1],
                                                    rstd[k][:, t:t + 1], ALU.subtract, ALU.mult)
                        ins.then_inc(s_xn, 1)
                    else:
                        dve.sem_inc(s_chain, 1)
                        ch.n += 1
                    if has(-1):
                        dve.wait_ge(s_lg, r)
                        dve.tensor_tensor(g.lg[:, ds((r - 1) * TC, TC), :],
                                          b_l[:, 0:TC * NE].rearrange("p (t e) -> p t e", t=TC),
                                          brb[:, :].unsqueeze(1).to_broadcast([P, TC, NE]),
                                          ALU.add).then_inc(s_lgr, 1)
                    assert ch.n == links

                all_turns(dve, turn)


def route_block(nc, ctx, io, g):
    g.wh, g.wl = (ctx.enter_context(nc.sbuf_tensor(n, [P, 2, NE, HID], F16)) for n in ("w12_hi", "w12_lo"))
    g.w3 = ctx.enter_context(nc.sbuf_tensor("w3", [P, NE, TC, D], F32))
    g.s_w = ctx.enter_context(nc.semaphore("expert_weights"))
    with ExitStack() as c:
        def sb(name, shape, dt=F32):
            return c.enter_context(nc.sbuf_tensor(name, shape, dt))

        def sem(name):
            return ctx.enter_context(nc.semaphore("ro_" + name))

        w12 = sb("w12", [P, 2, NE, HID])
        s_w12, s_whi = sem("w12_in"), sem("w12_hi_done")
        rank, index, before = sb("rank", [P, NE]), sb("index", [P, SLOTS]), sb("before", [P, NE, NE])
        tri, ones, last = sb("tri", [P, P]), sb("ones", [P, P]), sb("last", [P, 1])
        l2, key, oh0, oh1 = (sb(n, [P, NG, NE]) for n in ("l2", "key", "oh0", "oh1"))
        sa, sbb = sb("scan_a", [P, NG, NE]), sb("scan_b", [P, NG, NE])
        v0, v1, r0, r1, gap, ex, den, s0, s1, e0, e1, imax, posf = (
            sb(n, [P, NG]) for n in ("v0", "v1", "r0", "r1", "gap", "ex", "den", "s0", "s1", "e0", "e1", "imax",
                                     "posf"))
        cnt = sb("cnt", [P, 2, NE])
        full = sb("fullm", [P, 2, NE])
        drop, kept = sb("drop", [P, 2]), sb("kept", [P, 2])
        dsel = sb("dsel", [P, 2, NE])
        tot, nt, start, end, base = (sb(n, [P, NE]) for n in ("tot", "ntile", "start", "end", "base"))
        cmp_t, cmp_s, bsel = sb("cmp_t", [P, NE, NG]), sb("cmp_s", [P, SLOTS, NE]), sb("bsel", [P, NE, NE])
        tef = sb("tef", [P, SLOTS])
        cxl = sb("cxl", [P, 2])
        h1l, xnl = sb("h1l", [P, D]), sb("xnl", [P, D])
        token, meta = sb("token", [P, NG]), sb("meta", [P, NG, 2])
        rows, idx = [sb(f"rows{i}", [P, TC, ROW]) for i in range(RING)], [sb(f"idx{i}", [P, TC], I32) for i in range(RING)]
        bc, bp = (c.enter_context(nc.psum_tensor(n, [P, CH], F32)) for n in ("bc", "bp"))
        s_in, s_v, s_cnt, s_gap, s_ex, s_tp, s_pre, s_fix, s_fixed, s_pos = (
            sem(n) for n in ("in", "chain", "counts", "gap", "exp", "per_part", "prefix", "fix", "fixed", "pos"))
        s_idx, s_apart = sem("idx"), sem("apart")
        s_row, s_sc = ([sem(f"{n}{i}") for i in range(RING)] for n in ("row", "scattered"))
        TAIL = NR - 1
        with nc.Block() as block:
            @block.sync
            def _(sp):
                for dst, src in ((rank[:, :], io.rank), (index[:, :], io.index), (before[:, :, :], io.before),
                                 (tri[:, :], io.tri), (ones[:, :], io.ones), (last[:, :], io.last), (token[:, :], io.token),
                                 (h1l[:, :], io.H1[TAIL, :, (TC - 1) * D:TC * D]),
                                 (xnl[:, :], io.XN[TAIL, :, (TC - 1) * D:TC * D])):
                    sp.dma_start(dst, src).then_inc(s_in, 16)

                def load(r, p):
                    for n, part in enumerate((io.XN, io.H1)):
                        sp.dma_start(rows[p][:, :, n * D:(n + 1) * D], part[ds(r, 1)].rearrange(
                            "o p (t d) -> (o p) t d", t=TC)).then_inc(s_row[p], 16)

                for p in range(RING):
                    load(p, p)
                sp.dma_start(w12[:, 0, :, :], io.W1.rearrange("e k h -> k e h")).then_inc(s_w12, 16)
                sp.dma_start(w12[:, 1, :, :], io.W2.rearrange("e k h -> k e h")).then_inc(s_w12, 16)
                sp.dma_start(g.w3[:, :, :, :], io.W3.rearrange("e (c k) d -> k e c d", k=P)).then_inc(g.s_w, 16)
                sp.wait_ge(s_fix, 1)
                sp.dma_start(io.H1[TAIL, :, (TC - 1) * D:TC * D], h1l[:, :]).then_inc(s_fixed, 16)
                sp.wait_ge(s_fixed, 16)
                with sp.Fori(0, NR // RING - 1) as i:
                    for p in range(RING):
                        sp.wait_ge(s_sc[p], 16 * TC * (i + 1))
                        load(RING * (i + 1) + p, p)

            @block.scalar
            def _(act):
                act.wait_ge(s_gap, 1)
                act.activation(ex[:, :], gap[:, :], ACT.Exp).then_inc(s_ex, 1)
                act.wait_ge(s_w12, 32)
                act.activation(g.wh[:, :, :, :], w12[:, :, :, :], ACT.Identity, scale=WSCALE).then_inc(s_whi, 1)

            @block.tensor
            def _(pe):
                pe.wait_ge(s_in, 16 * 9)
                pe.wait_ge(s_cnt, 1)
                pe.matmul(bc[:, 0:2 * NE], ones[:, :], cnt[:, :, :].rearrange("p a e -> p (a e)"), start=True,
                          stop=True).then_inc(s_pre, 1)
                pe.wait_ge(s_tp, 1)
                pe.matmul(bp[:, 0:NE], tri[:, :], sa[:, NG - 1, :], start=True, stop=True)
                pe.matmul(bp[:, NE:2 * NE], ones[:, :], sa[:, NG - 1, :], start=True, stop=True).then_inc(s_pre, 1)

            @block.vector
            def _(dve):
                ch = Chain(dve, s_v)

                def do(ins):
                    ch.add(ins)
                    ch.settle()

                def over_e(x):
                    return x.unsqueeze(2).to_broadcast([P, NG, NE])

                def over_g(x):
                    return x.unsqueeze(1).to_broadcast([P, NG, NE])

                dve.wait_ge(s_in, 16 * 9)
                for lg, v, r, oh in ((g.lg, v0, r0, oh0), (l2, v1, r1, oh1)):
                    if lg is l2:
                        do(dve.scalar_tensor_tensor(l2[:, :, :], oh0[:, :, :], -3e38, g.lg[:, :, :], ALU.mult, ALU.add))
                    do(dve.tensor_reduce(v[:, :], lg[:, :, :], AX.X, ALU.max))
                    do(dve.tensor_tensor(key[:, :, :], lg[:, :, :], over_e(v[:, :]), ALU.is_equal))
                    do(dve.tensor_tensor(oh[:, :, :], key[:, :, :], over_g(rank[:, :]), ALU.mult))
                    do(dve.tensor_reduce(r[:, :], oh[:, :, :], AX.X, ALU.max))
                    do(dve.tensor_tensor(oh[:, :, :], oh[:, :, :], over_e(r[:, :]), ALU.is_equal))
                dve.tensor_tensor(gap[:, :], v1[:, :], v0[:, :], ALU.subtract).then_inc(s_gap, 1)
                ch.add(dve.tensor_reduce(cnt[:, 0, :], oh0[:, :, :].rearrange("p g e -> p e g"), AX.X, ALU.add))
                ch.add(dve.tensor_tensor(key[:, :, :], oh0[:, :, :], oh1[:, :, :], ALU.add))
                ch.settle()
                dve.tensor_reduce(cnt[:, 1, :], key[:, :, :].rearrange("p g e -> p e g"), AX.X, ALU.add).then_inc(s_cnt, 1)
                dve.wait_ge(s_pre, 1)
                do(dve.tensor_scalar(full[:, :, :], bc[:, 0:2 * NE].rearrange("p (a e) -> p a e", a=2),
                                     float(TOKENS), last[:, 0:1], ALU.is_ge, ALU.mult))
                ch.add(dve.tensor_tensor(dsel[:, 0, :], full[:, 0, :], oh0[:, NG - 1, :], ALU.mult))
                ch.add(dve.tensor_tensor(dsel[:, 1, :], full[:, 1, :], oh1[:, NG - 1, :], ALU.mult))
                ch.settle()
                do(dve.tensor_reduce(drop[:, :], dsel[:, :, :], AX.X, ALU.add))
                do(dve.tensor_scalar(kept[:, :], drop[:, :], -1.0, 1.0, ALU.mult, ALU.add))
                ch.add(dve.tensor_scalar(e0[:, :], r0[:, :], -1.0, float(NE), ALU.mult, ALU.add))
                ch.add(dve.tensor_scalar(e1[:, :], r1[:, :], -1.0, float(NE), ALU.mult, ALU.add))
                ch.settle()
                tail = slice(NG - 1, NG)
                ch.add(dve.tensor_tensor(e0[:, tail], e0[:, tail], kept[:, 0:1], ALU.mult))
                ch.add(dve.tensor_tensor(e1[:, tail], e1[:, tail], kept[:, 1:2], ALU.mult))
                ch.settle()
                do(dve.tensor_tensor(imax[:, :], e0[:, :], e1[:, :], ALU.max))
                dve.wait_ge(s_ex, 1)
                do(dve.tensor_scalar(den[:, :], ex[:, :], 1.0, None, ALU.add))
                do(dve.reciprocal(s0[:, :], den[:, :]))
                do(dve.tensor_tensor(s1[:, :], s0[:, :], ex[:, :], ALU.mult))
                ch.add(dve.tensor_tensor(cxl[:, 0:1], s0[:, tail], drop[:, 0:1], ALU.mult))
                ch.add(dve.tensor_tensor(cxl[:, 1:2], s1[:, tail], drop[:, 1:2], ALU.mult))
                ch.settle()
                do(dve.tensor_tensor(cxl[:, 0:1], cxl[:, 0:1], cxl[:, 1:2], ALU.add))
                dve.scalar_tensor_tensor(h1l[:, :], xnl[:, :], cxl[:, 0:1], h1l[:, :], ALU.mult,
                                         ALU.add).then_inc(s_fix, 1)
                ch.add(dve.tensor_tensor(s0[:, tail], s0[:, tail], kept[:, 0:1], ALU.mult))
                ch.add(dve.tensor_tensor(s1[:, tail], s1[:, tail], kept[:, 1:2], ALU.mult))
                ch.settle()
                ch.add(dve.tensor_tensor(meta[:, :, 0], s0[:, :], s1[:, :], ALU.add))
                ch.add(dve.tensor_copy(meta[:, :, 1], token[:, :]))
                ch.settle()
                do(dve.tensor_tensor(oh0[:, :, :], over_e(imax[:, :]), over_g(index[:, 0:NE]), ALU.is_equal))
                src, dst, step = oh0, sbb, 1
                while step < NG:
                    ch.add(dve.tensor_copy(dst[:, 0:step, :], src[:, 0:step, :]))
                    ch.add(dve.tensor_tensor(dst[:, step:NG, :], src[:, step:NG, :], src[:, 0:NG - step, :], ALU.add))
                    ch.settle()
                    src, dst, step = dst, (sa if dst is sbb else sbb), 2 * step
                assert src is sbb
                do(dve.tensor_copy(sa[:, :, :], sbb[:, :, :]))
                dve.sem_inc(s_tp, 1)
                dve.wait_ge(s_pre, 2)
                do(dve.tensor_copy(tot[:, :], bp[:, NE:2 * NE]))
                do(dve.tensor_scalar(posf[:, :], index[:, 0:NG], float(P), None, ALU.mult))
                do(dve.tensor_tensor(cmp_t[:, :, :], tot[:, :].unsqueeze(2).to_broadcast([P, NE, NG]),
                                     posf[:, :].unsqueeze(1).to_broadcast([P, NE, NG]), ALU.is_gt))
                do(dve.tensor_reduce(nt[:, :], cmp_t[:, :, :], AX.X, ALU.add))
                do(dve.tensor_tensor(bsel[:, :, :], before[:, :, :], nt[:, :].unsqueeze(1).to_broadcast([P, NE, NE]),
                                     ALU.mult))
                do(dve.tensor_reduce(start[:, :], bsel[:, :, :], AX.X, ALU.add))
                do(dve.tensor_tensor(end[:, :], start[:, :], nt[:, :], ALU.add))
                do(dve.tensor_scalar(base[:, :], start[:, :], float(P), -1.0, ALU.mult, ALU.add))
                do(dve.tensor_tensor(base[:, :], bp[:, 0:NE], base[:, :], ALU.add))
                do(dve.tensor_tensor(key[:, :, :], sa[:, :, :], over_g(base[:, :]), ALU.add))
                do(dve.tensor_tensor(key[:, :, :], key[:, :, :], oh0[:, :, :], ALU.mult))
                do(dve.tensor_reduce(posf[:, :], key[:, :, :], AX.X, ALU.add))
                do(dve.tensor_copy(g.pos[:, :], posf[:, :]))
                dve.sem_inc(s_pos, 1)
                do(dve.tensor_tensor(cmp_s[:, :, :], index[:, :].unsqueeze(2).to_broadcast([P, SLOTS, NE]),
                                     end[:, :].unsqueeze(1).to_broadcast([P, SLOTS, NE]), ALU.is_ge))
                do(dve.tensor_reduce(tef[:, :], cmp_s[:, :, :], AX.X, ALU.add))
                do(dve.tensor_scalar(tef[:, :], tef[:, :], float(NE - 1), None, ALU.min))
                do(dve.tensor_copy(g.te[:, :], tef[:, :]))
                dve.wait_ge(s_whi, 1)
                do(dve.scalar_tensor_tensor(g.wl[:, :, :, :], w12[:, :, :, :], WSCALE, g.wh[:, :, :, :], ALU.mult,
                                            ALU.subtract))

            @block.gpsimd
            def _(pool):
                pool.wait_ge(s_pos, 1)
                with pool.Fori(0, NR // RING) as i:
                    for p in range(RING):
                        r = RING * i + p
                        pool.wait_ge(s_row[p], 32 * (i + 1))
                        pool.sem_inc(s_apart, 1)
                        pool.tensor_copy(idx[p][:, :], g.pos[:, ds(r * TC, TC)]).then_inc(s_idx, 1)
                        pool.tensor_copy(rows[p][:, :, 2 * D:ROW], meta[:, ds(r * TC, TC), :]).then_inc(s_idx, 1)
                        pool.wait_ge(s_idx, 2 * r + 2)
                        pool.sem_inc(s_apart, 1)
                        for t in range(TC):
                            pool.indirect_dma_start(io.XS, bass.IndirectOffsetOnAxis(idx[p][:, t:t + 1], 0),
                                                    rows[p][:, t, :], None).then_inc(s_sc[p], 16)
                pool.wait_ge(s_apart, 2 * NR)
                for p in range(RING):
                    pool.wait_ge(s_sc[p], 16 * NR // RING * TC)


def expert_block(nc, ctx, io, g):
    with ExitStack() as c:
        def sb(name, shape, dt=F32):
            return c.enter_context(nc.sbuf_tensor(name, shape, dt))

        def bank(name):
            return c.enter_context(nc.psum_tensor(name, [P, CH], F32))

        def sem(name):
            return ctx.enter_context(nc.semaphore("ex_" + name))

        rows = [sb(f"ex_rows{i}", [P, ROW]) for i in range(UNROLL)]
        xth, xtl = ([sb(f"ex_{n}{i}", [P, P], F16) for i in range(2)] for n in ("xth", "xtl"))
        h1s, pr, gl = ([sb(f"ex_{n}{i}", [P, HID]) for i in range(2)] for n in ("h1s", "pr", "gl"))
        y = [sb(f"ex_y{i}", [P, D]) for i in range(2)]
        place = [sb(f"ex_place{i}", [P, 1], I32) for i in range(2)]
        b_x, b_y = bank("b_x"), bank("b_y")
        b1, b2 = ([bank(f"{n}{i}") for i in range(2)] for n in ("b1_", "b2_"))
        s_xt, s_xth, s_xts, s_h, s_h1, s_pr, s_gl, s_y, s_ys, s_place, s_apart, s_final = (
            sem(n) for n in ("xt_ready", "xt_hi", "xt_lo", "h_ready", "h1_copied", "product", "gelu", "y_ready",
                             "y_done", "place", "apart", "final"))
        s_x, s_out = [sem(f"rows{i}_in") for i in range(UNROLL)], [sem("y0_stored"), sem("y1_stored")]

        def half(i, m):
            return m % 2, UNROLL // 2 * i + m // 2

        def quarter(i, m):
            return m % UNROLL, i + m // UNROLL

        start = UNROLL
        loops = (SLOTS - start - UNROLL + 1) // UNROLL
        rest = start + UNROLL * loops

        def all_turns(eng, turn, experts=None):
            def several(s, count, turn_of):
                e = experts(s - 1, count + 1) if experts else [None] * (count + 1)
                for n in range(count):
                    turn_of(n, e[n:n + 2])

            def fixed(s, e):
                turn(0, s, lambda k: 0 <= s + k < SLOTS, e)

            fixed(-1, None)
            fixed(0, [None] + (experts(0, 1) if experts else []))
            several(1, start - 1, lambda n, e: fixed(1 + n, e))
            with eng.Fori(0, loops) as i:
                several(UNROLL * i + start, UNROLL, lambda n, e: turn(i, start + n, lambda k: True, e))
            several(rest, SLOTS - rest, lambda n, e: fixed(rest + n, e))
            fixed(SLOTS, experts(SLOTS - 1, 1) if experts else None)

        with nc.Block() as block:
            @block.sync
            def _(sp):
                xs = io.XS.rearrange("(s p) d -> s p d", p=P)

                def load(i, m):
                    n, _ = quarter(i, m)
                    sp.dma_start(rows[n][:, :], xs[ds(UNROLL * i + m, 1)].rearrange("o p d -> (o p) d")).then_inc(
                        s_x[n], 16)

                def turn(i, m, has, e):
                    s = UNROLL * i + m
                    if has(UNROLL - 1):
                        if has(-1):
                            sp.wait_ge(s_place, s)
                        load(i, m + UNROLL - 1)

                for m in range(UNROLL - 2):
                    load(0, m)
                all_turns(sp, turn)
                sp.wait_ge(s_final, 1)
                copies = TOKENS // B
                out = io.out.rearrange("b s d -> (b s) d")
                for b in range(B):
                    sp.dma_start(out[b * copies:(b + 1) * copies, :],
                                 io.OUT[b * copies:(b + 1) * copies, :]).then_inc(s_final, 16)
                sp.wait_ge(s_final, 16 * B + 1)

            @block.gpsimd
            def _(pool):
                def turn(i, m, has, e):
                    s = UNROLL * i + m
                    if has(-1):
                        n, _ = quarter(i, m - 1)
                        p, _ = half(i, m - 1)
                        pool.wait_ge(s_ys, s + 1)
                        pool.sem_inc(s_apart, 1)
                        pool.tensor_copy(place[p][:, :], rows[n][:, 2 * D + 1:ROW]).then_inc(s_place, 1)
                        pool.wait_ge(s_place, s)
                        pool.sem_inc(s_apart, 1)
                        pool.indirect_dma_start(io.OUT, bass.IndirectOffsetOnAxis(place[p][:, 0:1], 0),
                                                y[p][:, :], None).then_inc(s_out[p], 16)

                all_turns(pool, turn)
                pool.wait_ge(s_apart, 2 * SLOTS)
                for p in range(2):
                    pool.wait_ge(s_out[p], 16 * (SLOTS // 2))
                pool.sem_inc(s_final, 1)

            @block.tensor
            def _(pe):
                pe.wait_ge(g.s_w, 16)

                def turn(i, m, has, e):
                    s = UNROLL * i + m
                    p = m % 2
                    if has(1):
                        n, before = quarter(i, m + 1)
                        pe.wait_ge(s_x[n], 16 * (before + 1))
                        pe.wait_ge(s_xts, s + 2)
                        pe.transpose(b_x[:, 0:P], rows[n][:, 0:D], g.ident[:, :]).then_inc(s_xt, 1)
                    if has(0):
                        pe.wait_ge(s_xts, s + 2)
                        pe.wait_ge(s_pr, s + 1)
                        for j, out in enumerate((b1[p], b2[p])):
                            for q in range(TC):
                                for n, (w, x) in enumerate(((g.wh, xth), (g.wh, xtl), (g.wl, xth))):
                                    ins = pe.matmul(out[:, q * P:(q + 1) * P],
                                                    w[:, j, ds(e[1], 1), q * P:(q + 1) * P].rearrange("p o h -> p (o h)"),
                                                    x[p][:, :], start=(n == 0), stop=(n == 2))
                        ins.then_inc(s_h, 1)
                    if has(-1):
                        pe.wait_ge(s_gl, s)
                        pe.wait_ge(s_ys, s)
                        for q in range(TC):
                            ins = pe.matmul(b_y[:, 0:D], gl[1 - p][:, q * P:(q + 1) * P],
                                            g.w3[:, ds(e[0], 1), q, :].rearrange("p o d -> p (o d)"), start=(q == 0),
                                            stop=(q == TC - 1))
                        ins.then_inc(s_y, 1)

                registers = [pe.alloc_register(f"expert{n}") for n in range(2 * UNROLL + 1)]

                def experts(s, count):
                    pe.load(registers[:count], g.te[0:1, ds(s, count)])
                    return [pe.snap(r, min_val=0, max_val=NE - 1) for r in registers[:count]]

                all_turns(pe, turn, experts)

            @block.scalar
            def _(act):
                def turn(i, m, has, e):
                    s = UNROLL * i + m
                    p = m % 2
                    if has(1):
                        act.wait_ge(s_xt, s + 2)
                        if has(-1):
                            act.wait_ge(s_h, s)
                        act.activation(xth[1 - p][:, :], b_x[:, 0:P], ACT.Identity).then_inc(s_xth, 1)
                    if has(-1):
                        act.wait_ge(s_pr, s + 2)
                        act.activation(gl[1 - p][:, :], pr[1 - p][:, :], ACT.Gelu).then_inc(s_gl, 1)
                    if has(0):
                        act.wait_ge(s_h, s + 1)
                        act.activation(h1s[p][:, :], b1[p][:, :], ACT.Identity,
                                       scale=WSCALE ** -2).then_inc(s_h1, 1)

                all_turns(act, turn)

            @block.vector
            def _(dve):
                dve.sem_inc(s_pr, 2)
                dve.sem_inc(s_ys, 1)
                dve.sem_inc(s_xts, 1)

                def turn(i, m, has, e):
                    s = UNROLL * i + m
                    p = m % 2
                    if has(1):
                        dve.wait_ge(s_xth, s + 2)
                        dve.tensor_tensor(xtl[1 - p][:, :], b_x[:, 0:P], xth[1 - p][:, :],
                                          ALU.subtract).then_inc(s_xts, 1)
                    if has(0):
                        dve.wait_ge(s_h1, s + 1)
                        dve.tensor_tensor(pr[p][:, :], b2[p][:, :], h1s[p][:, :], ALU.mult).then_inc(s_pr, 1)
                    if has(-1):
                        n, _ = quarter(i, m - 1)
                        _, before = half(i, m - 1)
                        dve.wait_ge(s_y, s)
                        if m > 2:
                            dve.wait_ge(s_out[1 - p], 16 * before)
                        dve.scalar_tensor_tensor(y[1 - p][:, :], b_y[:, 0:D], rows[n][:, 2 * D:2 * D + 1],
                                                 rows[n][:, D:2 * D], ALU.mult, ALU.add).then_inc(s_ys, 1)

                all_turns(dve, turn)


STAGES = (setup_block, embed_block, attend_block, project_block, route_block, expert_block)


def program(nc, io):
    def dram(name, shape, dt=F32):
        return nc.dram_tensor(name, shape, dt, kind="Internal").ap()

    io.H0 = dram("h0_rows", (B, P, NT, D))
    io.QK = dram("qk_parts", (UNITS + 1, 2, PART, S), F16)
    io.VS = dram("v_rows", (UNITS + 1, P, NT * VW))
    io.WP3 = dram("wpos_parts", (NH + 1, PART, 2 * D), F16)
    io.CT = dram("context", (B, P, S))
    io.H1 = dram("residual", (NR, P, TC * D))
    io.XN = dram("normed_rows", (NR, P, TC * D))
    io.XS = dram("routed_rows", (SLOTS * P, ROW))
    io.OUT = dram("final_rows", (TOKENS + 2 * BLANK, D))
    with ExitStack() as ctx:
        def sb(name, shape, dt=F32):
            return ctx.enter_context(nc.sbuf_tensor(name, shape, dt))

        g = Names()
        g.ident, g.ident16 = sb("ident_sb", [P, P]), sb("ident16_sb", [P, P], F16)
        g.wt = sb("wt", [P, 4, D])
        g.bqs, g.bk, g.gamma, g.beta = (sb(n, [P, 1]) for n in ("bqs", "bk_sb", "gamma_sb", "beta_sb"))
        g.rb = sb("rb", [P, 2, NH + 1])
        g.lg = sb("logits", [P, NG, NE])
        g.pos = sb("pos", [P, NG], I32)
        g.te = sb("tile_expert", [P, SLOTS], I32)
        for stage in STAGES:
            stage(nc, ctx, io, g)


def tables():
    f = np.exp(np.arange(0, D, 2, dtype=np.float32) * np.float32(-np.log(10000.0) / D))
    w = f.astype(np.float64)[:, None]

    def table(n):
        return np.concatenate([np.sin(w * n), np.cos(w * n)], 0)

    j = np.arange(S, dtype=np.float64)[None, :]
    tabs = []
    for t in (table(j), table(j - S)):
        hi = t.astype(np.float16)
        tabs += [hi, (t - hi.astype(np.float64)).astype(np.float16)]
    turn = w * (S - 1 - j)
    rot = np.stack([np.concatenate([np.cos(turn), np.cos(turn)], 0), np.concatenate([-np.sin(turn), np.sin(turn)], 0)])
    pos = np.arange(2 * S_IMG, dtype=np.float32)[:, None]
    pe = np.zeros((2 * S_IMG, D), np.float32)
    pe[:, 0::2] = np.sin(pos * f)
    pe[:, 1::2] = np.cos(pos * f)
    row, col = np.arange(P)[:, None], np.arange(DW)[None, :]
    heads = np.zeros((P, NH + 1), np.float32)
    heads[np.arange(P), np.arange(P) // DH] = 1
    heads[:, NH] = heads[:, 0]
    pick = np.zeros((P, 2, 2, VW), np.float32)
    for g in range(4):
        for what in range(2):
            for par in range(2):
                for d in range(DH):
                    pick[g * VW + what * DH + d, what, par, par * DH + d] = 1
    last = np.zeros((P, 1), np.float32)
    last[P - 1] = 1
    c = {
        "pe_tok": pe[:S_IMG],
        "tabs": np.stack(tabs),
        "rot": rot.astype(np.float32),
        "ident": np.eye(P, dtype=np.float32),
        "ident16": np.eye(P, dtype=np.float16),
        "mask1": np.repeat((row < col).astype(np.float32)[:, None], 3, 1),
        "mask2": np.repeat((row > col).astype(np.int32)[:, None], 3, 1),
        "head_mask": heads,
        "pick": pick,
        "token": (np.arange(NG)[None, :] * P + row).astype(np.float32),
        "blank": np.concatenate([np.zeros((2 * BLANK, ROW - 1), np.float32),
                                 (TOKENS + np.arange(2 * BLANK, dtype=np.float32))[:, None]], 1).reshape(2, BLANK, ROW),
        "last": last,
        "tri": (row < np.arange(P)[None, :]).astype(np.float32),
        "ones": np.ones((P, P), np.float32),
        "rank": np.broadcast_to(NE - np.arange(NE, dtype=np.float32), (P, NE)).copy(),
        "index": np.broadcast_to(np.arange(SLOTS, dtype=np.float32), (P, SLOTS)).copy(),
        "before": np.broadcast_to((np.arange(NE)[None, :] < np.arange(NE)[:, None]).astype(np.float32),
                                  (P, NE, NE)).copy(),
    }
    return c


_INS = ["x", "txt", "L0_tok_W", "L0_attn_gamma", "L0_attn_beta", "L0_attn_Wq", "L0_attn_bq", "L0_attn_Wk",
        "L0_attn_bk", "L0_attn_Wv", "L0_attn_bv", "L0_attn_Wpos", "L0_attn_u_bias", "L0_attn_v_bias", "L0_attn_Wo",
        "L0_attn_bo", "L0_ffn_Wr", "L0_ffn_br", "L0_ffn_W1", "L0_ffn_W2", "L0_ffn_W3"]
_SHORT = ["x", "txt", "Wtok", "gamma", "beta", "Wq", "bq", "Wk", "bk", "Wv", "bv", "Wpos", "u", "v", "Wo", "bo",
          "Wr", "br", "W1", "W2", "W3"]


def kernel(**inputs):
    import concourse.bacc as bacc
    from concourse.bass_utils import run_bass_kernel_spmd

    nc = bacc.Bacc("TRN2", target_bir_lowering=False, num_devices=1)
    arrays, io = {}, Names()
    given = [(short, inputs[name]) for short, name in zip(_SHORT, _INS)] + list(tables().items())
    for name, a in given:
        a = np.ascontiguousarray(a)
        arrays[f"in_{name}"] = a
        vars(io)[name] = nc.dram_tensor(f"in_{name}", a.shape, mybir.dt.from_np(a.dtype), kind="ExternalInput").ap()
    io.out = nc.dram_tensor("out", (B, S, D), F32, kind="ExternalOutput").ap()
    program(nc, io)
    r = run_bass_kernel_spmd(nc, [arrays], core_ids=[0])
    return r.results[0]["out"]
```
